# Optimizing a Trainium2 kernel written in Bass

```python
import numpy as np
import jax
import jax.numpy as jnp

def _softmax(x, axis=-1):
    return jax.nn.softmax(x, axis=axis)

def _gelu(x):
    return jax.nn.gelu(x, approximate=True)

def _silu(x):
    return jax.nn.silu(x)

def _sigmoid(x):
    return jax.nn.sigmoid(x)

def _layernorm(x, axis=-1, eps=1e-05):
    m = jnp.mean(x, axis=axis, keepdims=True)
    v = jnp.var(x, axis=axis, keepdims=True)
    return (x - m) / jnp.sqrt(v + eps)

def _scatter_add(tgt, idx, src, axis=0):
    return tgt.at[idx].add(src)

def _segment_sum(src, seg, n):
    return jax.ops.segment_sum(src, seg, n)
kernel_name = 'mk_xattn_ffn_d2_seqx_r8_85df9a'

def setup_inputs(seed: int=0):
    np.random.seed(seed)
    _w = jnp.asarray

    def _rec_inputs():
        import jax
        import jax.numpy as jnp
        _rk = jax.random.key(seed)
        x = -0.0002928 + 1 * jax.random.normal(jax.random.fold_in(_rk, 1), (8, 256, 256), jnp.float32)
        _lenS = 256 - jax.random.randint(jax.random.fold_in(_rk, 7), (8,), 0, max(1, 256 // 4) + 1, jnp.int32)
        _lenS2 = 1601 - jax.random.randint(jax.random.fold_in(_rk, 8), (8,), 0, max(1, 1601 // 4) + 1, jnp.int32)
        _ctx_2048P = jax.random.normal(jax.random.fold_in(_rk, 11), (8, 16, 256), jnp.float32)
        _ctx_2048c = jax.random.dirichlet(jax.random.fold_in(_rk, 511), 0.3 * jnp.ones((16,), jnp.float32), (8, 1601))
        _ctx_2048t = jnp.einsum('bsk,bkd->bsd', _ctx_2048c, _ctx_2048P)
        _ctx_2048t = _ctx_2048t * jax.lax.rsqrt(jnp.mean(jnp.square(_ctx_2048t)) + 1e-12) * 0.953939
        ctx_2048 = 4.13588e-05 + 0.999923 * (_ctx_2048t + 0.3 * jax.random.normal(jax.random.fold_in(_rk, 611), (8, 1601, 256), jnp.float32))
        _validS = jnp.arange(256)[None, :] < _lenS[:, None]
        _validS2 = jnp.arange(1601)[None, :] < _lenS2[:, None]
        _causal = jnp.tril(jnp.ones((256, 256), dtype=bool))
        mask_1xSxS2_ff0 = jnp.where(jnp.ones((1, 256, 1601), dtype=bool), 0.0, -1000000000.0).astype(jnp.float32)
        mask_BxS2_bf1 = jnp.ones((8, 1601), dtype=bool)
        return (x, ctx_2048, mask_1xSxS2_ff0, mask_BxS2_bf1)
    x, ctx_2048, mask_1xSxS2_ff0, mask_BxS2_bf1 = _rec_inputs()

    def _L0_xattn_setup():
        import jax, jax.numpy as jnp
        import numpy as np
        H = 256
        NH = 16
        NKV = 4
        HD = 128
        GROUPS = NH // NKV
        EPS = 1e-06
        B, S, SE = (1, 256, 512)

        def _rmsnorm(x, w, eps=EPS):
            xf = x.astype(jnp.float32)
            var = jnp.mean(xf * xf, axis=-1, keepdims=True)
            return (xf * jax.lax.rsqrt(var + eps)).astype(x.dtype) * w
        key = jax.random.key(seed)
        ks = jax.random.split(key, 12)
        sc = 0.02
        return {'hidden_states': jax.random.normal(ks[0], (B, S, H), jnp.float32), 'encoder_hidden_states': jax.random.normal(ks[1], (B, SE, H), jnp.float32), 'attention_mask': jnp.zeros((B, S, SE), jnp.float32), 'Wq': jax.random.normal(ks[2], (H, NH * HD), jnp.float32) * sc, 'bq': jax.random.normal(ks[3], (NH * HD,), jnp.float32) * sc, 'Wk': jax.random.normal(ks[4], (H, NKV * HD), jnp.float32) * sc, 'bk': jax.random.normal(ks[5], (NKV * HD,), jnp.float32) * sc, 'Wv': jax.random.normal(ks[6], (H, NKV * HD), jnp.float32) * sc, 'bv': jax.random.normal(ks[7], (NKV * HD,), jnp.float32) * sc, 'Wo': jax.random.normal(ks[8], (NH * HD, H), jnp.float32) * sc, 'qn_w': jnp.ones((HD,), jnp.float32), 'kn_w': jnp.ones((HD,), jnp.float32)}
    _L0_xattn_all = _L0_xattn_setup()
    _L0_xattn_in = {k: v for k, v in _L0_xattn_all.items() if k in ('Wq', 'bq', 'Wk', 'bk', 'Wv', 'bv', 'Wo', 'qn_w', 'kn_w')}
    del _L0_xattn_all

    def _L0_ffn_setup():
        import jax, jax.numpy as jnp
        import numpy as np
        TOPK = 4
        key = jax.random.key(seed)
        k_x, k_a, k_b, k_w, k_bias = jax.random.split(key, 5)
        b, s, h, j, a, r = (4, 256, 256, 256, 64, 16)
        x = jax.random.normal(k_x, (b, s, h), dtype=jnp.float32)
        A = jax.random.normal(k_a, (a, r, h), dtype=jnp.float32) * 0.02
        B = jax.random.normal(k_b, (a, j, r), dtype=jnp.float32) * 0.02
        W = jax.random.normal(k_w, (j, h), dtype=jnp.float32) * 0.02
        bias = jax.random.normal(k_bias, (j,), dtype=jnp.float32) * 0.02
        return {'x': x, 'A': A, 'B': B, 'W': W, 'bias': bias}
    _L0_ffn_all = _L0_ffn_setup()
    _L0_ffn_in = {k: v for k, v in _L0_ffn_all.items() if k in ('A', 'B', 'W', 'bias')}
    del _L0_ffn_all

    def _L1_xattn_setup():
        import jax, jax.numpy as jnp
        import numpy as np
        import math
        D_MODEL = 256
        N_Q_HEADS = 16
        N_KV_HEADS = 4
        HEAD_DIM = D_MODEL // N_Q_HEADS
        B = 4
        S = 128

        def _alibi_slopes(num_heads):
            n = 2 ** int(math.floor(math.log2(num_heads)))
            m0 = 2.0 ** (-8.0 / n)
            return m0 ** jnp.arange(1, n + 1, dtype=jnp.float32)
        key = jax.random.key(seed)
        ks = jax.random.split(key, 8)
        xavier = lambda k, fi, fo: jax.random.normal(k, (fi, fo), jnp.float32) * math.sqrt(2.0 / (fi + fo))
        return {'query': jax.random.normal(ks[0], (B, S, D_MODEL), jnp.float32), 'key': jax.random.normal(ks[1], (B, S, D_MODEL), jnp.float32), 'value': jax.random.normal(ks[2], (B, S, D_MODEL), jnp.float32), 'mask': jnp.ones((B, S), dtype=bool), 'Wq': xavier(ks[3], D_MODEL, N_Q_HEADS * HEAD_DIM), 'Wk': xavier(ks[4], D_MODEL, N_KV_HEADS * HEAD_DIM), 'Wv': xavier(ks[5], D_MODEL, N_KV_HEADS * HEAD_DIM), 'Wo': xavier(ks[6], D_MODEL, D_MODEL)}
    _L1_xattn_all = _L1_xattn_setup()
    _L1_xattn_in = {k: v for k, v in _L1_xattn_all.items() if k in ('Wq', 'Wk', 'Wv', 'Wo')}
    del _L1_xattn_all

    def _L1_ffn_setup():
        import jax, jax.numpy as jnp
        import numpy as np
        _Q_IN = 128
        _LUT_MIN = -128
        _Q_OUT = 1 << 16
        _TOP_K = 2
        _EXP_LUT = (jnp.exp(jnp.arange(_LUT_MIN, 1, dtype=jnp.float32) / _Q_IN) * _Q_OUT).astype(jnp.int32)

        def softmax_integer(logits):
            li = jnp.round(logits.astype(jnp.float32) * _Q_IN).astype(jnp.int32)
            shifted = jnp.clip(li - li.max(axis=-1, keepdims=True), _LUT_MIN, None)
            exp_vals = _EXP_LUT[shifted - _LUT_MIN]
            exp_sum = jnp.clip(exp_vals.sum(axis=-1, keepdims=True), 1, None)
            return exp_vals.astype(jnp.float32) / exp_sum.astype(jnp.float32)
        key = jax.random.key(seed)
        k0, k1, k2, k3, k4 = jax.random.split(key, 5)
        B, S, H, I, E = (4, 256, 256, 704, 8)
        x = jax.random.normal(k0, (B, S, H), dtype=jnp.float32)
        w_gate = jax.random.normal(k1, (E, H), dtype=jnp.float32) * 0.02
        w1 = jax.random.normal(k2, (E, I, H), dtype=jnp.float32) * 0.02
        w2 = jax.random.normal(k3, (E, H, I), dtype=jnp.float32) * 0.02
        w3 = jax.random.normal(k4, (E, I, H), dtype=jnp.float32) * 0.02
        return {'x': x, 'w_gate': w_gate, 'w1': w1, 'w2': w2, 'w3': w3}
    _L1_ffn_all = _L1_ffn_setup()
    _L1_ffn_in = {k: v for k, v in _L1_ffn_all.items() if k in ('w_gate', 'w1', 'w2', 'w3')}
    del _L1_ffn_all
    return {'x': x, 'ctx_2048': ctx_2048, 'mask_1xSxS2_ff0': mask_1xSxS2_ff0, 'mask_BxS2_bf1': mask_BxS2_bf1, 'L0_xattn_Wq': _L0_xattn_in['Wq'], 'L0_xattn_bq': _L0_xattn_in['bq'], 'L0_xattn_Wk': _L0_xattn_in['Wk'], 'L0_xattn_bk': _L0_xattn_in['bk'], 'L0_xattn_Wv': _L0_xattn_in['Wv'], 'L0_xattn_bv': _L0_xattn_in['bv'], 'L0_xattn_Wo': _L0_xattn_in['Wo'], 'L0_xattn_qn_w': _L0_xattn_in['qn_w'], 'L0_xattn_kn_w': _L0_xattn_in['kn_w'], 'L0_ffn_A': _L0_ffn_in['A'], 'L0_ffn_B': _L0_ffn_in['B'], 'L0_ffn_W': _L0_ffn_in['W'], 'L0_ffn_bias': _L0_ffn_in['bias'], 'L1_xattn_Wq': _L1_xattn_in['Wq'], 'L1_xattn_Wk': _L1_xattn_in['Wk'], 'L1_xattn_Wv': _L1_xattn_in['Wv'], 'L1_xattn_Wo': _L1_xattn_in['Wo'], 'L1_ffn_w_gate': _L1_ffn_in['w_gate'], 'L1_ffn_w1': _L1_ffn_in['w1'], 'L1_ffn_w2': _L1_ffn_in['w2'], 'L1_ffn_w3': _L1_ffn_in['w3']}

def reference(x, ctx_2048, mask_1xSxS2_ff0, mask_BxS2_bf1, L0_xattn_Wq, L0_xattn_bq, L0_xattn_Wk, L0_xattn_bk, L0_xattn_Wv, L0_xattn_bv, L0_xattn_Wo, L0_xattn_qn_w, L0_xattn_kn_w, L0_ffn_A, L0_ffn_B, L0_ffn_W, L0_ffn_bias, L1_xattn_Wq, L1_xattn_Wk, L1_xattn_Wv, L1_xattn_Wo, L1_ffn_w_gate, L1_ffn_w1, L1_ffn_w2, L1_ffn_w3):
    import jax
    import jax.numpy as jnp

    def _L0_xattn_ref(hidden_states, encoder_hidden_states, attention_mask, Wq, bq, Wk, bk, Wv, bv, Wo, qn_w, kn_w):
        import jax, jax.numpy as jnp
        import numpy as np
        H = 256
        NH = 16
        NKV = 4
        HD = 128
        GROUPS = NH // NKV
        EPS = 1e-06
        B, S, SE = (1, 256, 512)

        def _rmsnorm(x, w, eps=EPS):
            xf = x.astype(jnp.float32)
            var = jnp.mean(xf * xf, axis=-1, keepdims=True)
            return (xf * jax.lax.rsqrt(var + eps)).astype(x.dtype) * w
        b, s, _ = hidden_states.shape
        se = encoder_hidden_states.shape[1]
        q = (hidden_states @ Wq + bq).reshape(b, s, NH, HD).transpose(0, 2, 1, 3)
        k = (encoder_hidden_states @ Wk + bk).reshape(b, se, NKV, HD).transpose(0, 2, 1, 3)
        v = (encoder_hidden_states @ Wv + bv).reshape(b, se, NKV, HD).transpose(0, 2, 1, 3)
        k = jnp.repeat(k, GROUPS, axis=1)
        v = jnp.repeat(v, GROUPS, axis=1)
        q = _rmsnorm(q, qn_w)
        k = _rmsnorm(k, kn_w)
        scale = 1.0 / np.sqrt(HD).astype(np.float32)
        scores = jnp.einsum('bhsd,bhed->bhse', q, k) * scale
        scores = scores + attention_mask[:, None, :, :]
        probs = jax.nn.softmax(scores.astype(jnp.float32), axis=-1).astype(q.dtype)
        out = jnp.einsum('bhse,bhed->bhsd', probs, v)
        out = out.transpose(0, 2, 1, 3).reshape(b, s, NH * HD)
        return out @ Wo

    def _L0_ffn_ref(x, A, B, W, bias):
        import jax, jax.numpy as jnp
        import numpy as np
        TOPK = 4
        vecs = jnp.einsum('arh,bsh->bsar', A, x)
        arrows = jnp.linalg.norm(vecs, axis=-1)
        _, idx = jax.lax.top_k(arrows, TOPK)
        routes = jax.nn.one_hot(idx, arrows.shape[-1], dtype=x.dtype).sum(-2) / TOPK
        v = jnp.einsum('bsa,bsar->bsr', routes, vecs)
        delta = jnp.einsum('bsa,ajr,bsr->bsj', routes, B, v)
        base = jnp.einsum('bsh,jh->bsj', x, W) + bias
        return base + delta

    def _L1_xattn_ref(query, key, value, mask, Wq, Wk, Wv, Wo):
        import jax, jax.numpy as jnp
        import numpy as np
        import math
        D_MODEL = 256
        N_Q_HEADS = 16
        N_KV_HEADS = 4
        HEAD_DIM = D_MODEL // N_Q_HEADS
        B = 4
        S = 128

        def _alibi_slopes(num_heads):
            n = 2 ** int(math.floor(math.log2(num_heads)))
            m0 = 2.0 ** (-8.0 / n)
            return m0 ** jnp.arange(1, n + 1, dtype=jnp.float32)
        b, q_len, d = query.shape
        kv_len = key.shape[1]
        G = N_KV_HEADS
        Hpg = N_Q_HEADS // G
        dh = HEAD_DIM
        Q = (query @ Wq).reshape(b, q_len, G, Hpg, dh)
        K = (key @ Wk).reshape(b, kv_len, G, dh)
        V = (value @ Wv).reshape(b, kv_len, G, dh)
        Q = Q / math.sqrt(dh)
        scores = jnp.einsum('bqghd,bkgd->bghqk', Q, K)
        rel = jnp.arange(kv_len, dtype=jnp.float32)[None, :] - jnp.arange(q_len, dtype=jnp.float32)[:, None]
        m = _alibi_slopes(N_Q_HEADS).reshape(1, G, Hpg, 1, 1)
        scores = scores + m * rel[None, None, None]
        neg = jnp.finfo(scores.dtype).min
        scores = jnp.where(mask[:, None, None, None, :], scores, neg)
        w = jax.nn.softmax(scores, axis=-1)
        out = jnp.einsum('bghqk,bkgd->bqghd', w, V)
        out = out.reshape(b, q_len, G * Hpg * dh)
        return out @ Wo

    def _L1_ffn_ref(x, w_gate, w1, w2, w3):
        import jax, jax.numpy as jnp
        import numpy as np
        _Q_IN = 128
        _LUT_MIN = -128
        _Q_OUT = 1 << 16
        _TOP_K = 2
        _EXP_LUT = (jnp.exp(jnp.arange(_LUT_MIN, 1, dtype=jnp.float32) / _Q_IN) * _Q_OUT).astype(jnp.int32)

        def softmax_integer(logits):
            li = jnp.round(logits.astype(jnp.float32) * _Q_IN).astype(jnp.int32)
            shifted = jnp.clip(li - li.max(axis=-1, keepdims=True), _LUT_MIN, None)
            exp_vals = _EXP_LUT[shifted - _LUT_MIN]
            exp_sum = jnp.clip(exp_vals.sum(axis=-1, keepdims=True), 1, None)
            return exp_vals.astype(jnp.float32) / exp_sum.astype(jnp.float32)
        orig_shape = x.shape
        H = orig_shape[-1]
        xf = x.reshape(-1, H)
        T = xf.shape[0]
        E = w_gate.shape[0]
        router_logits = xf @ w_gate.T
        routing_weights = softmax_integer(router_logits)
        top_w, top_i = jax.lax.top_k(routing_weights, _TOP_K)
        top_w = top_w / top_w.sum(axis=-1, keepdims=True)
        combine = jnp.zeros((T, E), xf.dtype).at[jnp.arange(T)[:, None], top_i].add(top_w)
        out = jnp.zeros_like(xf)
        for e in range(E):
            h = jax.nn.silu(xf @ w1[e].T) * (xf @ w3[e].T)
            out = out + combine[:, e:e + 1] * (h @ w2[e].T)
        return out.reshape(orig_shape)
    x = x + _L0_xattn_ref(_layernorm(x, axis=-1), ctx_2048, mask_1xSxS2_ff0, L0_xattn_Wq, L0_xattn_bq, L0_xattn_Wk, L0_xattn_bk, L0_xattn_Wv, L0_xattn_bv, L0_xattn_Wo, L0_xattn_qn_w, L0_xattn_kn_w)
    x = x + _L0_ffn_ref(_layernorm(x, axis=-1), L0_ffn_A, L0_ffn_B, L0_ffn_W, L0_ffn_bias)
    x = x + _L1_xattn_ref(_layernorm(x, axis=-1), ctx_2048, ctx_2048, mask_BxS2_bf1, L1_xattn_Wq, L1_xattn_Wk, L1_xattn_Wv, L1_xattn_Wo)
    x = x + _L1_ffn_ref(_layernorm(x, axis=-1), L1_ffn_w_gate, L1_ffn_w1, L1_ffn_w2, L1_ffn_w3)
    return x

_drawn_inputs = setup_inputs


def setup_inputs(seed=0):
    import zlib

    import numpy as np

    out = dict(_drawn_inputs(seed))
    spreads = {'L0_xattn_qn_w': (1.0, 0.6), 'L0_xattn_kn_w': (1.0, 0.6)}
    factors = {'L0_xattn_bq': 8.0,
     'L0_xattn_bk': 8.0,
     'L0_xattn_bv': 3.896,
     'L0_ffn_A': 6.603,
     'L0_ffn_B': 5.671,
     'L0_ffn_bias': 3.459,
     'L1_ffn_w_gate': 4.339,
     'L1_ffn_w1': 3.883,
     'L1_ffn_w2': 3.841,
     'L1_ffn_w3': 3.844}
    for name, (base, spread) in spreads.items():
        noise = np.random.default_rng([zlib.crc32(name.encode()), seed]).standard_normal(out[name].shape)
        drawn = base * np.exp(spread * noise) if base else spread * noise
        out[name] = jnp.asarray(drawn.astype(out[name].dtype))
    for name, factor in factors.items():
        out[name] = (out[name] * factor).astype(out[name].dtype)
    return out
```

```python
from contextlib import ExitStack

import concourse.bass as bass
from concourse import mybir

ALU = mybir.AluOpType
ACT = mybir.ActivationFunctionType
AX = mybir.AxisListType
F32 = mybir.dt.float32
F32R = mybir.dt.float32r

P = 128
B, S, H = 8, 256, 256
KC = H // P
QT = S // P
SK = 1601
KT = -(-SK // P)
SKP = KT * P
CHUNKS = 4
CW = 402
SKC = CHUNKS * CW
BANK = 512
NEG = -1.0e30
KGROUPS = [range(0, 4), range(4, 7), range(7, 10), range(10, 13)]
HD0, G0, HPG0 = 128, 4, 4
EPS_RMS, EPS_LN = 1e-6, 1e-5


def stand(eng, passed):
    eng.sem_inc(passed, 1)


def first_plan():
    def kv(g): return [("kv", g, i) for i in range(7)]
    def norms(g): return [("kt", g, j) for j in range(len(KGROUPS))] + [("qt", g, i) for i in range(QT)]
    steps = [("ctx", 0, 0), ("xt", 0, 0), *kv(0), ("vh", 0, 0), ("qp", 0, 0), ("qp", 0, 1),
             ("kstat", 0, 0), ("qstat", 0, 0), *norms(0)]
    tiles = G0 * HPG0 * QT
    per = HPG0 * QT
    for t in range(tiles + 3):
        work = []
        g, at = divmod(t, per)
        if g + 1 < G0:
            work = {0: kv(g + 1)[:4], 2: kv(g + 1)[4:] + [("vh", g + 1, 0), ("qp", g + 1, 0)],
                    3: [("kstat", g + 1, 0)], 4: [("qp", g + 1, 1)], 5: [("qstat", g + 1, 0)],
                    6: norms(g + 1)}.get(at, [])
        work = list(work)
        if t < tiles:
            steps.append(("scores", t, 0))
        turn = [("turn", t - 1, j) for j in range(4)] if 1 <= t <= tiles else []
        exp = [("exp", t, 0)] if t < tiles else []
        if t % 2 == 0:
            steps += turn[:2] + exp
            if t >= 2 and (t - 2) // 2 < tiles // 2:
                steps.append(("rinv", (t - 2) // 2, 0))
            if t >= per + 2 and (t - per - 2) % per == 0:
                steps.append(("wo", (t - per - 2) // per, 0))
            steps += turn[2:3] + work[:1] + turn[3:] + work[1:]
        else:
            pair = (t - 3) // 2
            pv = [("pv", pair, j) for j in range(4)] if t >= 3 else []
            for j in range(4):
                steps += pv[j:j + 1] + turn[j:j + 1]
                if j == 1:
                    steps += exp
            if pv:
                steps.append(("norm", pair, 0))
            steps += work
    return steps


def count(steps, kinds):
    at = {s: n for n, s in enumerate(s for s in steps if s[0] in kinds)}
    return at, len(at)


def first_attention(nc, x, out, ctxT, mask, wq, wkv, wo, bias, qn, kn):
    steps = first_plan()
    bank_at, BANKS = count(steps, ("xt", "kv", "qp", "kt", "qt", "turn"))
    high_at, HIGHS = count(steps, ("kt", "qt", "turn"))
    acc_at, ACCS = count([s for s in steps if s[0] != "pv" or s[2] == 3], ("pv", "wo"))
    TILES, PAIRS = G0 * HPG0 * QT, G0 * HPG0
    assert wq.shape[0] == G0

    with ExitStack() as ctx:
        def sb(name, shape, dt=F32):
            return ctx.enter_context(nc.sbuf_tensor("a0_" + name, shape, dt))

        def sem(name):
            return ctx.enter_context(nc.semaphore("a0_" + name))

        ctx_hi, ctx_lo = (sb(n, [P, KC, SKP], F32R) for n in ("ctx_hi", "ctx_lo"))
        wkv_raw = sb("wkv_raw", [P, KC, 2 * HD0])
        wkv_hi, wkv_lo = (sb(n, [P, KC, 2 * HD0], F32R) for n in ("wkv_hi", "wkv_lo"))
        wq_g = sb("wq_g", [P, KC, HPG0 * HD0])
        wo_g = sb("wo_g", [P, HPG0, H])
        bias_g = sb("bias_g", [P, HPG0 * HD0 + 2 * HD0])
        maskt = sb("mask", [P, QT, SKC])
        k_hi, k_lo = ([sb(f"{n}{i}", [P, SKP], F32R) for i in range(2)] for n in ("k_hi", "k_lo"))
        v_hi, v_lo = ([sb(f"{n}{i}", [P, KT, HD0], F32R) for i in range(2)] for n in ("v_hi", "v_lo"))
        q_hi, q_lo = ([sb(f"{n}{i}", [P, HPG0, S], F32R) for i in range(2)] for n in ("q_hi", "q_lo"))
        prob = [sb(f"prob{i}", [P, SKP]) for i in range(2)]
        pt_hi, pt_lo = (sb(n, [P, KT, S], F32R) for n in ("pt_hi", "pt_lo"))
        kv_raw = sb("kv_raw", [P, KT, 2 * HD0])
        square = sb("square", [P, KT * HD0])
        q_raw = sb("q_raw", [P, QT, HPG0 * HD0])
        heads = sb("heads", [P, HPG0, S])
        x_in = sb("x_in", [P, QT, H])
        x_out = sb("x_out", [P, QT, H])
        xT = sb("xT", [P, KC, S])
        rows = sb("rows", [P, S])
        ident = sb("ident", [P, P])
        qn_s, kn_s = sb("qn_s", [P, 1]), sb("kn_s", [P, 1])
        half = sb("half", [P, 16])
        top = sb("top", [P, 2, 2])
        negmax = sb("negmax", [P, 2])
        total = sb("total", [P, 4])
        inv = sb("inv", [P, 2, 2])
        kvar, krstd = sb("kvar", [P, KT]), sb("krstd", [P, KT])
        qvar, qrstd = sb("qvar", [P, QT * HPG0]), sb("qrstd", [P, QT * HPG0])
        ln6, ln2, lnr = sb("ln6", [P, QT, 6]), sb("ln2", [P, QT, 2]), sb("lnr", [P, QT])

        ps_s = ctx.enter_context(nc.psum_tensor("a0_ps_s", [P, CHUNKS, BANK], F32))
        ps_t = ctx.enter_context(nc.psum_tensor("a0_ps_t", [P, 2, BANK], F32))
        ps_o = ctx.enter_context(nc.psum_tensor("a0_ps_o", [P, 2, BANK], F32))

        const_in, const_set, const_ok, qn_scaled = (sem(n) for n in ("const_in", "const_set", "const_ok", "qn_scaled"))
        ctx_in, x_in_s, wkv_in, wq_in, wo_in = (sem(n) for n in ("ctx_in", "x_in_s", "wkv_in", "wq_in", "wo_in"))
        ctx_high, ctx_split, wkv_high, wkv_split = (sem(n) for n in ("ctx_high", "ctx_split", "wkv_high", "wkv_split"))
        ln_step, ln_var, ln_rstd, x_norm = (sem(n) for n in ("ln_step", "ln_var", "ln_rstd", "x_norm"))
        bank_full, bank_free = sem("bank_full"), sem("bank_free")
        acc_full, acc_free = sem("acc_full"), sem("acc_free")
        scores_full, scored, negmax_ok, exp_ok, high_ok = (
            sem(n) for n in ("scores_full", "scored", "negmax_ok", "exp_ok", "high_ok"))
        turned, pv_done, inv_ok, rows_ok = (sem(n) for n in ("turned", "pv_done", "inv_ok", "rows_ok"))
        k_square, k_sum, k_var, k_rstd, k_norm = (sem(n) for n in ("k_square", "k_sum", "k_var", "k_rstd", "k_norm"))
        q_square, q_sum, q_var, q_rstd, q_norm = (sem(n) for n in ("q_square", "q_sum", "q_var", "q_rstd", "q_norm"))
        dve_passed, pool_passed, sp_passed = (sem(n) for n in ("dve_passed", "pool_passed", "sp_passed"))
        v_high, v_split, x_done, x_stored = (sem(n) for n in ("v_high", "v_split", "x_done", "x_stored"))

        def f(ap):
            return ap.bitcast(F32)

        block = ctx.enter_context(nc.Block())

        @block.sync
        def _(sp):
            with nc.allow_non_contiguous_dma("one number a partition"):
                sp.dma_start(qn_s[:, :], qn).then_inc(const_in, 16)
                sp.dma_start(kn_s[:, :], kn).then_inc(const_in, 16)
            sp.wait_ge(const_set, 1)
            sp.dma_start(maskt[:, :, 0:SK], mask.rearrange("(t p) k -> p t k", p=P)).then_inc(const_in, 16)

            with sp.Fori(0, B) as b:
                sp.wait_ge(acc_free, b * ACCS + 1)
                sp.dma_start(x_in[:, :, :], x[b].rearrange("(t p) h -> p t h", p=P)).then_inc(x_in_s, 16)
                sp.wait_ge(k_norm, b * G0)
                stand(sp, sp_passed)
                sp.wait_ge(v_split, b * G0)
                stand(sp, sp_passed)
                sp.wait_ge(bank_full, b * BANKS)
                sp.dma_start(kv_raw[:, :, :].rearrange("p k d -> p (k d)"), ctxT[b]).then_inc(ctx_in, 16)
                for g in range(G0):
                    sp.wait_ge(wkv_split, b * G0 + g)
                    sp.dma_start(wkv_raw[:, :, :], wkv[g]).then_inc(wkv_in, 16)
                    if g == 0:
                        sp.wait_ge(bank_free, b * BANKS + 1)
                    else:
                        sp.wait_ge(bank_free, b * BANKS + bank_at["qp", g - 1, 1] + 2)
                    sp.dma_start(wq_g[:, :, :], wq[g]).then_inc(wq_in, 16)
                    sp.dma_start(bias_g[:, :], bias[g].partition_broadcast(P)).then_inc(wq_in, 16)
                    if g:
                        n = g - 1
                        if n == 0:
                            sp.wait_ge(acc_free, b * ACCS + 1)
                        else:
                            sp.wait_ge(acc_free, b * ACCS + acc_at["wo", n - 1, 0] + 2)
                        sp.dma_start(wo_g[:, :, :], wo[n]).then_inc(wo_in, 16)
                sp.wait_ge(acc_free, b * ACCS + acc_at["wo", G0 - 2, 0] + 2)
                sp.dma_start(wo_g[:, :, :], wo[G0 - 1]).then_inc(wo_in, 16)

        @block.gpsimd
        def _(pool):
            nc.gpsimd.memset(maskt[:, :, :], NEG).then_inc(const_set, 1)
            nc.gpsimd.memset(half[:, :], -0.5).then_inc(const_ok, 1)
            nc.gpsimd.memset(prob[0][:, SKC:], 0.0).then_inc(const_ok, 1)
            nc.gpsimd.memset(prob[1][:, SKC:], 0.0).then_inc(const_ok, 1)
            nc.gpsimd.memset(ident[:, :], 0.0).then_inc(const_set, 1)
            pool.wait_ge(const_set, 2)
            nc.gpsimd.affine_select(out=ident[:, :], in_=ident[:, :], compare_op=ALU.not_equal, fill=1.0, base=0,
                                    pattern=[[-1, P]], channel_multiplier=1).then_inc(const_ok, 1)
            pool.wait_ge(const_ok, 4)

            with pool.Fori(0, B) as b:
                for g in range(G0):
                    pool.wait_ge(wkv_in, (b * G0 + g) * 16 + 16)
                    if g:
                        pool.wait_ge(bank_full, b * BANKS + bank_at["kv", g - 1, 6] + 1)
                    else:
                        pool.wait_ge(bank_full, b * BANKS)
                    stand(pool, pool_passed)
                    nc.gpsimd.tensor_scalar(wkv_hi[:, :, :], wkv_raw[:, :, :], 1.0, None, ALU.mult).then_inc(wkv_high, 1)
                    pool.wait_ge(wkv_high, b * G0 + g + 1)
                    nc.gpsimd.tensor_tensor(wkv_lo[:, :, :], wkv_raw[:, :, :], f(wkv_hi[:, :, :]),
                                            ALU.subtract).then_inc(wkv_split, 1)
                    if g == 0:
                        pool.wait_ge(ln_var, b * QT + QT)
                        nc.gpsimd.tensor_tensor(lnr[:, :], ln2[:, :, 1], half[:, 0:QT], ALU.pow).then_inc(ln_rstd, 1)
                    pool.wait_ge(bank_free, b * BANKS + bank_at["kv", g, 6] + 2)
                    if g:
                        pool.wait_ge(q_sum, b * G0 + g)
                    else:
                        pool.wait_ge(q_sum, b * G0)
                    k3 = kv_raw[:, :, 0:HD0]
                    nc.gpsimd.tensor_tensor(square[:, :].rearrange("p (k d) -> p k d", d=HD0), k3, k3,
                                            ALU.mult).then_inc(k_square, 1)
                    pool.wait_ge(v_high, b * G0 + g + 1)
                    nc.gpsimd.tensor_tensor(v_lo[g % 2][:, :, :], kv_raw[:, :, HD0:], f(v_hi[g % 2][:, :, :]),
                                            ALU.subtract).then_inc(v_split, 1)
                    pool.wait_ge(k_var, b * G0 + g + 1)
                    nc.gpsimd.tensor_tensor(krstd[:, :], kvar[:, :], half[:, 0:KT], ALU.pow).then_inc(k_rstd, 1)
                    pool.wait_ge(k_rstd, b * G0 + g + 1)
                    nc.gpsimd.tensor_tensor(k3, k3, krstd[:, :].unsqueeze(2).to_broadcast([P, KT, HD0]),
                                            ALU.mult).then_inc(k_norm, 1)
                    pool.wait_ge(bank_free, b * BANKS + bank_at["qp", g, 1] + 2)
                    pool.wait_ge(k_sum, b * G0 + g + 1)
                    q3 = q_raw[:, :, :].rearrange("p t (h d) -> p (t h) d", d=HD0)
                    nc.gpsimd.tensor_tensor(square[:, 0:QT * HPG0 * HD0].rearrange("p (k d) -> p k d", d=HD0), q3, q3,
                                            ALU.mult).then_inc(q_square, 1)
                    pool.wait_ge(q_var, b * G0 + g + 1)
                    nc.gpsimd.tensor_tensor(qrstd[:, :], qvar[:, :], half[:, 0:QT * HPG0], ALU.pow).then_inc(q_rstd, 1)
                    pool.wait_ge(q_rstd, b * G0 + g + 1)
                    nc.gpsimd.tensor_tensor(q3, q3, qrstd[:, :].unsqueeze(2).to_broadcast([P, QT * HPG0, HD0]),
                                            ALU.mult).then_inc(q_norm, 1)

        @block.tensor
        def _(pe):
            pe.wait_ge(const_ok, 4)

            with pe.Fori(0, B) as b:
                def bank(step):
                    n = bank_at[step]
                    pe.wait_ge(bank_free, b * BANKS + n)
                    return ps_t[:, n % 2, :]

                def split_mm(to, lhs, rhs, first=True, last=True):
                    (lh, ll), (rh, rl) = lhs, rhs
                    nc.tensor.matmul(to, lh, rh, start=first, stop=False)
                    nc.tensor.matmul(to, ll, rh, start=False, stop=False)
                    return nc.tensor.matmul(to, lh, rl, start=False, stop=last)

                for kind, n, j in steps:
                    if kind == "xt":
                        ps = bank((kind, n, j)).rearrange("p (c s) -> p c s", c=KC)
                        pe.wait_ge(x_norm, b * QT + QT)
                        for c in range(KC):
                            for q in range(QT):
                                mm = nc.tensor.transpose(ps[:, c, q * P:(q + 1) * P],
                                                         q_raw[:, q, c * P:(c + 1) * P], ident[:, :])
                        mm.then_inc(bank_full, 1)
                    elif kind == "kv":
                        ps = bank((kind, n, j)).rearrange("p (k d) -> p k d", k=2)
                        if j == 0:
                            pe.wait_ge(wkv_split, b * G0 + n + 1)
                            if n == 0:
                                pe.wait_ge(ctx_split, b * KC + KC)
                        for i in range(min(2, KT - 2 * j)):
                            k = slice((2 * j + i) * P, (2 * j + i + 1) * P)
                            for c in range(KC):
                                mm = split_mm(ps[:, i, :], (ctx_hi[:, c, k], ctx_lo[:, c, k]),
                                              (wkv_hi[:, c, :], wkv_lo[:, c, :]), c == 0, c == KC - 1)
                        mm.then_inc(bank_full, 1)
                    elif kind == "qp":
                        ps = bank((kind, n, j))
                        pe.wait_ge(wq_in, (b * G0 + n) * 32 + 32)
                        for c in range(KC):
                            mm = nc.tensor.matmul(ps, xT[:, c, j * P:(j + 1) * P], wq_g[:, c, :],
                                                  start=c == 0, stop=c == KC - 1)
                        mm.then_inc(bank_full, 1)
                    elif kind == "kt":
                        ps = bank((kind, n, j))
                        pe.wait_ge(k_norm, b * G0 + n + 1)
                        for i, k in enumerate(KGROUPS[j]):
                            mm = nc.tensor.transpose(ps[:, i * P:(i + 1) * P], kv_raw[:, k, 0:HD0], ident[:, :])
                        mm.then_inc(bank_full, 1)
                    elif kind == "qt":
                        ps = bank((kind, n, j))
                        pe.wait_ge(q_norm, b * G0 + n + 1)
                        for i in range(HPG0):
                            mm = nc.tensor.transpose(ps[:, i * P:(i + 1) * P], q_raw[:, j, i * HD0:(i + 1) * HD0],
                                                     ident[:, :])
                        mm.then_inc(bank_full, 1)
                    elif kind == "scores":
                        g, at = divmod(n, HPG0 * QT)
                        head, q = divmod(at, QT)
                        if at == 0:
                            pe.wait_ge(bank_free, b * BANKS + bank_at["qt", g, 1] + 2)
                        q = slice(q * P, (q + 1) * P)
                        for c in range(CHUNKS):
                            if c % 2 == 0:
                                pe.wait_ge(scored, (b * TILES + n) * 2 + c // 2)
                            k = slice(c * CW, (c + 1) * CW)
                            mm = split_mm(ps_s[:, c, 0:CW], (q_hi[g % 2][:, head, q], q_lo[g % 2][:, head, q]),
                                          (k_hi[g % 2][:, k], k_lo[g % 2][:, k]))
                            if c % 2:
                                mm.then_inc(scores_full, 1)
                    elif kind == "turn":
                        ps = bank((kind, n, j))
                        pe.wait_ge(exp_ok, b * TILES + n + 1)
                        for i, k in enumerate(KGROUPS[j]):
                            mm = nc.tensor.transpose(ps[:, i * P:(i + 1) * P], prob[n % 2][:, k * P:(k + 1) * P],
                                                     ident[:, :])
                        mm.then_inc(bank_full, 1)
                    elif kind == "pv":
                        g = n // HPG0
                        acc = acc_at["pv", n, 3]
                        ps = ps_o[:, acc % 2, :]
                        if j == 0:
                            pe.wait_ge(acc_free, b * ACCS + acc)
                            pe.wait_ge(inv_ok, b * PAIRS + n + 1)
                            for q in range(QT):
                                nc.tensor.matmul(ps[:, S + q * P:S + (q + 1) * P],
                                                 inv[:, n % 2, q:q + 1].to_broadcast([P, P]), ident[:, :],
                                                 start=True, stop=True)
                        if j == 0 and n % HPG0 == 0:
                            pe.wait_ge(v_split, b * G0 + g + 1)
                        pe.wait_ge(bank_free, b * BANKS + bank_at["turn", 2 * n + 1, j] + 2)
                        for k in KGROUPS[j]:
                            mm = split_mm(ps[:, 0:S], (v_hi[g % 2][:, k, :], v_lo[g % 2][:, k, :]),
                                          (pt_hi[:, k, :], pt_lo[:, k, :]), k == 0, k == KT - 1)
                        mm.then_inc(pv_done, 1)
                    elif kind == "wo":
                        acc = acc_at[kind, n, j]
                        pe.wait_ge(acc_free, b * ACCS + acc + 1)
                        pe.wait_ge(wo_in, (b * G0 + n) * 16 + 16)
                        for q in range(QT):
                            for i in range(HPG0):
                                mm = nc.tensor.matmul(ps_o[:, acc % 2, q * H:(q + 1) * H], heads[:, i, q * P:(q + 1) * P],
                                                      wo_g[:, i, :], start=i == 0, stop=i == HPG0 - 1)
                        mm.then_inc(acc_full, 1)

        @block.scalar
        def _(act):
            with act.Fori(0, B) as b:
                for kind, n, j in steps:
                    if kind == "ctx":
                        act.wait_ge(ctx_in, b * 16 + 16)
                        act.wait_ge(bank_full, b * BANKS)
                        for c in range(KC):
                            nc.scalar.copy(ctx_hi[:, c, :], kv_raw[:, :, :].rearrange("p k d -> p (k d)")[
                                :, c * SKP:(c + 1) * SKP]).then_inc(ctx_high, 1)
                    elif kind == "vh":
                        act.wait_ge(bank_free, b * BANKS + bank_at["kv", n, 6] + 2)
                        if n >= 2:
                            act.wait_ge(pv_done, b * PAIRS * 4 + (n - 1) * HPG0 * 4)
                        else:
                            act.wait_ge(pv_done, b * PAIRS * 4)
                        nc.scalar.copy(v_hi[n % 2][:, :, :], kv_raw[:, :, HD0:]).then_inc(v_high, 1)
                    elif kind in ("kt", "qt", "turn"):
                        at = bank_at[kind, n, j]
                        act.wait_ge(bank_full, b * BANKS + at + 1)
                        ps = ps_t[:, at % 2, :]
                        w = len(KGROUPS[j])
                        k0 = KGROUPS[j][0]
                        if kind == "kt":
                            act.wait_ge(const_in, 48)
                            act.wait_ge(scored, b * TILES * 2 + 1)
                            nc.scalar.activation(k_hi[n % 2][:, k0 * P:(k0 + w) * P], ps[:, 0:w * P], ACT.Identity,
                                                 bias=0.0, scale=kn_s[:, :]).then_inc(high_ok, 1)
                        elif kind == "qt":
                            act.wait_ge(qn_scaled, 1)
                            nc.scalar.activation(q_hi[n % 2][:, :, j * P:(j + 1) * P],
                                                 ps.rearrange("p (h s) -> p h s", h=HPG0), ACT.Identity, bias=0.0,
                                                 scale=qn_s[:, :]).then_inc(high_ok, 1)
                        else:
                            pair, q = divmod(n, QT)
                            if q == 0:
                                act.wait_ge(pv_done, (b * PAIRS + pair) * 4 - 4 + j + 1 if pair else b * PAIRS * 4)
                            nc.scalar.copy(pt_hi[:, k0:k0 + w, q * P:(q + 1) * P],
                                           ps[:, 0:w * P].rearrange("p (k s) -> p k s", k=w)).then_inc(high_ok, 1)
                    elif kind == "exp":
                        act.wait_ge(negmax_ok, b * TILES + n + 1)
                        nc.scalar.activation(prob[n % 2][:, 0:SKC], prob[n % 2][:, 0:SKC], ACT.Exp,
                                             bias=negmax[:, n % 2:n % 2 + 1], scale=1.0,
                                             accum_out=total[:, n % 4:n % 4 + 1]).then_inc(exp_ok, 1)
                    elif kind == "norm":
                        acc = acc_at["pv", n, 3]
                        act.wait_ge(pv_done, (b * PAIRS + n) * 4 + 4)
                        act.wait_ge(acc_free, b * ACCS + acc)
                        nc.scalar.copy(rows[:, :], ps_o[:, acc % 2, S:2 * S]).then_inc(rows_ok, 1)
                act.wait_ge(x_done, b + 1)
                act.dma_start(out[b].rearrange("(t p) h -> p t h", p=P), x_out[:, :, :]).then_inc(x_stored, 16)
            act.wait_ge(x_stored, 16 * B)

        @block.vector
        def _(dve):
            nc.vector.memset(top[:, 0, :], 0.0).then_inc(bank_free, 1)
            nc.vector.memset(top[:, 1, :], 0.0).then_inc(acc_free, 1)
            nc.vector.memset(negmax[:, :], 0.0).then_inc(scored, 1)
            dve.wait_ge(const_in, 48)
            nc.vector.tensor_scalar(qn_s[:, :], qn_s[:, :], float(HD0) ** -0.5, None, ALU.mult).then_inc(qn_scaled, 1)
            dve.wait_ge(qn_scaled, 1)

            with dve.Fori(0, B) as b:
                def evac(step):
                    at = bank_at[step]
                    dve.wait_ge(bank_full, b * BANKS + at + 1)
                    return ps_t[:, at % 2, :]

                for kind, n, j in steps:
                    if kind == "ctx":
                        dve.wait_ge(x_in_s, b * 16 + 16)
                        for q in range(QT):
                            nc.vector.bn_stats(ln6[:, q, :], x_in[:, q, :]).then_inc(ln_step, 1)
                            dve.wait_ge(ln_step, (b * QT + q) * 2 + 1)
                            stand(dve, dve_passed)
                            nc.vector.bn_aggr(ln2[:, q, :], ln6[:, q, :]).then_inc(ln_step, 1)
                            dve.wait_ge(ln_step, (b * QT + q) * 2 + 2)
                            nc.vector.tensor_scalar(ln2[:, q, 1:2], ln2[:, q, 1:2], EPS_LN, None,
                                                    ALU.add).then_inc(ln_var, 1)
                        for c in range(KC):
                            dve.wait_ge(ctx_high, b * KC + c + 1)
                            nc.vector.tensor_tensor(ctx_lo[:, c, :], kv_raw[:, :, :].rearrange("p k d -> p (k d)")[
                                :, c * SKP:(c + 1) * SKP], f(ctx_hi[:, c, :]), ALU.subtract).then_inc(ctx_split, 1)
                        dve.wait_ge(ln_rstd, b + 1)
                        for q in range(QT):
                            nc.vector.tensor_scalar(q_raw[:, q, 0:H], x_in[:, q, :], ln2[:, q, 0:1], lnr[:, q:q + 1],
                                                    ALU.subtract, ALU.mult).then_inc(x_norm, 1)
                    elif kind == "xt":
                        ps = evac((kind, n, j))
                        nc.vector.tensor_copy(xT[:, :, :], ps.rearrange("p (c s) -> p c s", c=KC)).then_inc(bank_free, 1)
                    elif kind == "kv":
                        ps = evac((kind, n, j))
                        if j == 0:
                            dve.wait_ge(wq_in, (b * G0 + n) * 32 + 32)
                            dve.wait_ge(v_split, b * G0 + n)
                            if n == 0:
                                dve.wait_ge(ctx_split, b * KC + KC)
                        w = min(2, KT - 2 * j)
                        nc.vector.tensor_tensor(kv_raw[:, 2 * j:2 * j + w, :],
                                                ps[:, 0:w * 2 * HD0].rearrange("p (k d) -> p k d", k=w),
                                                bias_g[:, HPG0 * HD0:].unsqueeze(1).to_broadcast([P, w, 2 * HD0]),
                                                ALU.add).then_inc(bank_free, 1)
                    elif kind == "qp":
                        ps = evac((kind, n, j))
                        nc.vector.tensor_tensor(q_raw[:, j, :], ps, bias_g[:, 0:HPG0 * HD0],
                                                ALU.add).then_inc(bank_free, 1)
                    elif kind == "kstat":
                        dve.wait_ge(k_square, b * G0 + n + 1)
                        nc.vector.tensor_reduce(kvar[:, :], square[:, :].rearrange("p (k d) -> p k d", d=HD0), AX.X,
                                                ALU.add).then_inc(k_sum, 1)
                        dve.wait_ge(k_sum, b * G0 + n + 1)
                        nc.vector.tensor_scalar(kvar[:, :], kvar[:, :], 1.0 / HD0, EPS_RMS, ALU.mult,
                                                ALU.add).then_inc(k_var, 1)
                    elif kind == "qstat":
                        dve.wait_ge(q_square, b * G0 + n + 1)
                        nc.vector.tensor_reduce(qvar[:, :], square[:, 0:QT * HPG0 * HD0].rearrange(
                            "p (k d) -> p k d", d=HD0), AX.X, ALU.add).then_inc(q_sum, 1)
                        dve.wait_ge(q_sum, b * G0 + n + 1)
                        nc.vector.tensor_scalar(qvar[:, :], qvar[:, :], 1.0 / HD0, EPS_RMS, ALU.mult,
                                                ALU.add).then_inc(q_var, 1)
                    elif kind in ("kt", "qt", "turn"):
                        ps = ps_t[:, bank_at[kind, n, j] % 2, :]
                        dve.wait_ge(high_ok, b * HIGHS + high_at[kind, n, j] + 1)
                        w, k0 = len(KGROUPS[j]), KGROUPS[j][0]
                        if kind == "kt":
                            k = slice(k0 * P, (k0 + w) * P)
                            nc.vector.scalar_tensor_tensor(k_lo[n % 2][:, k], ps[:, 0:w * P], kn_s[:, :],
                                                           f(k_hi[n % 2][:, k]), ALU.mult,
                                                           ALU.subtract).then_inc(bank_free, 1)
                        elif kind == "qt":
                            q = slice(j * P, (j + 1) * P)
                            nc.vector.scalar_tensor_tensor(q_lo[n % 2][:, :, q], ps.rearrange("p (h s) -> p h s", h=HPG0),
                                                           qn_s[:, :], f(q_hi[n % 2][:, :, q]), ALU.mult,
                                                           ALU.subtract).then_inc(bank_free, 1)
                        else:
                            q = slice(n % QT * P, (n % QT + 1) * P)
                            nc.vector.tensor_tensor(pt_lo[:, k0:k0 + w, q],
                                                    ps[:, 0:w * P].rearrange("p (k s) -> p k s", k=w),
                                                    f(pt_hi[:, k0:k0 + w, q]), ALU.subtract).then_inc(bank_free, 1)
                    elif kind == "scores":
                        if n >= 2:
                            dve.wait_ge(bank_full, b * BANKS + bank_at["turn", n - 2, 3] + 1)
                        for c in range(2):
                            dve.wait_ge(scores_full, (b * TILES + n) * 2 + c + 1)
                            stand(dve, dve_passed)
                            k = slice(2 * c * CW, (2 * c + 2) * CW)
                            nc.vector.tensor_tensor_reduce(
                                prob[n % 2][:, k].rearrange("p (c k) -> p c k", c=2), ps_s[:, 2 * c:2 * c + 2, 0:CW],
                                maskt[:, n % QT, k].rearrange("p (c k) -> p c k", c=2), 1.0, -3.4e38, ALU.add,
                                ALU.max, top[:, n % 2, c:c + 1]).then_inc(scored, 1)
                        dve.wait_ge(scored, (b * TILES + n) * 2 + 3)
                        nc.vector.tensor_reduce(negmax[:, n % 2:n % 2 + 1], top[:, n % 2, :], AX.X, ALU.max,
                                                negate=True).then_inc(negmax_ok, 1)
                    elif kind == "rinv":
                        dve.wait_ge(exp_ok, b * TILES + 2 * n + 2)
                        if n >= 2:
                            dve.wait_ge(pv_done, (b * PAIRS + n) * 4 - 4)
                        nc.vector.reciprocal(inv[:, n % 2, :], total[:, 2 * n % 4:2 * n % 4 + 2]).then_inc(inv_ok, 1)
                    elif kind == "norm":
                        acc = acc_at["pv", n, 3]
                        dve.wait_ge(rows_ok, b * PAIRS + n + 1)
                        nc.vector.tensor_tensor(heads[:, n % HPG0, :], ps_o[:, acc % 2, 0:S], rows[:, :],
                                                ALU.mult).then_inc(acc_free, 1)
                    elif kind == "wo":
                        acc = acc_at[kind, n, j]
                        dve.wait_ge(acc_full, b * G0 + n + 1)
                        if n == 0:
                            dve.wait_ge(x_stored, b * 16)
                        else:
                            dve.wait_ge(x_done, b)
                        y = ps_o[:, acc % 2, :].rearrange("p (t h) -> p t h", t=QT)
                        mm = nc.vector.tensor_tensor(x_out[:, :, :], y, (x_out if n else x_in)[:, :, :], ALU.add)
                        mm.then_inc(acc_free, 1)
                        if n == G0 - 1:
                            dve.wait_ge(acc_free, b * ACCS + ACCS + 1)
                            nc.vector.memset(top[:, :, :], 0.0).then_inc(x_done, 1)
                        else:
                            dve.wait_ge(acc_free, b * ACCS + acc + 2)


NA, R, TOPK = 64, 16, 4
AR = NA * R
AC = AR // P


def first_ffn(nc, x, out, wa, wb, ww, bias):
    TILES = B * S // P
    PER = 4
    ORDER = [("a", 0), ("a", 1), ("b", 0), ("a", 2), ("b", 1), ("a", 3), ("b", 2), ("b", 3)]

    with ExitStack() as ctx:
        def sb(name, shape, dt=F32):
            return ctx.enter_context(nc.sbuf_tensor("f0_" + name, shape, dt))

        def sem(name):
            return ctx.enter_context(nc.semaphore("f0_" + name))

        wa_raw, wb_raw, ww_raw = sb("wa_raw", [P, KC, AR]), sb("wb_raw", [P, AC, H]), sb("ww_raw", [P, KC, H])
        wa_hi, wa_lo = (sb(n, [P, KC, AR], F32R) for n in ("wa_hi", "wa_lo"))
        wb_hi, wb_lo = (sb(n, [P, AC, H], F32R) for n in ("wb_hi", "wb_lo"))
        ww_hi, ww_lo = (sb(n, [P, KC, H], F32R) for n in ("ww_hi", "ww_lo"))
        bias_s = sb("bias", [P, H])
        ident, half = sb("ident", [P, P]), sb("half", [P, 1])
        ones = sb("ones", [P, NA])
        xs = sb("xs", [P, PER, H])
        xn = sb("xn", [P, 2, H])
        xT_hi, xT_lo = (sb(n, [P, 2, KC, P], F32R) for n in ("xT_hi", "xT_lo"))
        sq = sb("sq", [P, 2, AR])
        norms = sb("norms", [P, NA])
        m8 = sb("m8", [P, 8])
        above, equal, rank, keep = (sb(n, [P, NA]) for n in ("above", "equal", "rank", "keep"))
        nabove = sb("nabove", [P, 1])
        picked = sb("picked", [P, 2, NA])
        masked = sb("masked", [P, 2, AR])
        v = sb("v", [P, 2, R])
        z = sb("z", [P, 2, AR])
        zT_hi, zT_lo = (sb(n, [P, AC, P], F32R) for n in ("zT_hi", "zT_lo"))
        y = sb("y", [P, PER, H])
        ln6, ln2, rstd = sb("ln6", [P, 6]), sb("ln2", [P, 2, 2]), sb("rstd", [P, 2])

        ps_v = ctx.enter_context(nc.psum_tensor("f0_ps_v", [P, 2, 2 * BANK], F32))
        ps_z = ctx.enter_context(nc.psum_tensor("f0_ps_z", [P, 2, BANK], F32))
        ps_x = ctx.enter_context(nc.psum_tensor("f0_ps_x", [P, BANK], F32))
        ps_y = ctx.enter_context(nc.psum_tensor("f0_ps_y", [P, BANK], F32))

        (w_in, const_set, const_ok, w_high, w_split, chain, var_ok, rstd_ok, x_norm, xt_full, xt_high, xt_low,
         v_full, squared, v_used, picked_ok, z_ok, zt_full, zt_high, zt_low, y_full, y_read, y_ok, stored) = (
            sem(n) for n in ("w_in", "const_set", "const_ok", "w_high", "w_split", "chain", "var_ok", "rstd_ok",
                             "x_norm", "xt_full", "xt_high", "xt_low", "v_full", "squared", "v_used", "picked_ok",
                             "z_ok", "zt_full", "zt_high", "zt_low", "y_full", "y_read", "y_ok", "stored"))

        dve_passed = sem("dve_passed")
        x_in = [sem(f"x_in{n}") for n in range(PER)]

        def f(ap):
            return ap.bitcast(F32)

        block = ctx.enter_context(nc.Block())

        @block.sync
        def _(sp):
            sp.dma_start(wa_raw[:, :, :], wa).then_inc(w_in, 16)
            sp.dma_start(wb_raw[:, :, :], wb).then_inc(w_in, 16)
            sp.dma_start(ww_raw[:, :, :], ww).then_inc(w_in, 16)
            sp.dma_start(bias_s[:, :], bias.partition_broadcast(P)).then_inc(w_in, 16)
            with sp.Fori(0, TILES // PER) as i:
                for n in range(PER):
                    sp.wait_ge(y_ok, i * PER + n + 1)
                    sp.dma_start(xs[:, n, :], x[i * PER + n]).then_inc(x_in[n], 16)

        @block.gpsimd
        def _(pool):
            nc.gpsimd.memset(half[:, :], -0.5).then_inc(const_ok, 1)
            nc.gpsimd.memset(ones[:, :], 1.0).then_inc(const_ok, 1)
            nc.gpsimd.memset(ident[:, :], 0.0).then_inc(const_set, 1)
            pool.wait_ge(const_set, 1)
            nc.gpsimd.affine_select(out=ident[:, :], in_=ident[:, :], compare_op=ALU.not_equal, fill=1.0, base=0,
                                    pattern=[[-1, P]], channel_multiplier=1).then_inc(const_ok, 1)
            pool.wait_ge(const_ok, 3)
            with pool.Fori(0, TILES // PER) as i:
                for kind, n in ORDER:
                    if kind == "a":
                        pool.wait_ge(var_ok, i * PER + n + 1)
                        nc.gpsimd.tensor_tensor(rstd[:, n % 2:n % 2 + 1], ln2[:, n % 2, 1:2], half[:, :],
                                                ALU.pow).then_inc(rstd_ok, 1)

        @block.tensor
        def _(pe):
            pe.wait_ge(const_ok, 3)
            pe.wait_ge(w_split, 3)

            with pe.Fori(0, TILES // PER) as i:
                for kind, n in ORDER:
                    p, t = n % 2, i * PER + n
                    if kind == "a":
                        pe.wait_ge(x_norm, t + 1)
                        pe.wait_ge(xt_low, t)
                        for c in range(KC):
                            mm = nc.tensor.transpose(ps_x[:, c * P:(c + 1) * P], xn[:, p, c * P:(c + 1) * P], ident[:, :])
                        mm.then_inc(xt_full, 1)
                        pe.wait_ge(xt_low, t + 1)
                        if n >= 2:
                            pe.wait_ge(v_used, t - 1)
                        else:
                            pe.wait_ge(v_used, i * PER)
                        for q in range(2):
                            for c in range(KC):
                                for k, (l, r) in enumerate(((xT_hi, wa_hi), (xT_lo, wa_hi), (xT_hi, wa_lo))):
                                    mm = nc.tensor.matmul(ps_v[:, p, q * BANK:(q + 1) * BANK], l[:, p, c, :],
                                                          r[:, c, q * BANK:(q + 1) * BANK],
                                                          start=c == 0 and k == 0, stop=c == KC - 1 and k == 2)
                        mm.then_inc(v_full, 1)
                    else:
                        pe.wait_ge(z_ok, t + 1)
                        for q in range(2):
                            pe.wait_ge(zt_low, t * 2 + q)
                            for k in range(4):
                                mm = nc.tensor.transpose(ps_z[:, q, k * P:(k + 1) * P],
                                                         z[:, p, (4 * q + k) * P:(4 * q + k + 1) * P], ident[:, :])
                            mm.then_inc(zt_full, 1)
                        pe.wait_ge(y_read, t)
                        for c in range(KC):
                            for k, (l, r) in enumerate(((xT_hi, ww_hi), (xT_lo, ww_hi), (xT_hi, ww_lo))):
                                nc.tensor.matmul(ps_y[:, 0:H], l[:, p, c, :], r[:, c, :],
                                                 start=c == 0 and k == 0, stop=False)
                        for a in range(AC):
                            if a % 4 == 0:
                                pe.wait_ge(zt_low, t * 2 + a // 4 + 1)
                            for k, (l, r) in enumerate(((zT_hi, wb_hi), (zT_lo, wb_hi), (zT_hi, wb_lo))):
                                mm = nc.tensor.matmul(ps_y[:, 0:H], l[:, a, :], r[:, a, :], start=False,
                                                      stop=a == AC - 1 and k == 2)
                        mm.then_inc(y_full, 1)

        @block.scalar
        def _(act):
            act.wait_ge(w_in, 64)
            for hi, raw in ((wa_hi, wa_raw), (wb_hi, wb_raw), (ww_hi, ww_raw)):
                nc.scalar.copy(hi[:, :, :], raw[:, :, :]).then_inc(w_high, 1)
            with act.Fori(0, TILES // PER) as i:
                for kind, n in ORDER:
                    p, t = n % 2, i * PER + n
                    if kind == "a":
                        act.wait_ge(xt_full, t + 1)
                        if n >= 2:
                            act.wait_ge(y_full, t - 1)
                        else:
                            act.wait_ge(y_full, i * PER)
                        nc.scalar.copy(xT_hi[:, p, :, :], ps_x[:, 0:H].rearrange("p (c s) -> p c s", c=KC)).then_inc(
                            xt_high, 1)
                        act.wait_ge(v_full, t + 1)
                        nc.scalar.square(sq[:, p, :], ps_v[:, p, :]).then_inc(squared, 1)
                    else:
                        act.wait_ge(y_full, t)
                        for q in range(2):
                            act.wait_ge(zt_full, t * 2 + q + 1)
                            nc.scalar.copy(zT_hi[:, 4 * q:4 * q + 4, :], ps_z[:, q, :].rearrange(
                                "p (a s) -> p a s", a=4)).then_inc(zt_high, 1)
                for n in range(PER):
                    act.wait_ge(y_ok, i * PER + n + 1 + PER)
                    act.dma_start(out[i * PER + n], y[:, n, :]).then_inc(stored, 16)
            act.wait_ge(stored, 16 * TILES)

        @block.vector
        def _(dve):
            nc.vector.memset(m8[:, :], 0.0).then_inc(y_ok, PER)
            for n, (lo, hi, raw) in enumerate(((wa_lo, wa_hi, wa_raw), (wb_lo, wb_hi, wb_raw), (ww_lo, ww_hi, ww_raw))):
                dve.wait_ge(w_high, n + 1)
                nc.vector.tensor_tensor(lo[:, :, :], raw[:, :, :], f(hi[:, :, :]), ALU.subtract).then_inc(w_split, 1)
            dve.wait_ge(w_in, 64)
            dve.wait_ge(const_ok, 3)

            PER_LINKS = PER * 11

            with dve.Fori(0, TILES // PER) as i:
                done = [0]

                def link(ins):
                    done[0] += 1
                    ins.then_inc(chain, 1)
                    dve.wait_ge(chain, i * PER_LINKS + done[0])

                for kind, n in ORDER:
                    p, t = n % 2, i * PER + n
                    if kind == "a":
                        dve.wait_ge(x_in[n], i * 16 + 16)
                        link(nc.vector.bn_stats(ln6[:, :], xs[:, n, :]))
                        stand(dve, dve_passed)
                        link(nc.vector.bn_aggr(ln2[:, p, :], ln6[:, :]))
                        nc.vector.tensor_scalar(ln2[:, p, 1:2], ln2[:, p, 1:2], EPS_LN, None, ALU.add).then_inc(var_ok, 1)
                        dve.wait_ge(rstd_ok, t + 1)
                        if n >= 2:
                            dve.wait_ge(xt_full, t - 1)
                        else:
                            dve.wait_ge(xt_full, i * PER)
                        nc.vector.tensor_scalar(xn[:, p, :], xs[:, n, :], ln2[:, p, 0:1], rstd[:, p:p + 1],
                                                ALU.subtract, ALU.mult).then_inc(x_norm, 1)
                        dve.wait_ge(xt_high, t + 1)
                        nc.vector.tensor_tensor(xT_lo[:, p, :, :], ps_x[:, 0:H].rearrange("p (c s) -> p c s", c=KC),
                                                f(xT_hi[:, p, :, :]), ALU.subtract).then_inc(xt_low, 1)
                        dve.wait_ge(squared, t + 1)
                        link(nc.vector.tensor_reduce(norms[:, :], sq[:, p, :].rearrange("p (a r) -> p a r", r=R), AX.X,
                                                     ALU.add))
                        stand(dve, dve_passed)
                        link(nc.vector.max(m8[:, :], norms[:, :]))
                        last = m8[:, TOPK - 1:TOPK]
                        link(nc.vector.tensor_scalar(above[:, :], norms[:, :], last, None, ALU.is_gt))
                        link(nc.vector.tensor_reduce(nabove[:, :], above[:, :], AX.X, ALU.add))
                        link(nc.vector.tensor_scalar(equal[:, :], norms[:, :], last, None, ALU.is_equal))
                        link(nc.vector.tensor_tensor_scan(rank[:, :], ones[:, :], equal[:, :], nabove[:, 0:1],
                                                          ALU.mult, ALU.add))
                        link(nc.vector.tensor_scalar(keep[:, :], rank[:, :], float(TOPK), None, ALU.is_le))
                        link(nc.vector.tensor_tensor(keep[:, :], keep[:, :], equal[:, :], ALU.mult))
                        link(nc.vector.tensor_tensor(picked[:, p, :], above[:, :], keep[:, :], ALU.add))
                        nc.vector.tensor_tensor(masked[:, p, :].rearrange("p (a r) -> p a r", r=R),
                                                ps_v[:, p, :].rearrange("p (a r) -> p a r", r=R),
                                                picked[:, p, :].unsqueeze(2).to_broadcast([P, NA, R]),
                                                ALU.mult).then_inc(v_used, 1)
                        dve.wait_ge(v_used, t + 1)
                        nc.vector.tensor_reduce(v[:, p, :], masked[:, p, :].rearrange("p (a r) -> p r a", r=R), AX.X,
                                                ALU.add).then_inc(picked_ok, 1)
                        dve.wait_ge(picked_ok, t + 1)
                        if n >= 2:
                            dve.wait_ge(zt_full, 2 * t - 2)
                        else:
                            dve.wait_ge(zt_full, i * PER * 2)
                        nc.vector.scalar_tensor_tensor(z[:, p, :].rearrange("p (a r) -> p a r", r=R),
                                                       picked[:, p, :].unsqueeze(2).to_broadcast([P, NA, R]),
                                                       1.0 / TOPK ** 2, v[:, p, :].unsqueeze(1).to_broadcast([P, NA, R]),
                                                       ALU.mult, ALU.mult).then_inc(z_ok, 1)
                    else:
                        for q in range(2):
                            dve.wait_ge(zt_high, t * 2 + q + 1)
                            nc.vector.tensor_tensor(zT_lo[:, 4 * q:4 * q + 4, :],
                                                    ps_z[:, q, :].rearrange("p (a s) -> p a s", a=4),
                                                    f(zT_hi[:, 4 * q:4 * q + 4, :]), ALU.subtract).then_inc(zt_low, 1)
                        dve.wait_ge(y_full, t + 1)
                        dve.wait_ge(stored, 16 * PER * i)
                        nc.vector.tensor_tensor(y[:, n, :], ps_y[:, 0:H], bias_s[:, :], ALU.add).then_inc(y_read, 1)
                        dve.wait_ge(y_read, t + 1)
                        nc.vector.tensor_tensor(y[:, n, :], y[:, n, :], xs[:, n, :], ALU.add).then_inc(y_ok, 1)


HD1, NH1, G1, HPG1 = 16, 16, 4, 4
PAD = -3.0e38


def second_plan():
    tiles, per = NH1 * QT, HPG1 * QT

    def turns(g): return [[("qt", g, 0), ("qt", g, 1)], [("kt", g, 0), ("kt", g, 1)], [("kt", g, 2), ("kt", g, 3)]]
    steps = [("ctx", 0, 0), ("xt", 0, 0), ("qp", 0, 0), *(("kv", 0, j) for j in range(4)), *sum(turns(0), [])]
    for t in range(tiles + 3):
        g, at = divmod(t, per)
        work = turns(g + 1)[at // 2 - 1] if g + 1 < G1 and at in (2, 4, 6) else []
        if t < tiles:
            steps.append(("scores", t, 0))
        turn = [("turn", t - 1, j) for j in range(4)] if 1 <= t <= tiles else []
        exp = [("exp", t, 0)] if t < tiles else []
        if t % 2 == 0:
            steps += turn[:2] + exp + turn[2:3] + work[:1] + turn[3:] + work[1:]
        else:
            head = (t - 3) // 2
            pv = [("pv", head, j) for j in range(4)] if t >= 3 else []
            for j in range(4):
                steps += pv[j:j + 1] + turn[j:j + 1]
                if j == 1:
                    steps += exp
            if pv:
                steps.append(("take", head, 0))
    return steps + [("rows", 0, 0), ("rows", 1, 0), ("wo", 0, 0), ("wo", 1, 0)]


def second_attention(nc, x, out, ctxT, mask, alibi, wq, wkv, wo):
    steps = second_plan()
    bank_at, BANKS = count(steps, ("xt", "kv", "qp", "kt", "qt", "turn"))
    high_at, HIGHS = count(steps, ("turn",))
    acc_at, ACCS = count([s for s in steps if s[0] != "pv" or s[2] == 3], ("pv", "rows", "wo"))
    assert BANKS % 2 == 0 and ACCS % 2 == 0
    TILES = NH1 * QT
    ROWS = 4 * HD1

    with ExitStack() as ctx:
        def sb(name, shape, dt=F32):
            return ctx.enter_context(nc.sbuf_tensor("a1_" + name, shape, dt))

        def sem(name):
            return ctx.enter_context(nc.semaphore("a1_" + name))

        ctx_s = sb("ctx", [P, KC, SKP])
        wkv_s, wq_s, wo_s = sb("wkv", [P, KC, P]), sb("wq", [P, KC, H]), sb("wo", [P, HPG1, H])
        mask8 = sb("mask8", [P, SK], mybir.dt.uint8)
        maskt = sb("mask", [P, SKC])
        kv_raw = sb("kv_raw", [P, KT, P])
        k_rows = [sb(f"k_rows{i}", [P, KT, P]) for i in range(2)]
        q_rows = sb("q_rows", [P, QT, NH1, P])
        kk = [sb(f"kk{i}", [P, SKP], F32R) for i in range(2)]
        qq = sb("qq", [P, NH1, S], F32R)
        vv = sb("vv", [P, KT, G1, 2, HD1], F32R)
        q_raw = sb("q_raw", [P, QT, H])
        alibi_s = sb("alibi", [P, QT, NH1, 2])
        place = sb("place", [P, KT])
        prob = [sb(f"prob{i}", [P, SKP]) for i in range(2)]
        pt_hi, pt_lo = (sb(n, [P, KT, S], F32R) for n in ("pt_hi", "pt_lo"))
        heads = sb("heads", [P, HPG1, S])
        x_in, x_out, xn = sb("x_in", [P, QT, H]), sb("x_out", [P, QT, H]), sb("xn", [P, QT, H])
        xT = sb("xT", [P, KC, S])
        ident, half = sb("ident", [P, P]), sb("half", [P, QT])
        top, negmax = sb("top", [P, 2, 2]), sb("negmax", [P, 2])
        total, inv = sb("total", [P, QT * HPG1 * G1]), sb("inv", [P, QT * HPG1 * G1, P // G1])
        ln6, ln2, lnr = sb("ln6", [P, QT, 6]), sb("ln2", [P, QT, 2]), sb("lnr", [P, QT])

        ps_s = ctx.enter_context(nc.psum_tensor("a1_ps_s", [P, CHUNKS, BANK], F32))
        ps_t = ctx.enter_context(nc.psum_tensor("a1_ps_t", [P, 2, BANK], F32))
        ps_o = ctx.enter_context(nc.psum_tensor("a1_ps_o", [P, 2, BANK], F32))

        (w_in, al_in, const_set, const_ok, ctx_in, x_in_s, mask_in, mask_ok, ln_step, ln_var, ln_rstd, x_norm,
         al_step, q_high, q_low, v_high, v_split, k_high, k_low, bank_full, acc_full, scores_full, scored, negmax_ok,
         exp_ok, high_ok, pv_done, inv_ok, x_done, x_stored) = (
            sem(n) for n in ("w_in", "al_in", "const_set", "const_ok", "ctx_in", "x_in_s", "mask_in", "mask_ok",
                             "ln_step", "ln_var", "ln_rstd", "x_norm", "al_step", "q_high", "q_low", "v_high",
                             "v_split", "k_high", "k_low", "bank_full", "acc_full", "scores_full", "scored",
                             "negmax_ok", "exp_ok", "high_ok", "pv_done", "inv_ok", "x_done", "x_stored"))
        dve_passed, pool_passed, sp_passed = (sem(n) for n in ("dve_passed", "pool_passed", "sp_passed"))
        bank_free = [sem(f"bank_free{i}") for i in range(2)]
        acc_free = [sem(f"acc_free{i}") for i in range(2)]

        def f(ap):
            return ap.bitcast(F32)

        def r(ap):
            return ap.bitcast(F32R)

        def is_free(eng, b, step, done):
            at = bank_at[step]
            eng.wait_ge(bank_free[at % 2], b * (BANKS // 2) + at // 2 + done)
            return ps_t[:, at % 2, :]

        def acc_is_free(eng, b, step, done):
            at = acc_at[step]
            eng.wait_ge(acc_free[at % 2], b * (ACCS // 2) + at // 2 + done)
            return ps_o[:, at % 2, :]

        block = ctx.enter_context(nc.Block())

        @block.sync
        def _(sp):
            for t, src in ((wkv_s, wkv), (wq_s, wq), (wo_s, wo)):
                sp.dma_start(t[:, :, :], src).then_inc(w_in, 16)
            sp.dma_start(alibi_s[:, :, :, :], alibi.rearrange("(t p) h c -> p t h c", p=P)).then_inc(al_in, 16)
            with sp.Fori(0, B) as b:
                sp.wait_ge(x_done, b)
                sp.dma_start(x_in[:, :, :], x[b].rearrange("(t p) h -> p t h", p=P)).then_inc(x_in_s, 16)
                sp.wait_ge(mask_ok, b)
                stand(sp, sp_passed)
                sp.dma_start(mask8[:, :], mask[b].partition_broadcast(P)).then_inc(mask_in, 16)
                sp.wait_ge(bank_full, b * BANKS)
                sp.dma_start(ctx_s[:, :, :].rearrange("p c k -> p (c k)"), ctxT[b]).then_inc(ctx_in, 16)

        @block.gpsimd
        def _(pool):
            nc.gpsimd.memset(half[:, :], -0.5).then_inc(const_ok, 1)
            nc.gpsimd.memset(prob[0][:, SKC:], 0.0).then_inc(const_ok, 1)
            nc.gpsimd.memset(prob[1][:, SKC:], 0.0).then_inc(const_ok, 1)
            nc.gpsimd.memset(ident[:, :], 0.0).then_inc(const_set, 1)
            nc.gpsimd.memset(q_rows[:, :, :, :], 0.0).then_inc(const_set, 1)
            for t in k_rows:
                nc.gpsimd.memset(t[:, :, :], 0.0).then_inc(const_set, 1)
            nc.gpsimd.iota(place[:, :], pattern=[[P, KT]], base=0, channel_multiplier=1,
                           allow_small_or_imprecise_dtypes=True).then_inc(const_set, 1)
            pool.wait_ge(const_set, 5)
            nc.gpsimd.affine_select(out=ident[:, :], in_=ident[:, :], compare_op=ALU.not_equal, fill=1.0, base=0,
                                    pattern=[[-1, P]], channel_multiplier=1).then_inc(const_ok, 1)
            for t in k_rows:
                nc.gpsimd.tensor_scalar(t[:, :, ROWS:ROWS + 2], place[:, :].unsqueeze(2).to_broadcast([P, KT, 2]),
                                        1.0, None, ALU.mult).then_inc(const_ok, 1)
                nc.gpsimd.memset(t[:, :, ROWS + 2:ROWS + 4], 1.0).then_inc(const_ok, 1)
            pool.wait_ge(al_in, 16)
            for q in range(QT):
                hi, lo = q_rows[:, q, :, ROWS:ROWS + 4:2], q_rows[:, q, :, ROWS + 1:ROWS + 4:2]
                nc.gpsimd.tensor_scalar(r(hi), alibi_s[:, q, :, :], 1.0, None, ALU.mult).then_inc(al_step, 1)
                pool.wait_ge(al_step, q + 1)
                nc.gpsimd.tensor_tensor(lo, alibi_s[:, q, :, :], hi, ALU.subtract).then_inc(const_ok, 1)
            pool.wait_ge(const_ok, 10)

            with pool.Fori(0, B) as b:
                pool.wait_ge(ln_var, b * QT + QT)
                nc.gpsimd.tensor_tensor(lnr[:, :], ln2[:, :, 1], half[:, :], ALU.pow).then_inc(ln_rstd, 1)
                is_free(pool, b, ("qp", 0, 0), 1)
                pool.wait_ge(bank_full, b * BANKS)
                stand(pool, pool_passed)
                for q in range(QT):
                    src = q_raw[:, q, :].rearrange("p (h d) -> p h d", h=NH1)
                    hi = q_rows[:, q, :, 0:HD1]
                    nc.gpsimd.tensor_scalar(r(hi), src, 1.0, None, ALU.mult).then_inc(q_high, 1)
                    nc.gpsimd.tensor_scalar(r(q_rows[:, q, :, HD1:2 * HD1]), src, 1.0, None,
                                            ALU.mult).then_inc(q_high, 1)
                    pool.wait_ge(q_high, (b * QT + q) * 2 + 2)
                    for i in (2, 3):
                        nc.gpsimd.tensor_tensor(q_rows[:, q, :, i * HD1:(i + 1) * HD1], src, hi,
                                                ALU.subtract).then_inc(q_low, 1)
                is_free(pool, b, ("kv", 0, 3), 1)
                is_free(pool, b, ("kv", 0, 2), 1)
                stand(pool, pool_passed)
                for g in range(G1):
                    if g >= 2:
                        pool.wait_ge(bank_full, b * BANKS + bank_at["kt", g - 2, 3] + 1)
                        stand(pool, pool_passed)
                    t = k_rows[g % 2]
                    src = kv_raw[:, :, g * HD1:(g + 1) * HD1]
                    for i in (0, 2):
                        nc.gpsimd.tensor_scalar(r(t[:, :, i * HD1:(i + 1) * HD1]), src, 1.0, None,
                                                ALU.mult).then_inc(k_high, 1)
                    pool.wait_ge(k_high, (b * G1 + g) * 2 + 2)
                    for i in (1, 3):
                        nc.gpsimd.tensor_tensor(t[:, :, i * HD1:(i + 1) * HD1], src, t[:, :, 0:HD1],
                                                ALU.subtract).then_inc(k_low, 1)
                    if g == 0:
                        pool.wait_ge(pv_done, b * NH1 * 4)
                        stand(pool, pool_passed)
                        for i in range(G1):
                            v = kv_raw[:, :, P // 2 + i * HD1:P // 2 + (i + 1) * HD1]
                            nc.gpsimd.tensor_scalar(vv[:, :, i, 0, :], v, 1.0, None, ALU.mult).then_inc(v_high, 1)
                        pool.wait_ge(v_high, (b + 1) * G1)
                        for i in range(G1):
                            v = kv_raw[:, :, P // 2 + i * HD1:P // 2 + (i + 1) * HD1]
                            nc.gpsimd.tensor_tensor(vv[:, :, i, 1, :], v, f(vv[:, :, i, 0, :]),
                                                    ALU.subtract).then_inc(v_split, 1)

        @block.tensor
        def _(pe):
            pe.wait_ge(const_ok, 10)
            pe.wait_ge(w_in, 48)

            with pe.Fori(0, B) as b:
                for kind, n, j in steps:
                    if kind in ("xt", "qp", "kv", "kt", "qt", "turn"):
                        ps = is_free(pe, b, (kind, n, j), 0)
                    if kind == "xt":
                        pe.wait_ge(x_norm, b * QT + QT)
                        for c in range(KC):
                            for q in range(QT):
                                mm = nc.tensor.transpose(ps[:, c * S + q * P:c * S + (q + 1) * P],
                                                         xn[:, q, c * P:(c + 1) * P], ident[:, :])
                        mm.then_inc(bank_full, 1)
                    elif kind == "qp":
                        is_free(pe, b, ("xt", 0, 0), 1)
                        for q in range(QT):
                            for c in range(KC):
                                mm = nc.tensor.matmul(ps[:, q * H:(q + 1) * H], xT[:, c, q * P:(q + 1) * P],
                                                      wq_s[:, c, :], start=c == 0, stop=c == KC - 1)
                        mm.then_inc(bank_full, 1)
                    elif kind == "kv":
                        if j == 0:
                            pe.wait_ge(ctx_in, b * 16 + 16)
                        for i, k in enumerate(KGROUPS[j]):
                            for c in range(KC):
                                mm = nc.tensor.matmul(ps[:, i * P:(i + 1) * P], ctx_s[:, c, k * P:(k + 1) * P],
                                                      wkv_s[:, c, :], start=c == 0, stop=c == KC - 1)
                        mm.then_inc(bank_full, 1)
                    elif kind == "kt":
                        pe.wait_ge(k_low, (b * G1 + n) * 2 + 2)
                        for i, k in enumerate(KGROUPS[j]):
                            mm = nc.tensor.transpose(ps[:, i * P:(i + 1) * P], k_rows[n % 2][:, k, :], ident[:, :])
                        mm.then_inc(bank_full, 1)
                    elif kind == "qt":
                        pe.wait_ge(q_low, (b * QT + QT) * 2)
                        for i in range(HPG1):
                            mm = nc.tensor.transpose(ps[:, i * P:(i + 1) * P], q_rows[:, j, n * HPG1 + i, :],
                                                     ident[:, :])
                        mm.then_inc(bank_full, 1)
                    elif kind == "scores":
                        head, q = divmod(n, QT)
                        g = head // HPG1
                        if n % (HPG1 * QT) == 0:
                            for s in (("kt", g, 2), ("kt", g, 3)):
                                is_free(pe, b, s, 1)
                        for c in range(CHUNKS):
                            if c % 2 == 0:
                                pe.wait_ge(scored, (b * TILES + n) * 2 + c // 2)
                            mm = nc.tensor.matmul(ps_s[:, c, 0:CW], qq[:, head, q * P:(q + 1) * P],
                                                  kk[g % 2][:, c * CW:(c + 1) * CW], start=True, stop=True)
                            if c % 2:
                                mm.then_inc(scores_full, 1)
                    elif kind == "turn":
                        pe.wait_ge(exp_ok, b * TILES + n + 1)
                        for i, k in enumerate(KGROUPS[j]):
                            mm = nc.tensor.transpose(ps[:, i * P:(i + 1) * P], prob[n % 2][:, k * P:(k + 1) * P],
                                                     ident[:, :])
                        mm.then_inc(bank_full, 1)
                    elif kind == "pv":
                        ps = ps_o[:, acc_at["pv", n, 3] % 2, :]
                        if j == 0:
                            acc_is_free(pe, b, ("pv", n, 3), 0)
                            if n == 0:
                                pe.wait_ge(v_split, (b + 1) * G1)
                        is_free(pe, b, ("turn", 2 * n + 1, j), 1)
                        for k in KGROUPS[j]:
                            v = vv[:, k, :, :, :].rearrange("p g c d -> p (g c d)")
                            nc.tensor.matmul(ps[:, 0:S], v, pt_hi[:, k, :], start=k == 0, stop=False)
                            mm = nc.tensor.matmul(ps[:, 0:S], v, pt_lo[:, k, :], start=False, stop=k == KT - 1)
                        mm.then_inc(pv_done, 1)
                    elif kind == "rows":
                        ps = acc_is_free(pe, b, (kind, n, j), 0)
                        pe.wait_ge(inv_ok, b + 1)
                        for i in range(2):
                            for q in range(QT):
                                mm = nc.tensor.matmul(
                                    ps[:, i * S + q * P:i * S + (q + 1) * P],
                                    inv[:, (q * HPG1 + 2 * n + i) * G1:(q * HPG1 + 2 * n + i + 1) * G1, :].rearrange(
                                        "p g r -> p (g r)"),
                                    ident[:, :], start=True, stop=True)
                        mm.then_inc(acc_full, 1)
                    elif kind == "wo":
                        ps = acc_is_free(pe, b, (kind, n, j), 0)
                        for s in (("rows", 0, 0), ("rows", 1, 0)):
                            acc_is_free(pe, b, s, 1)
                        for i in range(HPG1):
                            mm = nc.tensor.matmul(ps[:, 0:H], heads[:, i, n * P:(n + 1) * P], wo_s[:, i, :],
                                                  start=i == 0, stop=i == HPG1 - 1)
                        mm.then_inc(acc_full, 1)

        @block.scalar
        def _(act):
            with act.Fori(0, B) as b:
                for kind, n, j in steps:
                    if kind in ("kt", "qt", "turn"):
                        at = bank_at[kind, n, j]
                        act.wait_ge(bank_full, b * BANKS + at + 1)
                        ps = ps_t[:, at % 2, :]
                        w, k0 = len(KGROUPS[j]), KGROUPS[j][0]
                        if kind == "kt":
                            act.wait_ge(scored, (b * TILES + max(n - 1, 0) * HPG1 * QT) * 2)
                            nc.scalar.copy(kk[n % 2][:, k0 * P:(k0 + w) * P], ps[:, 0:w * P]).then_inc(
                                bank_free[at % 2], 1)
                        elif kind == "qt":
                            act.wait_ge(scored, b * TILES * 2)
                            nc.scalar.copy(qq[:, n * HPG1:(n + 1) * HPG1, j * P:(j + 1) * P],
                                           ps.rearrange("p (h s) -> p h s", h=HPG1)).then_inc(bank_free[at % 2], 1)
                        else:
                            head, q = divmod(n, QT)
                            if q == 0:
                                act.wait_ge(pv_done, (b * NH1 + head) * 4 - 4 + j + 1 if head else b * NH1 * 4)
                            nc.scalar.copy(pt_hi[:, k0:k0 + w, q * P:(q + 1) * P],
                                           ps[:, 0:w * P].rearrange("p (k s) -> p k s", k=w)).then_inc(high_ok, 1)
                    elif kind == "exp":
                        head, q = divmod(n, QT)
                        act.wait_ge(negmax_ok, b * TILES + n + 1)
                        if n == 0:
                            act.wait_ge(inv_ok, b)
                        at = (q * HPG1 + head % HPG1) * G1 + head // HPG1
                        nc.scalar.activation(prob[n % 2][:, 0:SKC], prob[n % 2][:, 0:SKC], ACT.Exp,
                                             bias=negmax[:, n % 2:n % 2 + 1], scale=1.0,
                                             accum_out=total[:, at:at + 1]
                                             ).then_inc(exp_ok, 1)
                    elif kind == "take":
                        g, i = divmod(n, HPG1)
                        at = acc_at["pv", n, 3]
                        act.wait_ge(pv_done, (b * NH1 + n) * 4 + 4)
                        if n == 0:
                            act.wait_ge(acc_full, b * 4)
                        own = slice(g * P // G1, (g + 1) * P // G1)
                        nc.scalar.copy(heads[own, i, :], ps_o[own, at % 2, 0:S]).then_inc(acc_free[at % 2], 1)
                act.wait_ge(x_done, b + 1)
                act.dma_start(out[b].rearrange("(t p) h -> p t h", p=P), x_out[:, :, :]).then_inc(x_stored, 16)
            act.wait_ge(x_stored, 16 * B)

        @block.vector
        def _(dve):
            with dve.Fori(0, B) as b:
                for kind, n, j in steps:
                    if kind == "ctx":
                        dve.wait_ge(x_in_s, b * 16 + 16)
                        for q in range(QT):
                            nc.vector.bn_stats(ln6[:, q, :], x_in[:, q, :]).then_inc(ln_step, 1)
                            dve.wait_ge(ln_step, (b * QT + q) * 2 + 1)
                            stand(dve, dve_passed)
                            nc.vector.bn_aggr(ln2[:, q, :], ln6[:, q, :]).then_inc(ln_step, 1)
                            dve.wait_ge(ln_step, (b * QT + q) * 2 + 2)
                            nc.vector.tensor_scalar(ln2[:, q, 1:2], ln2[:, q, 1:2], EPS_LN, None,
                                                    ALU.add).then_inc(ln_var, 1)
                        dve.wait_ge(ln_rstd, b + 1)
                        for q in range(QT):
                            nc.vector.tensor_scalar(xn[:, q, :], x_in[:, q, :], ln2[:, q, 0:1], lnr[:, q:q + 1],
                                                    ALU.subtract, ALU.mult).then_inc(x_norm, 1)
                        dve.wait_ge(mask_in, b * 16 + 16)
                        nc.vector.memset(maskt[:, SK:], PAD)
                        nc.vector.tensor_scalar(maskt[:, 0:SK], mask8[:, :], -NEG, NEG, ALU.mult,
                                                ALU.add).then_inc(mask_ok, 1)
                    elif kind in ("xt", "qp", "kv"):
                        at = bank_at[kind, n, j]
                        dve.wait_ge(bank_full, b * BANKS + at + 1)
                        ps = ps_t[:, at % 2, :]
                        if kind == "xt":
                            nc.vector.tensor_copy(xT[:, :, :].rearrange("p c s -> p (c s)"), ps).then_inc(
                                bank_free[at % 2], 1)
                        elif kind == "qp":
                            nc.vector.tensor_scalar(q_raw[:, :, :].rearrange("p t h -> p (t h)"), ps,
                                                    float(HD1) ** -0.5, None, ALU.mult).then_inc(bank_free[at % 2], 1)
                        else:
                            if j == 0:
                                dve.wait_ge(k_low, b * G1 * 2)
                                dve.wait_ge(v_split, b * G1)
                            w, k0 = len(KGROUPS[j]), KGROUPS[j][0]
                            nc.vector.tensor_copy(kv_raw[:, k0:k0 + w, :].rearrange("p k d -> p (k d)"),
                                                  ps[:, 0:w * P]).then_inc(bank_free[at % 2], 1)
                    elif kind == "turn":
                        at = bank_at[kind, n, j]
                        dve.wait_ge(high_ok, b * HIGHS + high_at[kind, n, j] + 1)
                        w, k0 = len(KGROUPS[j]), KGROUPS[j][0]
                        q = slice(n % QT * P, (n % QT + 1) * P)
                        nc.vector.tensor_tensor(pt_lo[:, k0:k0 + w, q],
                                                ps_t[:, at % 2, 0:w * P].rearrange("p (k s) -> p k s", k=w),
                                                f(pt_hi[:, k0:k0 + w, q]), ALU.subtract).then_inc(bank_free[at % 2], 1)
                    elif kind == "scores":
                        if n == 0:
                            dve.wait_ge(mask_ok, b + 1)
                        if n >= 2:
                            dve.wait_ge(bank_full, b * BANKS + bank_at["turn", n - 2, 3] + 1)
                        for c in range(2):
                            dve.wait_ge(scores_full, (b * TILES + n) * 2 + c + 1)
                            stand(dve, dve_passed)
                            k = slice(2 * c * CW, (2 * c + 2) * CW)
                            nc.vector.tensor_tensor_reduce(
                                prob[n % 2][:, k].rearrange("p (c k) -> p c k", c=2), ps_s[:, 2 * c:2 * c + 2, 0:CW],
                                maskt[:, k].rearrange("p (c k) -> p c k", c=2), 1.0, -3.4e38, ALU.add,
                                ALU.max, top[:, n % 2, c:c + 1]).then_inc(scored, 1)
                        dve.wait_ge(scored, (b * TILES + n) * 2 + 2)
                        nc.vector.tensor_reduce(negmax[:, n % 2:n % 2 + 1], top[:, n % 2, :], AX.X, ALU.max,
                                                negate=True).then_inc(negmax_ok, 1)
                    elif kind == "rows":
                        if n == 0:
                            dve.wait_ge(exp_ok, (b + 1) * TILES)
                            nc.vector.reciprocal(inv[:, :, :], total[:, :].unsqueeze(2).to_broadcast([P, QT * HPG1 * G1, P // G1])).then_inc(inv_ok, 1)
                        at = acc_at[kind, n, j]
                        dve.wait_ge(acc_full, b * 4 + n + 1)
                        acc_is_free(dve, b, ("pv", NH1 - 1, 3), 1)
                        acc_is_free(dve, b, ("pv", NH1 - 2, 3), 1)
                        h = heads[:, 2 * n:2 * n + 2, :].rearrange("p h s -> p (h s)")
                        nc.vector.tensor_tensor(h, ps_o[:, at % 2, :], h, ALU.mult).then_inc(acc_free[at % 2], 1)
                    elif kind == "wo":
                        at = acc_at[kind, n, j]
                        dve.wait_ge(acc_full, b * 4 + 2 + n + 1)
                        if n == 0:
                            dve.wait_ge(x_stored, b * 16)
                        nc.vector.tensor_tensor(x_out[:, n, :], ps_o[:, at % 2, 0:H], x_in[:, n, :],
                                                ALU.add).then_inc(acc_free[at % 2], 1)
                        if n == 1:
                            acc_is_free(dve, b, ("wo", 0, 0), 1)
                            acc_is_free(dve, b, ("wo", 1, 0), 1)
                            nc.vector.memset(top[:, :, :], 0.0).then_inc(x_done, 1)


NE, INNER, TOP2 = 8, 704, 2
IT = -(-INNER // P)
Q_IN, Q_MIN = 128, -128
MAGIC = 1.5 * 2.0 ** 23


def second_ffn(nc, x, out, wg, w13, w2, table):
    TILES = B * S // P
    BLK = 4
    BLOCKS = TILES // BLK
    NT = -Q_MIN + 1

    with ExitStack() as ctx:
        def sb(name, shape, dt=F32):
            return ctx.enter_context(nc.sbuf_tensor("f1_" + name, shape, dt))

        def sem(name):
            return ctx.enter_context(nc.semaphore("f1_" + name))

        acc = sb("acc", [P, TILES, H])
        xT_hi, xT_lo = (sb(n, [P, KC, TILES * P], F32R) for n in ("xT_hi", "xT_lo"))
        weight = sb("weight", [P, TILES, NE])
        wg_raw = sb("wg_raw", [P, KC, NE])
        table_s, steps_s = sb("table", [P, NT]), sb("steps", [P, NT])
        w13_raw, w2_raw = sb("w13_raw", [P, 2, KC, IT * P]), sb("w2_raw", [P, IT, H])
        w13_hi, w13_lo = ([sb(f"{n}{i}", [P, 2, KC, IT * P], F32R) for i in range(2)] for n in ("w13_hi", "w13_lo"))
        w2_hi, w2_lo = ([sb(f"{n}{i}", [P, IT, H], F32R) for i in range(2)] for n in ("w2_hi", "w2_lo"))
        ident, half = sb("ident", [P, P]), sb("half", [P, 1])
        xn, xT = sb("xn", [P, H]), sb("xT", [P, KC, P])
        ln6, ln2, rstd = sb("ln6", [P, 6]), sb("ln2", [P, 2]), sb("rstd", [P, 1])
        level, top = sb("level", [P, NE]), sb("top", [P, 1])
        onehot = sb("onehot", [P, NE, NT])
        value, prob = sb("value", [P, NE]), sb("prob", [P, NE])
        total, m8 = sb("total", [P, 1]), sb("m8", [P, 8])
        above, equal, rank, keep, ones = (sb(n, [P, NE]) for n in ("above", "equal", "rank", "keep", "ones"))
        nabove = sb("nabove", [P, 1])
        gate = sb("gate", [P, 2, BLK * P])
        h_raw = sb("h_raw", [P, 2, BLK * P])
        h_hi, h_lo = (sb(n, [P, IT, BLK * P], F32R) for n in ("h_hi", "h_lo"))

        ps_h = ctx.enter_context(nc.psum_tensor("f1_ps_h", [P, 2, 2, BANK], F32))
        ps_y = ctx.enter_context(nc.psum_tensor("f1_ps_y", [P, 2, BANK], F32))
        ps_x = ctx.enter_context(nc.psum_tensor("f1_ps_x", [P, BANK], F32))
        ps_l = ctx.enter_context(nc.psum_tensor("f1_ps_l", [P, BANK], F32))

        (c_in, x_in, w_in, const_set, const_ok, chain, var_ok, rstd_ok, x_norm, xt_full, xt_ok, xt_high, xt_low,
         l_full, l_read, w_high, w_low, h_full, gate_ok, h_ok, h_high, h_split, y_full, y_read, stored, weight_sum,
         weight_ok) = (
            sem(n) for n in ("c_in", "x_in", "w_in", "const_set", "const_ok", "chain", "var_ok", "rstd_ok", "x_norm",
                             "xt_full", "xt_ok", "xt_high", "xt_low", "l_full", "l_read", "w_high", "w_low", "h_full",
                             "gate_ok", "h_ok", "h_high", "h_split", "y_full", "y_read", "stored",
                             "weight_sum", "weight_ok"))

        dve_passed, pe_passed, sp_passed = sem("dve_passed"), sem("pe_passed"), sem("sp_passed")

        def f(ap):
            return ap.bitcast(F32)

        block = ctx.enter_context(nc.Block())

        @block.sync
        def _(sp):
            sp.dma_start(acc[:, :, :], x.rearrange("t p h -> p t h")).then_inc(x_in, 16)
            sp.dma_start(wg_raw[:, :, :], wg).then_inc(c_in, 16)
            sp.dma_start(table_s[:, :], table[0].partition_broadcast(P)).then_inc(c_in, 16)
            sp.dma_start(steps_s[:, :], table[1].partition_broadcast(P)).then_inc(c_in, 16)
            with sp.Fori(0, NE) as e:
                sp.wait_ge(w_low, e * 2)
                stand(sp, sp_passed)
                sp.dma_start(w13_raw[:, :, :, :], w13[e]).then_inc(w_in, 16)
                sp.dma_start(w2_raw[:, :, :], w2[e]).then_inc(w_in, 16)
            sp.wait_ge(y_read, NE * TILES + 1)
            sp.dma_start(out.rearrange("t p h -> p t h"), acc[:, :, :]).then_inc(stored, 16)
            sp.wait_ge(stored, 16)

        @block.gpsimd
        def _(pool):
            nc.gpsimd.memset(half[:, :], -0.5).then_inc(const_ok, 1)
            nc.gpsimd.memset(ones[:, :], 1.0).then_inc(const_ok, 1)
            nc.gpsimd.memset(ident[:, :], 0.0).then_inc(const_set, 1)
            pool.wait_ge(const_set, 1)
            nc.gpsimd.affine_select(out=ident[:, :], in_=ident[:, :], compare_op=ALU.not_equal, fill=1.0, base=0,
                                    pattern=[[-1, P]], channel_multiplier=1).then_inc(const_ok, 1)
            pool.wait_ge(const_ok, 3)
            with pool.Fori(0, TILES) as t:
                pool.wait_ge(var_ok, t + 1)
                nc.gpsimd.tensor_tensor(rstd[:, :], ln2[:, 1:2], half[:, :], ALU.pow).then_inc(rstd_ok, 1)

            def weights(e, i):
                pool.wait_ge(w_in, e * 32 + 32)
                pool.wait_ge(w_high, e * 2 + 2)
                nc.gpsimd.tensor_tensor(w13_lo[i][:, :, :, :], w13_raw[:, :, :, :], f(w13_hi[i][:, :, :, :]),
                                        ALU.subtract).then_inc(w_low, 1)
                nc.gpsimd.tensor_tensor(w2_lo[i][:, :, :], w2_raw[:, :, :], f(w2_hi[i][:, :, :]),
                                        ALU.subtract).then_inc(w_low, 1)

            weights(0, 0)
            def experts(pair, more):
                for i in range(2):
                    e = pair * 2 + i
                    for blk in range(BLOCKS):
                        for m in range(IT):
                            n = (e * BLOCKS + blk) * IT + m
                            pool.wait_ge(h_high, n + 1)
                            nc.gpsimd.tensor_tensor(h_lo[:, m, :], h_raw[:, m % 2, :], f(h_hi[:, m, :]),
                                                    ALU.subtract).then_inc(h_split, 1)
                        if blk == 0 and i == 0:
                            weights(e + 1, 1)
                        if blk == 0 and i == 1 and more:
                            weights(e + 1, 0)

            with pool.Fori(0, NE // 2 - 1) as pair:
                experts(pair, True)
            experts(NE // 2 - 1, False)

        @block.tensor
        def _(pe):
            pe.wait_ge(const_ok, 3)
            pe.wait_ge(c_in, 48)
            with pe.Fori(0, TILES) as t:
                pe.wait_ge(x_norm, t + 1)
                for c in range(KC):
                    mm = nc.tensor.transpose(ps_x[:, c * P:(c + 1) * P], xn[:, c * P:(c + 1) * P], ident[:, :])
                mm.then_inc(xt_full, 1)
                pe.wait_ge(xt_ok, t + 1)
                pe.wait_ge(l_read, t)
                for c in range(KC):
                    mm = nc.tensor.matmul(ps_l[:, 0:NE], xT[:, c, :], wg_raw[:, c, :], start=c == 0, stop=c == KC - 1)
                mm.then_inc(l_full, 1)
            pe.wait_ge(xt_high, TILES)
            pe.wait_ge(xt_low, TILES)

            def split_mm(to, lhs, rhs, first, last):
                (lh, ll), (rh, rl) = lhs, rhs
                nc.tensor.matmul(to, lh, rh, start=first, stop=False)
                nc.tensor.matmul(to, ll, rh, start=False, stop=False)
                return nc.tensor.matmul(to, lh, rl, start=False, stop=last)

            with pe.Fori(0, NE // 2) as pair:
                for i in range(2):
                    e = pair * 2 + i
                    pe.wait_ge(w_low, e * 2 + 2)
                    stand(pe, pe_passed)
                    with pe.Fori(0, BLOCKS) as blk:
                        it = e * BLOCKS + blk
                        for m in range(IT):
                            n = it * IT + m
                            pe.wait_ge(h_ok, n)
                            for g in range(2):
                                for c in range(KC):
                                    mm = split_mm(ps_h[:, m % 2, g, :],
                                                  (w13_hi[i][:, g, c, m * P:(m + 1) * P], w13_lo[i][:, g, c, m * P:(m + 1) * P]),
                                                  (xT_hi[:, c, bass.ts(blk, BLK * P)], xT_lo[:, c, bass.ts(blk, BLK * P)]),
                                                  c == 0, c == KC - 1)
                            mm.then_inc(h_full, 1)
                        for q in range(BLK):
                            pe.wait_ge(y_read, it * BLK + q)
                            for m in range(IT):
                                if q == 0:
                                    pe.wait_ge(h_split, it * IT + m + 1)
                                k = slice(q * P, (q + 1) * P)
                                mm = split_mm(ps_y[:, q % 2, 0:H], (h_hi[:, m, k], h_lo[:, m, k]),
                                              (w2_hi[i][:, m, :], w2_lo[i][:, m, :]), m == 0, m == IT - 1)
                            mm.then_inc(y_full, 1)

        @block.scalar
        def _(act):
            with act.Fori(0, TILES) as t:
                act.wait_ge(xt_ok, t + 1)
                nc.scalar.copy(xT_hi[:, :, bass.ts(t, P)], xT[:, :, :]).then_inc(xt_high, 1)

            def weights(e, i):
                act.wait_ge(w_in, e * 32 + 32)
                nc.scalar.copy(w13_hi[i][:, :, :, :], w13_raw[:, :, :, :]).then_inc(w_high, 1)
                nc.scalar.copy(w2_hi[i][:, :, :], w2_raw[:, :, :]).then_inc(w_high, 1)

            weights(0, 0)
            def experts(pair, more):
                for i in range(2):
                    e = pair * 2 + i
                    for blk in range(BLOCKS):
                        for m in range(IT):
                            n = (e * BLOCKS + blk) * IT + m
                            act.wait_ge(h_full, n + 1)
                            if m < 2:
                                act.wait_ge(h_ok, (e * BLOCKS + blk) * IT + 1)
                            else:
                                act.wait_ge(h_ok, n)
                            nc.scalar.activation(gate[:, m % 2, :], ps_h[:, m % 2, 0, :], ACT.Silu).then_inc(gate_ok, 1)
                            act.wait_ge(h_ok, n + 2)
                            act.wait_ge(y_full, (e * BLOCKS + blk) * BLK)
                            nc.scalar.copy(h_hi[:, m, :], h_raw[:, m % 2, :]).then_inc(h_high, 1)
                        if blk == 0 and i == 0:
                            act.wait_ge(y_full, e * BLOCKS * BLK)
                            weights(e + 1, 1)
                        if blk == 0 and i == 1 and more:
                            act.wait_ge(y_full, e * BLOCKS * BLK)
                            weights(e + 1, 0)

            with act.Fori(0, NE // 2 - 1) as pair:
                experts(pair, True)
            experts(NE // 2 - 1, False)

        @block.vector
        def _(dve):
            nc.vector.memset(m8[:, :], 0.0).then_inc(h_ok, 1)
            nc.vector.memset(total[:, :], 0.0).then_inc(y_read, 1)
            dve.wait_ge(x_in, 16)
            dve.wait_ge(c_in, 48)
            dve.wait_ge(const_ok, 3)
            LINKS = 19
            with dve.Fori(0, TILES) as t:
                done = [0]

                def link(ins):
                    done[0] += 1
                    ins.then_inc(chain, 1)
                    dve.wait_ge(chain, t * LINKS + done[0])

                link(nc.vector.bn_stats(ln6[:, :], acc[:, bass.ds(t, 1), :].rearrange("p o h -> p (o h)")))
                stand(dve, dve_passed)
                link(nc.vector.bn_aggr(ln2[:, :], ln6[:, :]))
                nc.vector.tensor_scalar(ln2[:, 1:2], ln2[:, 1:2], EPS_LN, None, ALU.add).then_inc(var_ok, 1)
                dve.wait_ge(rstd_ok, t + 1)
                dve.wait_ge(xt_full, t)
                nc.vector.tensor_scalar(xn[:, :], acc[:, bass.ds(t, 1), :].rearrange("p o h -> p (o h)"), ln2[:, 0:1],
                                        rstd[:, :], ALU.subtract, ALU.mult).then_inc(x_norm, 1)
                dve.wait_ge(xt_full, t + 1)
                dve.wait_ge(xt_high, t)
                dve.wait_ge(l_full, t)
                nc.vector.tensor_copy(xT[:, :, :], ps_x[:, 0:H].rearrange("p (c s) -> p c s", c=KC)).then_inc(xt_ok, 1)
                dve.wait_ge(xt_high, t + 1)
                nc.vector.tensor_tensor(xT_lo[:, :, bass.ts(t, P)], xT[:, :, :], f(xT_hi[:, :, bass.ts(t, P)]),
                                        ALU.subtract).then_inc(xt_low, 1)
                dve.wait_ge(l_full, t + 1)
                link(nc.vector.tensor_scalar(level[:, :], ps_l[:, 0:NE], float(Q_IN), MAGIC, ALU.mult, ALU.add))
                nc.vector.tensor_scalar(level[:, :], level[:, :], MAGIC, None, ALU.subtract).then_inc(l_read, 1)
                dve.wait_ge(l_read, t + 1)
                link(nc.vector.tensor_reduce(top[:, :], level[:, :], AX.X, ALU.max))
                link(nc.vector.tensor_scalar(level[:, :], level[:, :], top[:, :], float(Q_MIN), ALU.subtract, ALU.max))
                link(nc.vector.tensor_tensor(onehot[:, :, :], level[:, :].unsqueeze(2).to_broadcast([P, NE, NT]),
                                             steps_s[:, :].unsqueeze(1).to_broadcast([P, NE, NT]), ALU.is_equal))
                link(nc.vector.tensor_tensor(onehot[:, :, :], onehot[:, :, :],
                                             table_s[:, :].unsqueeze(1).to_broadcast([P, NE, NT]), ALU.mult))
                link(nc.vector.tensor_reduce(value[:, :], onehot[:, :, :], AX.X, ALU.add))
                link(nc.vector.tensor_reduce(total[:, :], value[:, :], AX.X, ALU.add))
                link(nc.vector.reciprocal(total[:, :], total[:, :]))
                link(nc.vector.tensor_scalar(prob[:, :], value[:, :], total[:, :], None, ALU.mult))
                stand(dve, dve_passed)
                link(nc.vector.max(m8[:, :], value[:, :]))
                last = m8[:, TOP2 - 1:TOP2]
                link(nc.vector.tensor_scalar(above[:, :], value[:, :], last, None, ALU.is_gt))
                link(nc.vector.tensor_reduce(nabove[:, :], above[:, :], AX.X, ALU.add))
                link(nc.vector.tensor_scalar(equal[:, :], value[:, :], last, None, ALU.is_equal))
                link(nc.vector.tensor_tensor_scan(rank[:, :], ones[:, :], equal[:, :], nabove[:, 0:1], ALU.mult, ALU.add))
                link(nc.vector.scalar_tensor_tensor(keep[:, :], rank[:, :], float(TOP2), equal[:, :], ALU.is_le, ALU.mult))
                link(nc.vector.tensor_tensor(keep[:, :], above[:, :], keep[:, :], ALU.add))
                link(nc.vector.tensor_tensor(prob[:, :], prob[:, :], keep[:, :], ALU.mult))
                nc.vector.tensor_reduce(total[:, :], prob[:, :], AX.X, ALU.add).then_inc(weight_sum, 1)
                dve.wait_ge(weight_sum, 2 * t + 1)
                nc.vector.reciprocal(total[:, :], total[:, :]).then_inc(weight_sum, 1)
                dve.wait_ge(weight_sum, 2 * t + 2)
                nc.vector.tensor_scalar(weight[:, bass.ds(t, 1), :].rearrange("p o e -> p (o e)"), prob[:, :],
                                        total[:, :], None, ALU.mult).then_inc(weight_ok, 1)

            dve.wait_ge(weight_ok, TILES)
            with dve.Fori(0, NE // 2) as pair:
                for i in range(2):
                    e = pair * 2 + i
                    for blk in range(BLOCKS):
                        it = e * BLOCKS + blk
                        for m in range(IT):
                            n = it * IT + m
                            dve.wait_ge(gate_ok, n + 1)
                            if m < 2:
                                dve.wait_ge(h_split, it * IT)
                            else:
                                dve.wait_ge(h_split, n - 1)
                            nc.vector.tensor_tensor(h_raw[:, m % 2, :], gate[:, m % 2, :], ps_h[:, m % 2, 1, :],
                                                    ALU.mult).then_inc(h_ok, 1)
                        for q in range(BLK):
                            t = blk * BLK + q
                            dve.wait_ge(y_full, it * BLK + q + 1)
                            nc.vector.scalar_tensor_tensor(
                                acc[:, t, :], ps_y[:, q % 2, 0:H],
                                weight[:, t, bass.ds(e, 1)], acc[:, t, :], ALU.mult, ALU.add).then_inc(y_read, 1)


def network(nc, x, mask_q, mask_k, ctxT, wq0, wkv0, wo0, bias0, qn, kn, wa, wb, ww, bias_f, alibi, wq1, wkv1, wo1,
            wg, w13, w2, table, out):
    def rows(name):
        return nc.dram_tensor(name, (B, S, H), F32, kind="Internal").ap()

    def tiles(a):
        return a.rearrange("b (t p) h -> (b t) p h", p=P)

    x1, x2, x3 = rows("x1"), rows("x2"), rows("x3")
    first_attention(nc, x, x1, ctxT, mask_q, wq0, wkv0, wo0, bias0, qn, kn)
    first_ffn(nc, tiles(x1), tiles(x2), wa, wb, ww, bias_f)
    second_attention(nc, x2, x3, ctxT, mask_k, alibi, wq1, wkv1, wo1)
    second_ffn(nc, tiles(x3), tiles(out), wg, w13, w2, table)


def _sliced(np, w, kc):
    return np.ascontiguousarray(w.reshape(kc, w.shape[0] // kc, -1).transpose(1, 0, 2))


def _grouped(np, w, groups):
    n = w.shape[1] // groups
    return w.reshape(KC, P, groups, n).transpose(2, 1, 0, 3)


def kernel(**inputs):
    import numpy as np
    import concourse.bacc as _bacc
    from concourse import mybir as _mybir
    from concourse.bass_utils import run_bass_kernel_spmd as _run

    a = {k: np.asarray(v) for k, v in inputs.items()}
    f32 = np.float32

    ctxT = np.zeros((B, H, SKP), f32)
    ctxT[:, :, :SK] = a["ctx_2048"].transpose(0, 2, 1)
    w1, w3, w2 = a["L1_ffn_w1"], a["L1_ffn_w3"], a["L1_ffn_w2"]
    w13 = np.zeros((NE, 2, H, IT * P), f32)
    w13[:, 0, :, :INNER] = w1.transpose(0, 2, 1)
    w13[:, 1, :, :INNER] = w3.transpose(0, 2, 1)
    w2T = np.zeros((NE, IT * P, H), f32)
    w2T[:, :INNER] = w2.transpose(0, 2, 1)
    wo1 = np.repeat(a["L1_xattn_Wo"].reshape(G1, HPG1, 1, HD1, H), 2, axis=2)

    slopes = f32(2.0 ** -0.5) ** np.arange(1, NH1 + 1, dtype=f32)
    alibi = np.zeros((S, NH1, 2), f32)
    alibi[:, :, 0] = slopes
    alibi[:, :, 1] = -slopes * np.arange(S, dtype=f32)[:, None]
    logits = np.arange(Q_MIN, 1)
    table = np.stack([np.floor(np.exp(logits / float(Q_IN)) * 65536.0), logits]).astype(f32)

    arrays = {
        "x": a["x"],
        "mask_q": a["mask_1xSxS2_ff0"].reshape(S, SK),
        "mask_k": a["mask_BxS2_bf1"].view(np.uint8),
        "ctxT": ctxT.reshape(B, KC, P, SKP).transpose(0, 2, 1, 3).reshape(B, P, KC * SKP),
        "wq0": _grouped(np, a["L0_xattn_Wq"], G0),
        "wkv0": np.concatenate([_grouped(np, a["L0_xattn_Wk"], G0), _grouped(np, a["L0_xattn_Wv"], G0)], axis=3),
        "wo0": a["L0_xattn_Wo"].reshape(G0, HPG0, HD0, H).transpose(0, 2, 1, 3),
        "bias0": np.concatenate([a["L0_xattn_" + n].reshape(G0, -1) for n in ("bq", "bk", "bv")], axis=1),
        "qn": a["L0_xattn_qn_w"].reshape(HD0, 1),
        "kn": a["L0_xattn_kn_w"].reshape(HD0, 1),
        "wa": _sliced(np, a["L0_ffn_A"].reshape(AR, H).T, KC),
        "wb": _sliced(np, a["L0_ffn_B"].transpose(0, 2, 1).reshape(AR, H), AC),
        "ww": _sliced(np, a["L0_ffn_W"].T, KC),
        "bias_f": a["L0_ffn_bias"],
        "alibi": alibi,
        "wq1": _sliced(np, a["L1_xattn_Wq"], KC),
        "wkv1": _sliced(np, np.concatenate([a["L1_xattn_Wk"], a["L1_xattn_Wv"]], axis=1), KC),
        "wo1": wo1.transpose(0, 2, 3, 1, 4).reshape(P, HPG1, H),
        "wg": _sliced(np, a["L1_ffn_w_gate"].T, KC),
        "w13": w13.reshape(NE, 2, KC, P, IT * P).transpose(0, 3, 1, 2, 4),
        "w2": w2T.reshape(NE, IT, P, H).transpose(0, 2, 1, 3),
        "table": table,
    }
    nc = _bacc.Bacc("TRN2", target_bir_lowering=False, num_devices=1)
    feeds, args = {}, {}
    for name, array in arrays.items():
        array = np.ascontiguousarray(array)
        feeds[f"in_{name}"] = array
        args[name] = nc.dram_tensor(f"in_{name}", array.shape, _mybir.dt.from_np(array.dtype), kind="ExternalInput").ap()
    args["out"] = nc.dram_tensor("out_0", (B, S, H), F32, kind="ExternalOutput").ap()
    network(nc, **args)
    return _run(nc, [feeds], core_ids=[0]).results[0]["out_0"]
```

```python
from contextlib import ExitStack

import concourse.bass as bass
from concourse import mybir

ALU = mybir.AluOpType
ACT = mybir.ActivationFunctionType
AX = mybir.AxisListType
F32 = mybir.dt.float32
F32R = mybir.dt.float32r

P = 128
B, S, H = 8, 256, 256
KC = H // P
QT = S // P
SK = 1601
KT = -(-SK // P)
SKP = KT * P
CHUNKS = 4
CW = 402
SKC = CHUNKS * CW
BANK = 512
NEG = -1.0e30
KGROUPS = [range(0, 4), range(4, 7), range(7, 10), range(10, 13)]
HD0, G0, HPG0 = 128, 4, 4
EPS_RMS, EPS_LN = 1e-6, 1e-5


class Ring:

    def __init__(self, steps, kinds, size):
        self.size = size
        lists = ([s for s in steps if s[-1]], steps, [s for s in steps if not s[-1]])
        self.at = [{s: i for i, s in enumerate(s for s in part if s[0] in kinds)} for part in lists]

    def uses(self, part, bank):
        return len(range(bank, len(self.at[part]), self.size))

    def bank(self, part, step):
        return self.at[part][step] % self.size

    def tenants(self, part, b, step):
        i = self.at[part][step]
        bank, n = i % self.size, i // self.size
        return n if part == 0 else self.uses(0, bank) + b * self.uses(1, bank) + n

    def before(self, part, b, step=None):
        n = 0 if step is None else self.at[part][step]
        return n if part == 0 else len(self.at[0]) + b * len(self.at[1]) + n


def stand(eng, passed):
    eng.sem_inc(passed, 1)


def first_plan():
    def kv(g): return [("kv", g, i) for i in range(7)]
    def norms(g): return [("kt", g, j) for j in range(len(KGROUPS))] + [("qt", g, i) for i in range(QT)]
    steps = [("ctx", 0, 0), ("xt", 0, 0), *kv(0), ("vh", 0, 0), ("qp", 0, 0), ("qp", 0, 1),
             ("kstat", 0, 0), ("qstat", 0, 0), *norms(0)]
    tiles = G0 * HPG0 * QT
    per = HPG0 * QT
    for t in range(tiles + 3):
        work = []
        g, at = divmod(t, per)
        if g + 1 < G0:
            work = {0: kv(g + 1)[:4], 2: kv(g + 1)[4:] + [("vh", g + 1, 0), ("qp", g + 1, 0)],
                    3: [("kstat", g + 1, 0)], 4: [("qp", g + 1, 1)], 5: [("qstat", g + 1, 0)],
                    6: norms(g + 1)}.get(at, [])
        work = list(work)
        if t < tiles:
            steps.append(("scores", t, 0))
        turn = [("turn", t - 1, j) for j in range(4)] if 1 <= t <= tiles else []
        exp = [("exp", t, 0)] if t < tiles else []
        if t % 2 == 0:
            steps += turn[:2] + exp
            if t >= 2 and (t - 2) // 2 < tiles // 2:
                steps.append(("rinv", (t - 2) // 2, 0))
            if t >= per + 2 and (t - per - 2) % per == 0:
                steps.append(("wo", (t - per - 2) // per, 0))
            steps += turn[2:3] + work[:1] + turn[3:] + work[1:]
        else:
            pair = (t - 3) // 2
            pv = [("pv", pair, j) for j in range(4)] if t >= 3 else []
            for j in range(4):
                steps += pv[j:j + 1] + turn[j:j + 1]
                if j == 1:
                    steps += exp
            if pv:
                steps.append(("norm", pair, 0))
            steps += work
    return steps


def count(steps, kinds):
    at = {s: n for n, s in enumerate(s for s in steps if s[0] in kinds)}
    return at, len(at)


def first_attention(nc, x, out, ctxT, mask, wq, wkv, wo, bias, qn, kn):
    steps = first_plan()
    bank_at, BANKS = count(steps, ("xt", "kv", "qp", "kt", "qt", "turn"))
    high_at, HIGHS = count(steps, ("kt", "qt", "turn"))
    acc_at, ACCS = count([s for s in steps if s[0] != "pv" or s[2] == 3], ("pv", "wo"))
    TILES, PAIRS = G0 * HPG0 * QT, G0 * HPG0
    assert wq.shape[0] == G0

    with ExitStack() as ctx:
        def sb(name, shape, dt=F32):
            return ctx.enter_context(nc.sbuf_tensor("a0_" + name, shape, dt))

        def sem(name):
            return ctx.enter_context(nc.semaphore("a0_" + name))

        ctx_hi, ctx_lo = (sb(n, [P, KC, SKP], F32R) for n in ("ctx_hi", "ctx_lo"))
        wkv_raw = sb("wkv_raw", [P, KC, 2 * HD0])
        wkv_hi, wkv_lo = (sb(n, [P, KC, 2 * HD0], F32R) for n in ("wkv_hi", "wkv_lo"))
        wq_g = sb("wq_g", [P, KC, HPG0 * HD0])
        wo_g = sb("wo_g", [P, HPG0, H])
        bias_g = sb("bias_g", [P, HPG0 * HD0 + 2 * HD0])
        maskt = sb("mask", [P, QT, SKC])
        k_hi, k_lo = ([sb(f"{n}{i}", [P, SKP], F32R) for i in range(2)] for n in ("k_hi", "k_lo"))
        v_hi, v_lo = ([sb(f"{n}{i}", [P, KT, HD0], F32R) for i in range(2)] for n in ("v_hi", "v_lo"))
        q_hi, q_lo = ([sb(f"{n}{i}", [P, HPG0, S], F32R) for i in range(2)] for n in ("q_hi", "q_lo"))
        prob = [sb(f"prob{i}", [P, SKP]) for i in range(2)]
        pt_hi, pt_lo = (sb(n, [P, KT, S], F32R) for n in ("pt_hi", "pt_lo"))
        kv_raw = sb("kv_raw", [P, KT, 2 * HD0])
        square = sb("square", [P, KT * HD0])
        q_raw = sb("q_raw", [P, QT, HPG0 * HD0])
        heads = sb("heads", [P, HPG0, S])
        x_in = sb("x_in", [P, QT, H])
        x_out = sb("x_out", [P, QT, H])
        xT = sb("xT", [P, KC, S])
        rows = sb("rows", [P, S])
        ident = sb("ident", [P, P])
        qn_s, kn_s = sb("qn_s", [P, 1]), sb("kn_s", [P, 1])
        half = sb("half", [P, 16])
        top = sb("top", [P, 2, 2])
        negmax = sb("negmax", [P, 2])
        total = sb("total", [P, 4])
        inv = sb("inv", [P, 2, 2])
        kvar, krstd = sb("kvar", [P, KT]), sb("krstd", [P, KT])
        qvar, qrstd = sb("qvar", [P, QT * HPG0]), sb("qrstd", [P, QT * HPG0])
        ln6, ln2, lnr = sb("ln6", [P, QT, 6]), sb("ln2", [P, QT, 2]), sb("lnr", [P, QT])

        ps_s = ctx.enter_context(nc.psum_tensor("a0_ps_s", [P, CHUNKS, BANK], F32))
        ps_t = ctx.enter_context(nc.psum_tensor("a0_ps_t", [P, 2, BANK], F32))
        ps_o = ctx.enter_context(nc.psum_tensor("a0_ps_o", [P, 2, BANK], F32))

        const_in, const_set, const_ok, qn_scaled = (sem(n) for n in ("const_in", "const_set", "const_ok", "qn_scaled"))
        ctx_in, x_in_s, wkv_in, wq_in, wo_in = (sem(n) for n in ("ctx_in", "x_in_s", "wkv_in", "wq_in", "wo_in"))
        ctx_high, ctx_split, wkv_high, wkv_split = (sem(n) for n in ("ctx_high", "ctx_split", "wkv_high", "wkv_split"))
        ln_step, ln_var, ln_rstd, x_norm = (sem(n) for n in ("ln_step", "ln_var", "ln_rstd", "x_norm"))
        bank_full, bank_free = sem("bank_full"), sem("bank_free")
        acc_full, acc_free = sem("acc_full"), sem("acc_free")
        scores_full, scored, negmax_ok, exp_ok, high_ok = (
            sem(n) for n in ("scores_full", "scored", "negmax_ok", "exp_ok", "high_ok"))
        turned, pv_done, inv_ok, rows_ok = (sem(n) for n in ("turned", "pv_done", "inv_ok", "rows_ok"))
        k_square, k_sum, k_var, k_rstd, k_norm = (sem(n) for n in ("k_square", "k_sum", "k_var", "k_rstd", "k_norm"))
        q_square, q_sum, q_var, q_rstd, q_norm = (sem(n) for n in ("q_square", "q_sum", "q_var", "q_rstd", "q_norm"))
        dve_passed, pool_passed, sp_passed = (sem(n) for n in ("dve_passed", "pool_passed", "sp_passed"))
        v_high, v_split, x_done, x_stored = (sem(n) for n in ("v_high", "v_split", "x_done", "x_stored"))

        def f(ap):
            return ap.bitcast(F32)

        block = ctx.enter_context(nc.Block())

        @block.sync
        def _(sp):
            with nc.allow_non_contiguous_dma("one number a partition"):
                sp.dma_start(qn_s[:, :], qn).then_inc(const_in, 16)
                sp.dma_start(kn_s[:, :], kn).then_inc(const_in, 16)
            sp.wait_ge(const_set, 1)
            sp.dma_start(maskt[:, :, 0:SK], mask.rearrange("(t p) k -> p t k", p=P)).then_inc(const_in, 16)

            with sp.Fori(0, B) as b:
                sp.wait_ge(acc_free, b * ACCS + 1)
                sp.dma_start(x_in[:, :, :], x[b].rearrange("(t p) h -> p t h", p=P)).then_inc(x_in_s, 16)
                sp.wait_ge(k_norm, b * G0)
                stand(sp, sp_passed)
                sp.wait_ge(v_split, b * G0)
                stand(sp, sp_passed)
                sp.wait_ge(bank_full, b * BANKS)
                sp.dma_start(kv_raw[:, :, :].rearrange("p k d -> p (k d)"), ctxT[b]).then_inc(ctx_in, 16)
                for g in range(G0):
                    sp.wait_ge(wkv_split, b * G0 + g)
                    sp.dma_start(wkv_raw[:, :, :], wkv[g]).then_inc(wkv_in, 16)
                    if g == 0:
                        sp.wait_ge(bank_free, b * BANKS + 1)
                    else:
                        sp.wait_ge(bank_free, b * BANKS + bank_at["qp", g - 1, 1] + 2)
                    sp.dma_start(wq_g[:, :, :], wq[g]).then_inc(wq_in, 16)
                    sp.dma_start(bias_g[:, :], bias[g].partition_broadcast(P)).then_inc(wq_in, 16)
                    if g:
                        n = g - 1
                        if n == 0:
                            sp.wait_ge(acc_free, b * ACCS + 1)
                        else:
                            sp.wait_ge(acc_free, b * ACCS + acc_at["wo", n - 1, 0] + 2)
                        sp.dma_start(wo_g[:, :, :], wo[n]).then_inc(wo_in, 16)
                sp.wait_ge(acc_free, b * ACCS + acc_at["wo", G0 - 2, 0] + 2)
                sp.dma_start(wo_g[:, :, :], wo[G0 - 1]).then_inc(wo_in, 16)

        @block.gpsimd
        def _(pool):
            nc.gpsimd.memset(maskt[:, :, :], NEG).then_inc(const_set, 1)
            nc.gpsimd.memset(half[:, :], -0.5).then_inc(const_ok, 1)
            nc.gpsimd.memset(prob[0][:, SKC:], 0.0).then_inc(const_ok, 1)
            nc.gpsimd.memset(prob[1][:, SKC:], 0.0).then_inc(const_ok, 1)
            nc.gpsimd.memset(ident[:, :], 0.0).then_inc(const_set, 1)
            pool.wait_ge(const_set, 2)
            nc.gpsimd.affine_select(out=ident[:, :], in_=ident[:, :], compare_op=ALU.not_equal, fill=1.0, base=0,
                                    pattern=[[-1, P]], channel_multiplier=1).then_inc(const_ok, 1)
            pool.wait_ge(const_ok, 4)

            with pool.Fori(0, B) as b:
                for g in range(G0):
                    pool.wait_ge(wkv_in, (b * G0 + g) * 16 + 16)
                    if g:
                        pool.wait_ge(bank_full, b * BANKS + bank_at["kv", g - 1, 6] + 1)
                    else:
                        pool.wait_ge(bank_full, b * BANKS)
                    stand(pool, pool_passed)
                    nc.gpsimd.tensor_scalar(wkv_hi[:, :, :], wkv_raw[:, :, :], 1.0, None, ALU.mult).then_inc(wkv_high, 1)
                    pool.wait_ge(wkv_high, b * G0 + g + 1)
                    nc.gpsimd.tensor_tensor(wkv_lo[:, :, :], wkv_raw[:, :, :], f(wkv_hi[:, :, :]),
                                            ALU.subtract).then_inc(wkv_split, 1)
                    if g == 0:
                        pool.wait_ge(ln_var, b * QT + QT)
                        nc.gpsimd.tensor_tensor(lnr[:, :], ln2[:, :, 1], half[:, 0:QT], ALU.pow).then_inc(ln_rstd, 1)
                    pool.wait_ge(bank_free, b * BANKS + bank_at["kv", g, 6] + 2)
                    if g:
                        pool.wait_ge(q_sum, b * G0 + g)
                    else:
                        pool.wait_ge(q_sum, b * G0)
                    k3 = kv_raw[:, :, 0:HD0]
                    nc.gpsimd.tensor_tensor(square[:, :].rearrange("p (k d) -> p k d", d=HD0), k3, k3,
                                            ALU.mult).then_inc(k_square, 1)
                    pool.wait_ge(v_high, b * G0 + g + 1)
                    nc.gpsimd.tensor_tensor(v_lo[g % 2][:, :, :], kv_raw[:, :, HD0:], f(v_hi[g % 2][:, :, :]),
                                            ALU.subtract).then_inc(v_split, 1)
                    pool.wait_ge(k_var, b * G0 + g + 1)
                    nc.gpsimd.tensor_tensor(krstd[:, :], kvar[:, :], half[:, 0:KT], ALU.pow).then_inc(k_rstd, 1)
                    pool.wait_ge(k_rstd, b * G0 + g + 1)
                    nc.gpsimd.tensor_tensor(k3, k3, krstd[:, :].unsqueeze(2).to_broadcast([P, KT, HD0]),
                                            ALU.mult).then_inc(k_norm, 1)
                    pool.wait_ge(bank_free, b * BANKS + bank_at["qp", g, 1] + 2)
                    pool.wait_ge(k_sum, b * G0 + g + 1)
                    q3 = q_raw[:, :, :].rearrange("p t (h d) -> p (t h) d", d=HD0)
                    nc.gpsimd.tensor_tensor(square[:, 0:QT * HPG0 * HD0].rearrange("p (k d) -> p k d", d=HD0), q3, q3,
                                            ALU.mult).then_inc(q_square, 1)
                    pool.wait_ge(q_var, b * G0 + g + 1)
                    nc.gpsimd.tensor_tensor(qrstd[:, :], qvar[:, :], half[:, 0:QT * HPG0], ALU.pow).then_inc(q_rstd, 1)
                    pool.wait_ge(q_rstd, b * G0 + g + 1)
                    nc.gpsimd.tensor_tensor(q3, q3, qrstd[:, :].unsqueeze(2).to_broadcast([P, QT * HPG0, HD0]),
                                            ALU.mult).then_inc(q_norm, 1)

        @block.tensor
        def _(pe):
            pe.wait_ge(const_ok, 4)

            with pe.Fori(0, B) as b:
                def bank(step):
                    n = bank_at[step]
                    pe.wait_ge(bank_free, b * BANKS + n)
                    return ps_t[:, n % 2, :]

                def split_mm(to, lhs, rhs, first=True, last=True):
                    (lh, ll), (rh, rl) = lhs, rhs
                    nc.tensor.matmul(to, lh, rh, start=first, stop=False)
                    nc.tensor.matmul(to, ll, rh, start=False, stop=False)
                    return nc.tensor.matmul(to, lh, rl, start=False, stop=last)

                for kind, n, j in steps:
                    if kind == "xt":
                        ps = bank((kind, n, j)).rearrange("p (c s) -> p c s", c=KC)
                        pe.wait_ge(x_norm, b * QT + QT)
                        for c in range(KC):
                            for q in range(QT):
                                mm = nc.tensor.transpose(ps[:, c, q * P:(q + 1) * P],
                                                         q_raw[:, q, c * P:(c + 1) * P], ident[:, :])
                        mm.then_inc(bank_full, 1)
                    elif kind == "kv":
                        ps = bank((kind, n, j)).rearrange("p (k d) -> p k d", k=2)
                        if j == 0:
                            pe.wait_ge(wkv_split, b * G0 + n + 1)
                            if n == 0:
                                pe.wait_ge(ctx_split, b * KC + KC)
                        for i in range(min(2, KT - 2 * j)):
                            k = slice((2 * j + i) * P, (2 * j + i + 1) * P)
                            for c in range(KC):
                                mm = split_mm(ps[:, i, :], (ctx_hi[:, c, k], ctx_lo[:, c, k]),
                                              (wkv_hi[:, c, :], wkv_lo[:, c, :]), c == 0, c == KC - 1)
                        mm.then_inc(bank_full, 1)
                    elif kind == "qp":
                        ps = bank((kind, n, j))
                        pe.wait_ge(wq_in, (b * G0 + n) * 32 + 32)
                        for c in range(KC):
                            mm = nc.tensor.matmul(ps, xT[:, c, j * P:(j + 1) * P], wq_g[:, c, :],
                                                  start=c == 0, stop=c == KC - 1)
                        mm.then_inc(bank_full, 1)
                    elif kind == "kt":
                        ps = bank((kind, n, j))
                        pe.wait_ge(k_norm, b * G0 + n + 1)
                        for i, k in enumerate(KGROUPS[j]):
                            mm = nc.tensor.transpose(ps[:, i * P:(i + 1) * P], kv_raw[:, k, 0:HD0], ident[:, :])
                        mm.then_inc(bank_full, 1)
                    elif kind == "qt":
                        ps = bank((kind, n, j))
                        pe.wait_ge(q_norm, b * G0 + n + 1)
                        for i in range(HPG0):
                            mm = nc.tensor.transpose(ps[:, i * P:(i + 1) * P], q_raw[:, j, i * HD0:(i + 1) * HD0],
                                                     ident[:, :])
                        mm.then_inc(bank_full, 1)
                    elif kind == "scores":
                        g, at = divmod(n, HPG0 * QT)
                        head, q = divmod(at, QT)
                        if at == 0:
                            pe.wait_ge(bank_free, b * BANKS + bank_at["qt", g, 1] + 2)
                        q = slice(q * P, (q + 1) * P)
                        for c in range(CHUNKS):
                            if c % 2 == 0:
                                pe.wait_ge(scored, (b * TILES + n) * 2 + c // 2)
                            k = slice(c * CW, (c + 1) * CW)
                            mm = split_mm(ps_s[:, c, 0:CW], (q_hi[g % 2][:, head, q], q_lo[g % 2][:, head, q]),
                                          (k_hi[g % 2][:, k], k_lo[g % 2][:, k]))
                            if c % 2:
                                mm.then_inc(scores_full, 1)
                    elif kind == "turn":
                        ps = bank((kind, n, j))
                        pe.wait_ge(exp_ok, b * TILES + n + 1)
                        for i, k in enumerate(KGROUPS[j]):
                            mm = nc.tensor.transpose(ps[:, i * P:(i + 1) * P], prob[n % 2][:, k * P:(k + 1) * P],
                                                     ident[:, :])
                        mm.then_inc(bank_full, 1)
                    elif kind == "pv":
                        g = n // HPG0
                        acc = acc_at["pv", n, 3]
                        ps = ps_o[:, acc % 2, :]
                        if j == 0:
                            pe.wait_ge(acc_free, b * ACCS + acc)
                            pe.wait_ge(inv_ok, b * PAIRS + n + 1)
                            for q in range(QT):
                                nc.tensor.matmul(ps[:, S + q * P:S + (q + 1) * P],
                                                 inv[:, n % 2, q:q + 1].to_broadcast([P, P]), ident[:, :],
                                                 start=True, stop=True)
                        if j == 0 and n % HPG0 == 0:
                            pe.wait_ge(v_split, b * G0 + g + 1)
                        pe.wait_ge(bank_free, b * BANKS + bank_at["turn", 2 * n + 1, j] + 2)
                        for k in KGROUPS[j]:
                            mm = split_mm(ps[:, 0:S], (v_hi[g % 2][:, k, :], v_lo[g % 2][:, k, :]),
                                          (pt_hi[:, k, :], pt_lo[:, k, :]), k == 0, k == KT - 1)
                        mm.then_inc(pv_done, 1)
                    elif kind == "wo":
                        acc = acc_at[kind, n, j]
                        pe.wait_ge(acc_free, b * ACCS + acc + 1)
                        pe.wait_ge(wo_in, (b * G0 + n) * 16 + 16)
                        for q in range(QT):
                            for i in range(HPG0):
                                mm = nc.tensor.matmul(ps_o[:, acc % 2, q * H:(q + 1) * H], heads[:, i, q * P:(q + 1) * P],
                                                      wo_g[:, i, :], start=i == 0, stop=i == HPG0 - 1)
                        mm.then_inc(acc_full, 1)

        @block.scalar
        def _(act):
            with act.Fori(0, B) as b:
                for kind, n, j in steps:
                    if kind == "ctx":
                        act.wait_ge(ctx_in, b * 16 + 16)
                        act.wait_ge(bank_full, b * BANKS)
                        for c in range(KC):
                            nc.scalar.copy(ctx_hi[:, c, :], kv_raw[:, :, :].rearrange("p k d -> p (k d)")[
                                :, c * SKP:(c + 1) * SKP]).then_inc(ctx_high, 1)
                    elif kind == "vh":
                        act.wait_ge(bank_free, b * BANKS + bank_at["kv", n, 6] + 2)
                        if n >= 2:
                            act.wait_ge(pv_done, b * PAIRS * 4 + (n - 1) * HPG0 * 4)
                        else:
                            act.wait_ge(pv_done, b * PAIRS * 4)
                        nc.scalar.copy(v_hi[n % 2][:, :, :], kv_raw[:, :, HD0:]).then_inc(v_high, 1)
                    elif kind in ("kt", "qt", "turn"):
                        at = bank_at[kind, n, j]
                        act.wait_ge(bank_full, b * BANKS + at + 1)
                        ps = ps_t[:, at % 2, :]
                        w = len(KGROUPS[j])
                        k0 = KGROUPS[j][0]
                        if kind == "kt":
                            act.wait_ge(const_in, 48)
                            act.wait_ge(scored, b * TILES * 2 + 1)
                            nc.scalar.activation(k_hi[n % 2][:, k0 * P:(k0 + w) * P], ps[:, 0:w * P], ACT.Identity,
                                                 bias=0.0, scale=kn_s[:, :]).then_inc(high_ok, 1)
                        elif kind == "qt":
                            act.wait_ge(qn_scaled, 1)
                            nc.scalar.activation(q_hi[n % 2][:, :, j * P:(j + 1) * P],
                                                 ps.rearrange("p (h s) -> p h s", h=HPG0), ACT.Identity, bias=0.0,
                                                 scale=qn_s[:, :]).then_inc(high_ok, 1)
                        else:
                            pair, q = divmod(n, QT)
                            if q == 0:
                                act.wait_ge(pv_done, (b * PAIRS + pair) * 4 - 4 + j + 1 if pair else b * PAIRS * 4)
                            nc.scalar.copy(pt_hi[:, k0:k0 + w, q * P:(q + 1) * P],
                                           ps[:, 0:w * P].rearrange("p (k s) -> p k s", k=w)).then_inc(high_ok, 1)
                    elif kind == "exp":
                        act.wait_ge(negmax_ok, b * TILES + n + 1)
                        nc.scalar.activation(prob[n % 2][:, 0:SKC], prob[n % 2][:, 0:SKC], ACT.Exp,
                                             bias=negmax[:, n % 2:n % 2 + 1], scale=1.0,
                                             accum_out=total[:, n % 4:n % 4 + 1]).then_inc(exp_ok, 1)
                    elif kind == "norm":
                        acc = acc_at["pv", n, 3]
                        act.wait_ge(pv_done, (b * PAIRS + n) * 4 + 4)
                        act.wait_ge(acc_free, b * ACCS + acc)
                        nc.scalar.copy(rows[:, :], ps_o[:, acc % 2, S:2 * S]).then_inc(rows_ok, 1)
                act.wait_ge(x_done, b + 1)
                act.dma_start(out[b].rearrange("(t p) h -> p t h", p=P), x_out[:, :, :]).then_inc(x_stored, 16)
            act.wait_ge(x_stored, 16 * B)

        @block.vector
        def _(dve):
            nc.vector.memset(top[:, 0, :], 0.0).then_inc(bank_free, 1)
            nc.vector.memset(top[:, 1, :], 0.0).then_inc(acc_free, 1)
            nc.vector.memset(negmax[:, :], 0.0).then_inc(scored, 1)
            dve.wait_ge(const_in, 48)
            nc.vector.tensor_scalar(qn_s[:, :], qn_s[:, :], float(HD0) ** -0.5, None, ALU.mult).then_inc(qn_scaled, 1)
            dve.wait_ge(qn_scaled, 1)

            with dve.Fori(0, B) as b:
                def evac(step):
                    at = bank_at[step]
                    dve.wait_ge(bank_full, b * BANKS + at + 1)
                    return ps_t[:, at % 2, :]

                for kind, n, j in steps:
                    if kind == "ctx":
                        dve.wait_ge(x_in_s, b * 16 + 16)
                        for q in range(QT):
                            nc.vector.bn_stats(ln6[:, q, :], x_in[:, q, :]).then_inc(ln_step, 1)
                            dve.wait_ge(ln_step, (b * QT + q) * 2 + 1)
                            stand(dve, dve_passed)
                            nc.vector.bn_aggr(ln2[:, q, :], ln6[:, q, :]).then_inc(ln_step, 1)
                            dve.wait_ge(ln_step, (b * QT + q) * 2 + 2)
                            nc.vector.tensor_scalar(ln2[:, q, 1:2], ln2[:, q, 1:2], EPS_LN, None,
                                                    ALU.add).then_inc(ln_var, 1)
                        for c in range(KC):
                            dve.wait_ge(ctx_high, b * KC + c + 1)
                            nc.vector.tensor_tensor(ctx_lo[:, c, :], kv_raw[:, :, :].rearrange("p k d -> p (k d)")[
                                :, c * SKP:(c + 1) * SKP], f(ctx_hi[:, c, :]), ALU.subtract).then_inc(ctx_split, 1)
                        dve.wait_ge(ln_rstd, b + 1)
                        for q in range(QT):
                            nc.vector.tensor_scalar(q_raw[:, q, 0:H], x_in[:, q, :], ln2[:, q, 0:1], lnr[:, q:q + 1],
                                                    ALU.subtract, ALU.mult).then_inc(x_norm, 1)
                    elif kind == "xt":
                        ps = evac((kind, n, j))
                        nc.vector.tensor_copy(xT[:, :, :], ps.rearrange("p (c s) -> p c s", c=KC)).then_inc(bank_free, 1)
                    elif kind == "kv":
                        ps = evac((kind, n, j))
                        if j == 0:
                            dve.wait_ge(wq_in, (b * G0 + n) * 32 + 32)
                            dve.wait_ge(v_split, b * G0 + n)
                            if n == 0:
                                dve.wait_ge(ctx_split, b * KC + KC)
                        w = min(2, KT - 2 * j)
                        nc.vector.tensor_tensor(kv_raw[:, 2 * j:2 * j + w, :],
                                                ps[:, 0:w * 2 * HD0].rearrange("p (k d) -> p k d", k=w),
                                                bias_g[:, HPG0 * HD0:].unsqueeze(1).to_broadcast([P, w, 2 * HD0]),
                                                ALU.add).then_inc(bank_free, 1)
                    elif kind == "qp":
                        ps = evac((kind, n, j))
                        nc.vector.tensor_tensor(q_raw[:, j, :], ps, bias_g[:, 0:HPG0 * HD0],
                                                ALU.add).then_inc(bank_free, 1)
                    elif kind == "kstat":
                        dve.wait_ge(k_square, b * G0 + n + 1)
                        nc.vector.tensor_reduce(kvar[:, :], square[:, :].rearrange("p (k d) -> p k d", d=HD0), AX.X,
                                                ALU.add).then_inc(k_sum, 1)
                        dve.wait_ge(k_sum, b * G0 + n + 1)
                        nc.vector.tensor_scalar(kvar[:, :], kvar[:, :], 1.0 / HD0, EPS_RMS, ALU.mult,
                                                ALU.add).then_inc(k_var, 1)
                    elif kind == "qstat":
                        dve.wait_ge(q_square, b * G0 + n + 1)
                        nc.vector.tensor_reduce(qvar[:, :], square[:, 0:QT * HPG0 * HD0].rearrange(
                            "p (k d) -> p k d", d=HD0), AX.X, ALU.add).then_inc(q_sum, 1)
                        dve.wait_ge(q_sum, b * G0 + n + 1)
                        nc.vector.tensor_scalar(qvar[:, :], qvar[:, :], 1.0 / HD0, EPS_RMS, ALU.mult,
                                                ALU.add).then_inc(q_var, 1)
                    elif kind in ("kt", "qt", "turn"):
                        ps = ps_t[:, bank_at[kind, n, j] % 2, :]
                        dve.wait_ge(high_ok, b * HIGHS + high_at[kind, n, j] + 1)
                        w, k0 = len(KGROUPS[j]), KGROUPS[j][0]
                        if kind == "kt":
                            k = slice(k0 * P, (k0 + w) * P)
                            nc.vector.scalar_tensor_tensor(k_lo[n % 2][:, k], ps[:, 0:w * P], kn_s[:, :],
                                                           f(k_hi[n % 2][:, k]), ALU.mult,
                                                           ALU.subtract).then_inc(bank_free, 1)
                        elif kind == "qt":
                            q = slice(j * P, (j + 1) * P)
                            nc.vector.scalar_tensor_tensor(q_lo[n % 2][:, :, q], ps.rearrange("p (h s) -> p h s", h=HPG0),
                                                           qn_s[:, :], f(q_hi[n % 2][:, :, q]), ALU.mult,
                                                           ALU.subtract).then_inc(bank_free, 1)
                        else:
                            q = slice(n % QT * P, (n % QT + 1) * P)
                            nc.vector.tensor_tensor(pt_lo[:, k0:k0 + w, q],
                                                    ps[:, 0:w * P].rearrange("p (k s) -> p k s", k=w),
                                                    f(pt_hi[:, k0:k0 + w, q]), ALU.subtract).then_inc(bank_free, 1)
                    elif kind == "scores":
                        if n >= 2:
                            dve.wait_ge(bank_full, b * BANKS + bank_at["turn", n - 2, 3] + 1)
                        for c in range(2):
                            dve.wait_ge(scores_full, (b * TILES + n) * 2 + c + 1)
                            stand(dve, dve_passed)
                            k = slice(2 * c * CW, (2 * c + 2) * CW)
                            nc.vector.tensor_tensor_reduce(
                                prob[n % 2][:, k].rearrange("p (c k) -> p c k", c=2), ps_s[:, 2 * c:2 * c + 2, 0:CW],
                                maskt[:, n % QT, k].rearrange("p (c k) -> p c k", c=2), 1.0, -3.4e38, ALU.add,
                                ALU.max, top[:, n % 2, c:c + 1]).then_inc(scored, 1)
                        dve.wait_ge(scored, (b * TILES + n) * 2 + 3)
                        nc.vector.tensor_reduce(negmax[:, n % 2:n % 2 + 1], top[:, n % 2, :], AX.X, ALU.max,
                                                negate=True).then_inc(negmax_ok, 1)
                    elif kind == "rinv":
                        dve.wait_ge(exp_ok, b * TILES + 2 * n + 2)
                        if n >= 2:
                            dve.wait_ge(pv_done, (b * PAIRS + n) * 4 - 4)
                        nc.vector.reciprocal(inv[:, n % 2, :], total[:, 2 * n % 4:2 * n % 4 + 2]).then_inc(inv_ok, 1)
                    elif kind == "norm":
                        acc = acc_at["pv", n, 3]
                        dve.wait_ge(rows_ok, b * PAIRS + n + 1)
                        nc.vector.tensor_tensor(heads[:, n % HPG0, :], ps_o[:, acc % 2, 0:S], rows[:, :],
                                                ALU.mult).then_inc(acc_free, 1)
                    elif kind == "wo":
                        acc = acc_at[kind, n, j]
                        dve.wait_ge(acc_full, b * G0 + n + 1)
                        if n == 0:
                            dve.wait_ge(x_stored, b * 16)
                        else:
                            dve.wait_ge(x_done, b)
                        y = ps_o[:, acc % 2, :].rearrange("p (t h) -> p t h", t=QT)
                        mm = nc.vector.tensor_tensor(x_out[:, :, :], y, (x_out if n else x_in)[:, :, :], ALU.add)
                        mm.then_inc(acc_free, 1)
                        if n == G0 - 1:
                            dve.wait_ge(acc_free, b * ACCS + ACCS + 1)
                            nc.vector.memset(top[:, :, :], 0.0).then_inc(x_done, 1)
                        else:
                            dve.wait_ge(acc_free, b * ACCS + acc + 2)


NA, R, TOPK = 64, 16, 4
AR = NA * R
AC = AR // P


def first_ffn(nc, x, out, wa, wb, ww, bias):
    TILES = B * S // P
    PER = 4
    ORDER = [("a", 0), ("a", 1), ("b", 0), ("a", 2), ("b", 1), ("a", 3), ("b", 2), ("b", 3)]

    with ExitStack() as ctx:
        def sb(name, shape, dt=F32):
            return ctx.enter_context(nc.sbuf_tensor("f0_" + name, shape, dt))

        def sem(name):
            return ctx.enter_context(nc.semaphore("f0_" + name))

        wa_raw, wb_raw, ww_raw = sb("wa_raw", [P, KC, AR]), sb("wb_raw", [P, AC, H]), sb("ww_raw", [P, KC, H])
        wa_hi, wa_lo = (sb(n, [P, KC, AR], F32R) for n in ("wa_hi", "wa_lo"))
        wb_hi, wb_lo = (sb(n, [P, AC, H], F32R) for n in ("wb_hi", "wb_lo"))
        ww_hi, ww_lo = (sb(n, [P, KC, H], F32R) for n in ("ww_hi", "ww_lo"))
        bias_s = sb("bias", [P, H])
        ident, half = sb("ident", [P, P]), sb("half", [P, 1])
        ones = sb("ones", [P, NA])
        xs = sb("xs", [P, PER, H])
        xn = sb("xn", [P, 2, H])
        xT_hi, xT_lo = (sb(n, [P, 2, KC, P], F32R) for n in ("xT_hi", "xT_lo"))
        sq = sb("sq", [P, 2, AR])
        norms = sb("norms", [P, NA])
        m8 = sb("m8", [P, 8])
        above, equal, rank, keep = (sb(n, [P, NA]) for n in ("above", "equal", "rank", "keep"))
        nabove = sb("nabove", [P, 1])
        picked = sb("picked", [P, 2, NA])
        masked = sb("masked", [P, 2, AR])
        v = sb("v", [P, 2, R])
        z = sb("z", [P, 2, AR])
        zT_hi, zT_lo = (sb(n, [P, AC, P], F32R) for n in ("zT_hi", "zT_lo"))
        y = sb("y", [P, PER, H])
        ln6, ln2, rstd = sb("ln6", [P, 6]), sb("ln2", [P, 2, 2]), sb("rstd", [P, 2])

        ps_v = ctx.enter_context(nc.psum_tensor("f0_ps_v", [P, 2, 2 * BANK], F32))
        ps_z = ctx.enter_context(nc.psum_tensor("f0_ps_z", [P, 2, BANK], F32))
        ps_x = ctx.enter_context(nc.psum_tensor("f0_ps_x", [P, BANK], F32))
        ps_y = ctx.enter_context(nc.psum_tensor("f0_ps_y", [P, BANK], F32))

        (w_in, const_set, const_ok, w_high, w_split, chain, var_ok, rstd_ok, x_norm, xt_full, xt_high, xt_low,
         v_full, squared, v_used, picked_ok, z_ok, zt_full, zt_high, zt_low, y_full, y_read, y_ok, stored) = (
            sem(n) for n in ("w_in", "const_set", "const_ok", "w_high", "w_split", "chain", "var_ok", "rstd_ok",
                             "x_norm", "xt_full", "xt_high", "xt_low", "v_full", "squared", "v_used", "picked_ok",
                             "z_ok", "zt_full", "zt_high", "zt_low", "y_full", "y_read", "y_ok", "stored"))

        dve_passed = sem("dve_passed")
        x_in = [sem(f"x_in{n}") for n in range(PER)]

        def f(ap):
            return ap.bitcast(F32)

        block = ctx.enter_context(nc.Block())

        @block.sync
        def _(sp):
            sp.dma_start(wa_raw[:, :, :], wa).then_inc(w_in, 16)
            sp.dma_start(wb_raw[:, :, :], wb).then_inc(w_in, 16)
            sp.dma_start(ww_raw[:, :, :], ww).then_inc(w_in, 16)
            sp.dma_start(bias_s[:, :], bias.partition_broadcast(P)).then_inc(w_in, 16)
            with sp.Fori(0, TILES // PER) as i:
                for n in range(PER):
                    sp.wait_ge(y_ok, i * PER + n + 1)
                    sp.dma_start(xs[:, n, :], x[i * PER + n]).then_inc(x_in[n], 16)

        @block.gpsimd
        def _(pool):
            nc.gpsimd.memset(half[:, :], -0.5).then_inc(const_ok, 1)
            nc.gpsimd.memset(ones[:, :], 1.0).then_inc(const_ok, 1)
            nc.gpsimd.memset(ident[:, :], 0.0).then_inc(const_set, 1)
            pool.wait_ge(const_set, 1)
            nc.gpsimd.affine_select(out=ident[:, :], in_=ident[:, :], compare_op=ALU.not_equal, fill=1.0, base=0,
                                    pattern=[[-1, P]], channel_multiplier=1).then_inc(const_ok, 1)
            pool.wait_ge(const_ok, 3)
            with pool.Fori(0, TILES // PER) as i:
                for kind, n in ORDER:
                    if kind == "a":
                        pool.wait_ge(var_ok, i * PER + n + 1)
                        nc.gpsimd.tensor_tensor(rstd[:, n % 2:n % 2 + 1], ln2[:, n % 2, 1:2], half[:, :],
                                                ALU.pow).then_inc(rstd_ok, 1)

        @block.tensor
        def _(pe):
            pe.wait_ge(const_ok, 3)
            pe.wait_ge(w_split, 3)

            with pe.Fori(0, TILES // PER) as i:
                for kind, n in ORDER:
                    p, t = n % 2, i * PER + n
                    if kind == "a":
                        pe.wait_ge(x_norm, t + 1)
                        pe.wait_ge(xt_low, t)
                        for c in range(KC):
                            mm = nc.tensor.transpose(ps_x[:, c * P:(c + 1) * P], xn[:, p, c * P:(c + 1) * P], ident[:, :])
                        mm.then_inc(xt_full, 1)
                        pe.wait_ge(xt_low, t + 1)
                        if n >= 2:
                            pe.wait_ge(v_used, t - 1)
                        else:
                            pe.wait_ge(v_used, i * PER)
                        for q in range(2):
                            for c in range(KC):
                                for k, (l, r) in enumerate(((xT_hi, wa_hi), (xT_lo, wa_hi), (xT_hi, wa_lo))):
                                    mm = nc.tensor.matmul(ps_v[:, p, q * BANK:(q + 1) * BANK], l[:, p, c, :],
                                                          r[:, c, q * BANK:(q + 1) * BANK],
                                                          start=c == 0 and k == 0, stop=c == KC - 1 and k == 2)
                        mm.then_inc(v_full, 1)
                    else:
                        pe.wait_ge(z_ok, t + 1)
                        for q in range(2):
                            pe.wait_ge(zt_low, t * 2 + q)
                            for k in range(4):
                                mm = nc.tensor.transpose(ps_z[:, q, k * P:(k + 1) * P],
                                                         z[:, p, (4 * q + k) * P:(4 * q + k + 1) * P], ident[:, :])
                            mm.then_inc(zt_full, 1)
                        pe.wait_ge(y_read, t)
                        for c in range(KC):
                            for k, (l, r) in enumerate(((xT_hi, ww_hi), (xT_lo, ww_hi), (xT_hi, ww_lo))):
                                nc.tensor.matmul(ps_y[:, 0:H], l[:, p, c, :], r[:, c, :],
                                                 start=c == 0 and k == 0, stop=False)
                        for a in range(AC):
                            if a % 4 == 0:
                                pe.wait_ge(zt_low, t * 2 + a // 4 + 1)
                            for k, (l, r) in enumerate(((zT_hi, wb_hi), (zT_lo, wb_hi), (zT_hi, wb_lo))):
                                mm = nc.tensor.matmul(ps_y[:, 0:H], l[:, a, :], r[:, a, :], start=False,
                                                      stop=a == AC - 1 and k == 2)
                        mm.then_inc(y_full, 1)

        @block.scalar
        def _(act):
            act.wait_ge(w_in, 64)
            for hi, raw in ((wa_hi, wa_raw), (wb_hi, wb_raw), (ww_hi, ww_raw)):
                nc.scalar.copy(hi[:, :, :], raw[:, :, :]).then_inc(w_high, 1)
            with act.Fori(0, TILES // PER) as i:
                for kind, n in ORDER:
                    p, t = n % 2, i * PER + n
                    if kind == "a":
                        act.wait_ge(xt_full, t + 1)
                        if n >= 2:
                            act.wait_ge(y_full, t - 1)
                        else:
                            act.wait_ge(y_full, i * PER)
                        nc.scalar.copy(xT_hi[:, p, :, :], ps_x[:, 0:H].rearrange("p (c s) -> p c s", c=KC)).then_inc(
                            xt_high, 1)
                        act.wait_ge(v_full, t + 1)
                        nc.scalar.square(sq[:, p, :], ps_v[:, p, :]).then_inc(squared, 1)
                    else:
                        act.wait_ge(y_full, t)
                        for q in range(2):
                            act.wait_ge(zt_full, t * 2 + q + 1)
                            nc.scalar.copy(zT_hi[:, 4 * q:4 * q + 4, :], ps_z[:, q, :].rearrange(
                                "p (a s) -> p a s", a=4)).then_inc(zt_high, 1)
                for n in range(PER):
                    act.wait_ge(y_ok, i * PER + n + 1 + PER)
                    act.dma_start(out[i * PER + n], y[:, n, :]).then_inc(stored, 16)
            act.wait_ge(stored, 16 * TILES)

        @block.vector
        def _(dve):
            nc.vector.memset(m8[:, :], 0.0).then_inc(y_ok, PER)
            for n, (lo, hi, raw) in enumerate(((wa_lo, wa_hi, wa_raw), (wb_lo, wb_hi, wb_raw), (ww_lo, ww_hi, ww_raw))):
                dve.wait_ge(w_high, n + 1)
                nc.vector.tensor_tensor(lo[:, :, :], raw[:, :, :], f(hi[:, :, :]), ALU.subtract).then_inc(w_split, 1)
            dve.wait_ge(w_in, 64)
            dve.wait_ge(const_ok, 3)

            PER_LINKS = PER * 11

            with dve.Fori(0, TILES // PER) as i:
                done = [0]

                def link(ins):
                    done[0] += 1
                    ins.then_inc(chain, 1)
                    dve.wait_ge(chain, i * PER_LINKS + done[0])

                for kind, n in ORDER:
                    p, t = n % 2, i * PER + n
                    if kind == "a":
                        dve.wait_ge(x_in[n], i * 16 + 16)
                        link(nc.vector.bn_stats(ln6[:, :], xs[:, n, :]))
                        stand(dve, dve_passed)
                        link(nc.vector.bn_aggr(ln2[:, p, :], ln6[:, :]))
                        nc.vector.tensor_scalar(ln2[:, p, 1:2], ln2[:, p, 1:2], EPS_LN, None, ALU.add).then_inc(var_ok, 1)
                        dve.wait_ge(rstd_ok, t + 1)
                        if n >= 2:
                            dve.wait_ge(xt_full, t - 1)
                        else:
                            dve.wait_ge(xt_full, i * PER)
                        nc.vector.tensor_scalar(xn[:, p, :], xs[:, n, :], ln2[:, p, 0:1], rstd[:, p:p + 1],
                                                ALU.subtract, ALU.mult).then_inc(x_norm, 1)
                        dve.wait_ge(xt_high, t + 1)
                        nc.vector.tensor_tensor(xT_lo[:, p, :, :], ps_x[:, 0:H].rearrange("p (c s) -> p c s", c=KC),
                                                f(xT_hi[:, p, :, :]), ALU.subtract).then_inc(xt_low, 1)
                        dve.wait_ge(squared, t + 1)
                        link(nc.vector.tensor_reduce(norms[:, :], sq[:, p, :].rearrange("p (a r) -> p a r", r=R), AX.X,
                                                     ALU.add))
                        stand(dve, dve_passed)
                        link(nc.vector.max(m8[:, :], norms[:, :]))
                        last = m8[:, TOPK - 1:TOPK]
                        link(nc.vector.tensor_scalar(above[:, :], norms[:, :], last, None, ALU.is_gt))
                        link(nc.vector.tensor_reduce(nabove[:, :], above[:, :], AX.X, ALU.add))
                        link(nc.vector.tensor_scalar(equal[:, :], norms[:, :], last, None, ALU.is_equal))
                        link(nc.vector.tensor_tensor_scan(rank[:, :], ones[:, :], equal[:, :], nabove[:, 0:1],
                                                          ALU.mult, ALU.add))
                        link(nc.vector.tensor_scalar(keep[:, :], rank[:, :], float(TOPK), None, ALU.is_le))
                        link(nc.vector.tensor_tensor(keep[:, :], keep[:, :], equal[:, :], ALU.mult))
                        link(nc.vector.tensor_tensor(picked[:, p, :], above[:, :], keep[:, :], ALU.add))
                        nc.vector.tensor_tensor(masked[:, p, :].rearrange("p (a r) -> p a r", r=R),
                                                ps_v[:, p, :].rearrange("p (a r) -> p a r", r=R),
                                                picked[:, p, :].unsqueeze(2).to_broadcast([P, NA, R]),
                                                ALU.mult).then_inc(v_used, 1)
                        dve.wait_ge(v_used, t + 1)
                        nc.vector.tensor_reduce(v[:, p, :], masked[:, p, :].rearrange("p (a r) -> p r a", r=R), AX.X,
                                                ALU.add).then_inc(picked_ok, 1)
                        dve.wait_ge(picked_ok, t + 1)
                        if n >= 2:
                            dve.wait_ge(zt_full, 2 * t - 2)
                        else:
                            dve.wait_ge(zt_full, i * PER * 2)
                        nc.vector.scalar_tensor_tensor(z[:, p, :].rearrange("p (a r) -> p a r", r=R),
                                                       picked[:, p, :].unsqueeze(2).to_broadcast([P, NA, R]),
                                                       1.0 / TOPK ** 2, v[:, p, :].unsqueeze(1).to_broadcast([P, NA, R]),
                                                       ALU.mult, ALU.mult).then_inc(z_ok, 1)
                    else:
                        for q in range(2):
                            dve.wait_ge(zt_high, t * 2 + q + 1)
                            nc.vector.tensor_tensor(zT_lo[:, 4 * q:4 * q + 4, :],
                                                    ps_z[:, q, :].rearrange("p (a s) -> p a s", a=4),
                                                    f(zT_hi[:, 4 * q:4 * q + 4, :]), ALU.subtract).then_inc(zt_low, 1)
                        dve.wait_ge(y_full, t + 1)
                        dve.wait_ge(stored, 16 * PER * i)
                        nc.vector.tensor_tensor(y[:, n, :], ps_y[:, 0:H], bias_s[:, :], ALU.add).then_inc(y_read, 1)
                        dve.wait_ge(y_read, t + 1)
                        nc.vector.tensor_tensor(y[:, n, :], y[:, n, :], xs[:, n, :], ALU.add).then_inc(y_ok, 1)


HD1, NH1, G1, HPG1 = 16, 16, 4, 4
PAD = -3.0e38


def second_plan():
    tiles, per = NH1 * QT, HPG1 * QT

    def turns(g):
        nxt, g = divmod(g, G1)
        kt, qt = [("kt", g, j, nxt) for j in range(4)], [("qt", g, j, nxt) for j in range(QT)]
        return {1: [qt[0], kt[0]], 3: [kt[1], qt[1]], 5: kt[2:]}

    steps = []
    for t in range(tiles + 2):
        g, at = divmod(t, per)
        work = turns(g + 1).get(at, []) if g < G1 else []
        if g == G1 // 2:
            work = work + {0: [("ln", 0, 0, 1), ("xt", 0, 0, 1)], 1: [("qp", 0, 0, 1)], 2: [("kv", 0, 0, 1)],
                           4: [("kv", 0, 1, 1)], 6: [("kv", 0, 2, 1)], 7: [("kv", 0, 3, 1)]}.get(at, [])
        head = t // 2 - 1
        pv = [("pv", head, 2 * (t % 2) + j, 0) for j in range(2)] if head >= 0 else []
        if 1 <= t < tiles:
            steps.append(("exp", t, 0, 0))
        if t == tiles - 1:
            steps.append(("mask", 0, 0, 1))
        if t < tiles:
            steps.append(("max", (t + 1) % tiles, 0, (t + 1) // tiles))
        if t < tiles:
            steps += pv + [("turn", t, j, 0) for j in range(3)] + [("scores", (t + 2) % tiles, 0, (t + 2) // tiles), ("turn", t, 3, 0)]
        else:
            steps += pv
            if t == tiles:
                steps += [("inv", 0, 0, 0), ("exp", 0, 0, 1)]
        steps += work
        if t % 2 and pv:
            steps.append(("take", head, 0, 0))
    return steps + [("rows", 0, 0, 0), ("rows", 1, 0, 0), ("wo", 0, 0, 0), ("wo", 1, 0, 0)]


def second_attention(nc, x, out, ctxT, mask, alibi, wq, wkv, wo):
    steps = second_plan()
    TURN_BANKS = 3
    ring = Ring(steps, ("xt", "kv", "qp", "kt", "qt", "turn", "rows", "wo"), TURN_BANKS)
    TILES = NH1 * QT
    ROWS = 4 * HD1
    C = 1

    with ExitStack() as ctx:
        def sb(name, shape, dt=F32):
            return ctx.enter_context(nc.sbuf_tensor("a1_" + name, shape, dt))

        def sem(name):
            return ctx.enter_context(nc.semaphore("a1_" + name))

        ctx_s = sb("ctx", [P, KC, SKP])
        wkv_s, wq_s, wo_s = sb("wkv", [P, KC, P]), sb("wq", [P, KC, H]), sb("wo", [P, HPG1, H])
        mask8 = sb("mask8", [P, SK], mybir.dt.uint8)
        maskt = sb("mask", [P, SKC])
        kv_raw = sb("kv_raw", [P, KT, P])
        k_rows = [sb(f"k_rows{i}", [P, KT, P]) for i in range(2)]
        q_rows = sb("q_rows", [P, QT, NH1, P])
        kk = [sb(f"kk{i}", [P, SKP], F32R) for i in range(2)]
        qq = [sb(f"qq{i}", [P, HPG1, S], F32R) for i in range(2)]
        vv = sb("vv", [P, KT, G1, 2, HD1], F32R)
        q_raw = sb("q_raw", [P, QT, H])
        alibi_s = sb("alibi", [P, QT, NH1, 2])
        place = sb("place", [P, KT])
        prob = [sb(f"prob{i}", [P, SKP]) for i in range(2)]
        pt_hi, pt_lo = ([sb(f"{n}{i}", [P, KT, S], F32R) for i in range(2)] for n in ("pt_hi", "pt_lo"))
        heads = sb("heads", [P, HPG1, S])
        x_in, x_res, x_out, xn = (sb(n, [P, QT, H]) for n in ("x_in", "x_res", "x_out", "xn"))
        xT = sb("xT", [P, KC, S])
        ident, half = sb("ident", [P, P]), sb("half", [P, QT])
        top, negmax = sb("top", [P, 2, 2]), sb("negmax", [P, 2])
        total, inv = sb("total", [P, QT * HPG1 * G1]), sb("inv", [P, QT * HPG1 * G1])
        inv_rows = sb("inv_rows", [P, QT * HPG1 * G1, P // G1])
        ln6, ln2, lnr = sb("ln6", [P, QT, 6]), sb("ln2", [P, QT, 2]), sb("lnr", [P, QT])

        ps_s = ctx.enter_context(nc.psum_tensor("a1_ps_s", [P, CHUNKS, BANK], F32))
        ps_t = ctx.enter_context(nc.psum_tensor("a1_ps_t", [P, TURN_BANKS, BANK], F32))
        ps_o = ctx.enter_context(nc.psum_tensor("a1_ps_o", [P, BANK], F32))

        (w_in, al_in, const_set, const_ok, ctx_in, ctx_used, x_in_s, x_kept, mask_in, mask_ok, ln_step, ln_var,
         ln_rstd, x_norm, al_step, q_high, q_low, v_high, v_split, k_high, k_low, bank_full, scores_full, scored,
         negmax_ok, exp_ok, high_ok, pv_done, taken, inv_step, inv_ok, x_done, x_stored, dve_passed, pool_passed,
         sp_passed) = (
            sem(n) for n in ("w_in", "al_in", "const_set", "const_ok", "ctx_in", "ctx_used", "x_in_s", "x_kept",
                             "mask_in", "mask_ok", "ln_step", "ln_var", "ln_rstd", "x_norm", "al_step", "q_high",
                             "q_low", "v_high", "v_split", "k_high", "k_low", "bank_full", "scores_full", "scored",
                             "negmax_ok", "exp_ok", "high_ok", "pv_done", "taken", "inv_step", "inv_ok", "x_done",
                             "x_stored", "dve_passed", "pool_passed", "sp_passed"))
        bank_free = [sem(f"bank_free{i}") for i in range(TURN_BANKS)]

        def f(ap):
            return ap.bitcast(F32)

        def r(ap):
            return ap.bitcast(F32R)

        def is_free(eng, part, b, step, done):
            bank = ring.bank(part, step)
            eng.wait_ge(bank_free[bank], ring.tenants(part, b, step) + done + C)
            return ps_t[:, bank, :]

        def is_full(eng, part, b, step):
            eng.wait_ge(bank_full, ring.before(part, b, step) + 1 + C)
            return ps_t[:, ring.bank(part, step), :]

        def batches(eng, body):
            body(0, -1, [s for s in steps if s[-1]])
            if B > 1:
                with eng.Fori(0, B - 1) as b:
                    body(1, b, steps)
            body(2, B - 1, [s for s in steps if not s[-1]])

        block = ctx.enter_context(nc.Block())

        @block.sync
        def _(sp):
            sp.sem_inc(x_stored, C)
            for t, src in ((wkv_s, wkv), (wq_s, wq), (wo_s, wo)):
                sp.dma_start(t[:, :, :], src).then_inc(w_in, 16)
            sp.dma_start(alibi_s[:, :, :, :], alibi.rearrange("(t p) h c -> p t h c", p=P)).then_inc(al_in, 16)

            def batch(part, b, _):
                if part < 2:
                    sp.wait_ge(x_kept, b + 1 + C)
                    stand(sp, sp_passed)
                    sp.dma_start(x_in[:, :, :], x[b + 1].rearrange("(t p) h -> p t h", p=P)).then_inc(x_in_s, 16)
                    sp.wait_ge(ctx_used, b + 1 + C)
                    stand(sp, sp_passed)
                    sp.dma_start(ctx_s[:, :, :].rearrange("p c k -> p (c k)"), ctxT[b + 1]).then_inc(ctx_in, 16)
                    sp.wait_ge(mask_ok, b + 1 + C)
                    stand(sp, sp_passed)
                    sp.dma_start(mask8[:, :], mask[b + 1].partition_broadcast(P)).then_inc(mask_in, 16)
                if part:
                    sp.wait_ge(x_done, b + 1 + C)
                    stand(sp, sp_passed)
                    sp.dma_start(out[b].rearrange("(t p) h -> p t h", p=P), x_out[:, :, :]).then_inc(x_stored, 16)

            batches(sp, batch)
            sp.wait_ge(x_stored, 16 * B + C)

        @block.gpsimd
        def _(pool):
            for s in (x_kept, ctx_used, q_low, v_split, k_low):
                pool.sem_inc(s, C)
            nc.gpsimd.memset(half[:, :], -0.5).then_inc(const_ok, 1)
            nc.gpsimd.memset(prob[0][:, SKC:], 0.0).then_inc(const_ok, 1)
            nc.gpsimd.memset(prob[1][:, SKC:], 0.0).then_inc(const_ok, 1)
            nc.gpsimd.memset(ident[:, :], 0.0).then_inc(const_set, 1)
            nc.gpsimd.memset(q_rows[:, :, :, :], 0.0).then_inc(const_set, 1)
            for t in k_rows:
                nc.gpsimd.memset(t[:, :, :], 0.0).then_inc(const_set, 1)
            nc.gpsimd.iota(place[:, :], pattern=[[P, KT]], base=0, channel_multiplier=1,
                           allow_small_or_imprecise_dtypes=True).then_inc(const_set, 1)
            pool.wait_ge(const_set, 5)
            nc.gpsimd.affine_select(out=ident[:, :], in_=ident[:, :], compare_op=ALU.not_equal, fill=1.0, base=0,
                                    pattern=[[-1, P]], channel_multiplier=1).then_inc(const_ok, 1)
            for t in k_rows:
                nc.gpsimd.tensor_scalar(t[:, :, ROWS:ROWS + 2], place[:, :].unsqueeze(2).to_broadcast([P, KT, 2]),
                                        1.0, None, ALU.mult).then_inc(const_ok, 1)
                nc.gpsimd.memset(t[:, :, ROWS + 2:ROWS + 4], 1.0).then_inc(const_ok, 1)
            pool.wait_ge(al_in, 16)
            for q in range(QT):
                hi, lo = q_rows[:, q, :, ROWS:ROWS + 4:2], q_rows[:, q, :, ROWS + 1:ROWS + 4:2]
                nc.gpsimd.tensor_scalar(r(hi), alibi_s[:, q, :, :], 1.0, None, ALU.mult).then_inc(al_step, 1)
                pool.wait_ge(al_step, q + 1)
                nc.gpsimd.tensor_tensor(lo, alibi_s[:, q, :, :], hi, ALU.subtract).then_inc(const_ok, 1)
            pool.wait_ge(const_ok, 10)

            def keys(b, g):
                stand(pool, pool_passed)
                t = k_rows[g % 2]
                src = kv_raw[:, :, g * HD1:(g + 1) * HD1]
                for i in (0, 2):
                    nc.gpsimd.tensor_scalar(r(t[:, :, i * HD1:(i + 1) * HD1]), src, 1.0, None,
                                            ALU.mult).then_inc(k_high, 1)
                pool.wait_ge(k_high, (b * G1 + g) * 2 + 2)
                for i in (1, 3):
                    nc.gpsimd.tensor_tensor(t[:, :, i * HD1:(i + 1) * HD1], src, t[:, :, 0:HD1],
                                            ALU.subtract).then_inc(k_low, 1)

            def batch(part, b, _):
                if part:
                    pool.wait_ge(x_done, b + C)
                    stand(pool, pool_passed)
                    nc.gpsimd.tensor_scalar(x_res[:, :, :], x_in[:, :, :], 1.0, None, ALU.mult).then_inc(x_kept, 1)
                    is_full(pool, part, b, ("kt", 1, 3, 0))
                    keys(b, 3)
                if part == 2:
                    return
                nb = b + 1
                pool.wait_ge(ln_var, nb * QT + QT)
                nc.gpsimd.tensor_tensor(lnr[:, :], ln2[:, :, 1], half[:, :], ALU.pow).then_inc(ln_rstd, 1)
                is_free(pool, part, b, ("qp", 0, 0, 1), 1)
                if part:
                    is_full(pool, part, b, ("qt", 3, 1, 0))
                stand(pool, pool_passed)
                for q in range(QT):
                    src = q_raw[:, q, :].rearrange("p (h d) -> p h d", h=NH1)
                    hi = q_rows[:, q, :, 0:HD1]
                    nc.gpsimd.tensor_scalar(r(hi), src, 1.0, None, ALU.mult).then_inc(q_high, 1)
                    nc.gpsimd.tensor_scalar(r(q_rows[:, q, :, HD1:2 * HD1]), src, 1.0, None,
                                            ALU.mult).then_inc(q_high, 1)
                    pool.wait_ge(q_high, (nb * QT + q) * 2 + 2)
                    for i in (2, 3):
                        nc.gpsimd.tensor_tensor(q_rows[:, q, :, i * HD1:(i + 1) * HD1], src, hi,
                                                ALU.subtract).then_inc(q_low, 1)
                is_free(pool, part, b, ("kv", 0, 3, 1), 1)
                pool.sem_inc(ctx_used, 1)
                for g in range(3):
                    if part:
                        is_full(pool, part, b, ("kt", g + 2, 3, 0) if g < 2 else ("kt", 0, 3, 1))
                    elif g == 2:
                        is_full(pool, part, b, ("kt", 0, 3, 1))
                    keys(nb, g)
                pool.wait_ge(pv_done, nb * NH1 * 4 + C)
                stand(pool, pool_passed)
                for i in range(G1):
                    v = kv_raw[:, :, P // 2 + i * HD1:P // 2 + (i + 1) * HD1]
                    nc.gpsimd.tensor_scalar(vv[:, :, i, 0, :], v, 1.0, None, ALU.mult).then_inc(v_high, 1)
                pool.wait_ge(v_high, nb * G1 + G1)
                for i in range(G1):
                    v = kv_raw[:, :, P // 2 + i * HD1:P // 2 + (i + 1) * HD1]
                    nc.gpsimd.tensor_tensor(vv[:, :, i, 1, :], v, f(vv[:, :, i, 0, :]),
                                            ALU.subtract).then_inc(v_split, 1)

            batches(pool, batch)

        @block.tensor
        def _(pe):
            for s in (bank_full, pv_done):
                pe.sem_inc(s, C)
            pe.wait_ge(const_ok, 10)
            pe.wait_ge(w_in, 48)

            def batch(part, b, order):
                for step in order:
                    kind, n, j, nxt = step
                    nb = b + nxt
                    if kind in ("xt", "qp", "kv", "kt", "qt", "turn", "rows", "wo"):
                        ps = is_free(pe, part, b, step, 0)
                    if kind == "xt":
                        pe.wait_ge(x_norm, nb * QT + QT)
                        for c in range(KC):
                            for q in range(QT):
                                mm = nc.tensor.transpose(ps[:, c * S + q * P:c * S + (q + 1) * P],
                                                         xn[:, q, c * P:(c + 1) * P], ident[:, :])
                        mm.then_inc(bank_full, 1)
                    elif kind == "qp":
                        is_free(pe, part, b, ("xt", 0, 0, nxt), 1)
                        for q in range(QT):
                            for c in range(KC):
                                mm = nc.tensor.matmul(ps[:, q * H:(q + 1) * H], xT[:, c, q * P:(q + 1) * P],
                                                      wq_s[:, c, :], start=c == 0, stop=c == KC - 1)
                        mm.then_inc(bank_full, 1)
                    elif kind == "kv":
                        if j == 0:
                            pe.wait_ge(ctx_in, nb * 16 + 16)
                        for i, k in enumerate(KGROUPS[j]):
                            for c in range(KC):
                                mm = nc.tensor.matmul(ps[:, i * P:(i + 1) * P], ctx_s[:, c, k * P:(k + 1) * P],
                                                      wkv_s[:, c, :], start=c == 0, stop=c == KC - 1)
                        mm.then_inc(bank_full, 1)
                    elif kind == "kt":
                        pe.wait_ge(k_low, (nb * G1 + n) * 2 + 2 + C)
                        for i, k in enumerate(KGROUPS[j]):
                            mm = nc.tensor.transpose(ps[:, i * P:(i + 1) * P], k_rows[n % 2][:, k, :], ident[:, :])
                        mm.then_inc(bank_full, 1)
                    elif kind == "qt":
                        pe.wait_ge(q_low, (nb * QT + QT) * 2 + C)
                        for i in range(HPG1):
                            mm = nc.tensor.transpose(ps[:, i * P:(i + 1) * P], q_rows[:, j, n * HPG1 + i, :],
                                                     ident[:, :])
                        mm.then_inc(bank_full, 1)
                    elif kind == "scores":
                        head, q = divmod(n, QT)
                        g = head // HPG1
                        if n % (HPG1 * QT) == 0:
                            for s in [("kt", g, i, nxt) for i in range(4)] + [("qt", g, i, nxt) for i in range(QT)]:
                                is_free(pe, part, b, s, 1)
                        for c in range(CHUNKS):
                            if c % 2 == 0:
                                pe.wait_ge(scored, (nb * TILES + n) * 2 + c // 2 + C)
                            mm = nc.tensor.matmul(ps_s[:, c, 0:CW], qq[g % 2][:, head % HPG1, q * P:(q + 1) * P],
                                                  kk[g % 2][:, c * CW:(c + 1) * CW], start=True, stop=True)
                            if c % 2:
                                mm.then_inc(scores_full, 1)
                    elif kind == "turn":
                        pe.wait_ge(exp_ok, b * TILES + n + 1)
                        for i, k in enumerate(KGROUPS[j]):
                            mm = nc.tensor.transpose(ps[:, i * P:(i + 1) * P], prob[n % 2][:, k * P:(k + 1) * P],
                                                     ident[:, :])
                        mm.then_inc(bank_full, 1)
                    elif kind == "pv":
                        if j == 0:
                            pe.wait_ge(taken, b * NH1 + n + C)
                            if n == 0:
                                pe.wait_ge(v_split, (b + 1) * G1 + C)
                        is_free(pe, part, b, ("turn", 2 * n + 1, j, 0), 1)
                        for k in KGROUPS[j]:
                            v = vv[:, k, :, :, :].rearrange("p g c d -> p (g c d)")
                            nc.tensor.matmul(ps_o[:, 0:S], v, pt_hi[n % 2][:, k, :], start=k == 0, stop=False)
                            mm = nc.tensor.matmul(ps_o[:, 0:S], v, pt_lo[n % 2][:, k, :], start=False,
                                                  stop=k == KT - 1)
                        mm.then_inc(pv_done, 1)
                    elif kind == "rows":
                        pe.wait_ge(inv_step, b + 1)
                        for i in range(2):
                            for q in range(QT):
                                at = (q * HPG1 + 2 * n + i) * G1
                                mm = nc.tensor.matmul(ps[:, i * S + q * P:i * S + (q + 1) * P],
                                                      inv_rows[:, at:at + G1, :].rearrange("p g r -> p (g r)"),
                                                      ident[:, :], start=True, stop=True)
                        mm.then_inc(bank_full, 1)
                    elif kind == "wo":
                        if n == 0:
                            for s in (("rows", 0, 0, 0), ("rows", 1, 0, 0)):
                                is_free(pe, part, b, s, 1)
                        for i in range(HPG1):
                            mm = nc.tensor.matmul(ps[:, 0:H], heads[:, i, n * P:(n + 1) * P], wo_s[:, i, :],
                                                  start=i == 0, stop=i == HPG1 - 1)
                        mm.then_inc(bank_full, 1)

            batches(pe, batch)

        @block.scalar
        def _(act):
            act.sem_inc(taken, C)

            def batch(part, b, order):
                for step in order:
                    kind, n, j, nxt = step
                    nb = b + nxt
                    if kind in ("kt", "qt"):
                        ps = is_full(act, part, b, step)
                        free = bank_free[ring.bank(part, step)]
                        if n >= 1 or part:
                            act.wait_ge(scored, (nb * TILES + (n - 1) * HPG1 * QT) * 2 + C + 1)
                        if kind == "kt":
                            w, k0 = len(KGROUPS[j]), KGROUPS[j][0]
                            nc.scalar.copy(kk[n % 2][:, k0 * P:(k0 + w) * P], ps[:, 0:w * P]).then_inc(free, 1)
                        else:
                            nc.scalar.copy(qq[n % 2][:, :, j * P:(j + 1) * P],
                                           ps.rearrange("p (h s) -> p h s", h=HPG1)).then_inc(free, 1)
                    elif kind == "turn":
                        ps = is_full(act, part, b, step)
                        w, k0 = len(KGROUPS[j]), KGROUPS[j][0]
                        head, q = divmod(n, QT)
                        if q == 0:
                            act.wait_ge(pv_done, (b * NH1 + head - 2) * 4 + j + 1 + C if head >= 2
                                        else b * NH1 * 4 + C)
                        nc.scalar.copy(pt_hi[head % 2][:, k0:k0 + w, q * P:(q + 1) * P],
                                       ps[:, 0:w * P].rearrange("p (k s) -> p k s", k=w)).then_inc(high_ok, 1)
                    elif kind == "exp":
                        head, q = divmod(n, QT)
                        act.wait_ge(negmax_ok, nb * TILES + n + 1)
                        if n == 0:
                            act.wait_ge(inv_ok, nb + C)
                        at = (q * HPG1 + head % HPG1) * G1 + head // HPG1
                        nc.scalar.activation(prob[n % 2][:, 0:SKC], prob[n % 2][:, 0:SKC], ACT.Exp,
                                             bias=negmax[:, n % 2:n % 2 + 1], scale=1.0,
                                             accum_out=total[:, at:at + 1]).then_inc(exp_ok, 1)
                    elif kind == "take":
                        g, i = divmod(n, HPG1)
                        act.wait_ge(pv_done, (b * NH1 + n) * 4 + 4 + C)
                        if n == 0:
                            act.wait_ge(bank_full, ring.before(part, b) + C)
                        own = slice(g * P // G1, (g + 1) * P // G1)
                        nc.scalar.copy(heads[own, i, :], ps_o[own, 0:S]).then_inc(taken, 1)

            batches(act, batch)

        @block.vector
        def _(dve):
            for s in (*bank_free, mask_ok, inv_ok, x_done):
                dve.sem_inc(s, C)
            dve.sem_inc(scored, C + 1)
            nc.vector.memset(maskt[:, SK:], PAD)

            def batch(part, b, order):
                for step in order:
                    kind, n, j, nxt = step
                    nb = b + nxt
                    if kind == "ln":
                        dve.wait_ge(x_in_s, nb * 16 + 16)
                        for q in range(QT):
                            nc.vector.bn_stats(ln6[:, q, :], x_in[:, q, :]).then_inc(ln_step, 1)
                            dve.wait_ge(ln_step, (nb * QT + q) * 2 + 1)
                            stand(dve, dve_passed)
                            nc.vector.bn_aggr(ln2[:, q, :], ln6[:, q, :]).then_inc(ln_step, 1)
                            dve.wait_ge(ln_step, (nb * QT + q) * 2 + 2)
                            nc.vector.tensor_scalar(ln2[:, q, 1:2], ln2[:, q, 1:2], EPS_LN, None,
                                                    ALU.add).then_inc(ln_var, 1)
                        dve.wait_ge(ln_rstd, nb + 1)
                        if part:
                            dve.wait_ge(bank_full, ring.before(part, b) + C)
                        for q in range(QT):
                            nc.vector.tensor_scalar(xn[:, q, :], x_in[:, q, :], ln2[:, q, 0:1], lnr[:, q:q + 1],
                                                    ALU.subtract, ALU.mult).then_inc(x_norm, 1)
                    elif kind == "mask":
                        dve.wait_ge(mask_in, nb * 16 + 16)
                        nc.vector.tensor_scalar(maskt[:, 0:SK], mask8[:, :], -NEG, NEG, ALU.mult,
                                                ALU.add).then_inc(mask_ok, 1)
                    elif kind in ("xt", "qp", "kv"):
                        ps = is_full(dve, part, b, step)
                        free = bank_free[ring.bank(part, step)]
                        if kind == "xt":
                            nc.vector.tensor_copy(xT[:, :, :].rearrange("p c s -> p (c s)"), ps).then_inc(free, 1)
                        elif kind == "qp":
                            dve.wait_ge(q_low, nb * QT * 2 + C)
                            nc.vector.tensor_scalar(q_raw[:, :, :].rearrange("p t h -> p (t h)"), ps,
                                                    float(HD1) ** -0.5, None, ALU.mult).then_inc(free, 1)
                        else:
                            if j == 0:
                                dve.wait_ge(k_low, nb * G1 * 2 + C)
                                dve.wait_ge(v_split, nb * G1 + C)
                            w, k0 = len(KGROUPS[j]), KGROUPS[j][0]
                            nc.vector.tensor_copy(kv_raw[:, k0:k0 + w, :].rearrange("p k d -> p (k d)"),
                                                  ps[:, 0:w * P]).then_inc(free, 1)
                    elif kind == "turn":
                        w, k0 = len(KGROUPS[j]), KGROUPS[j][0]
                        head, q = divmod(n, QT)
                        bank = ring.bank(part, step)
                        dve.wait_ge(high_ok, (b * TILES + n) * 4 + j + 1)
                        nc.vector.tensor_tensor(pt_lo[head % 2][:, k0:k0 + w, q * P:(q + 1) * P],
                                                ps_t[:, bank, 0:w * P].rearrange("p (k s) -> p k s", k=w),
                                                f(pt_hi[head % 2][:, k0:k0 + w, q * P:(q + 1) * P]),
                                                ALU.subtract).then_inc(bank_free[bank], 1)
                    elif kind == "max":
                        if n == 0:
                            dve.wait_ge(mask_ok, nb + 1 + C)
                        if n >= 2:
                            is_full(dve, part, b, ("turn", n - 2, 3, 0))
                        elif n == 1:
                            dve.wait_ge(bank_full, ring.before(part, b) + C)
                        elif part:
                            is_full(dve, part, b, ("turn", TILES - 2, 3, 0))
                        for c in range(2):
                            dve.wait_ge(scores_full, (nb * TILES + n) * 2 + c + 1)
                            stand(dve, dve_passed)
                            k = slice(2 * c * CW, (2 * c + 2) * CW)
                            nc.vector.tensor_tensor_reduce(
                                prob[n % 2][:, k].rearrange("p (c k) -> p c k", c=2), ps_s[:, 2 * c:2 * c + 2, 0:CW],
                                maskt[:, k].rearrange("p (c k) -> p c k", c=2), 1.0, -3.4e38, ALU.add,
                                ALU.max, top[:, n % 2, c:c + 1]).then_inc(scored, 1)
                        dve.wait_ge(scored, (nb * TILES + n) * 2 + 3 + C)
                        nc.vector.tensor_reduce(negmax[:, n % 2:n % 2 + 1], top[:, n % 2, :], AX.X, ALU.max,
                                                negate=True).then_inc(negmax_ok, 1)
                    elif kind == "inv":
                        dve.wait_ge(exp_ok, (b + 1) * TILES)
                        nc.vector.reciprocal(inv[:, :], total[:, :]).then_inc(inv_ok, 1)
                        dve.wait_ge(inv_ok, b + 1 + C)
                        nc.vector.tensor_copy(inv_rows[:, :, :], inv[:, :].unsqueeze(2).to_broadcast(
                            [P, QT * HPG1 * G1, P // G1])).then_inc(inv_step, 1)
                    elif kind == "rows":
                        ps = is_full(dve, part, b, step)
                        if n == 0:
                            dve.wait_ge(taken, (b + 1) * NH1 + C)
                        h = heads[:, 2 * n:2 * n + 2, :].rearrange("p h s -> p (h s)")
                        nc.vector.tensor_tensor(h, ps, h, ALU.mult).then_inc(bank_free[ring.bank(part, step)], 1)
                    elif kind == "wo":
                        ps = is_full(dve, part, b, step)
                        if n == 0:
                            dve.wait_ge(x_kept, b + 1 + C)
                            dve.wait_ge(x_stored, b * 16 + C)
                        nc.vector.tensor_tensor(x_out[:, n, :], ps[:, 0:H], x_res[:, n, :],
                                                ALU.add).then_inc(bank_free[ring.bank(part, step)], 1)
                        if n == 1:
                            is_free(dve, part, b, ("wo", 0, 0, 0), 1)
                            is_free(dve, part, b, ("wo", 1, 0, 0), 1)
                            dve.sem_inc(x_done, 1)

            batches(dve, batch)


NE, INNER, TOP2 = 8, 704, 2
IT = -(-INNER // P)
Q_IN, Q_MIN = 128, -128
MAGIC = 1.5 * 2.0 ** 23


def second_ffn(nc, x, out, wg, w13, w2, table):
    TILES = B * S // P
    BLK = 4
    BLOCKS = TILES // BLK
    NT = -Q_MIN + 1

    with ExitStack() as ctx:
        def sb(name, shape, dt=F32):
            return ctx.enter_context(nc.sbuf_tensor("f1_" + name, shape, dt))

        def sem(name):
            return ctx.enter_context(nc.semaphore("f1_" + name))

        acc = sb("acc", [P, TILES, H])
        xT_hi, xT_lo = (sb(n, [P, KC, TILES * P], F32R) for n in ("xT_hi", "xT_lo"))
        weight = sb("weight", [P, TILES, NE])
        wg_raw = sb("wg_raw", [P, KC, NE])
        table_s, steps_s = sb("table", [P, NT]), sb("steps", [P, NT])
        w13_raw, w2_raw = sb("w13_raw", [P, 2, KC, IT * P]), sb("w2_raw", [P, IT, H])
        w13_hi, w13_lo = ([sb(f"{n}{i}", [P, 2, KC, IT * P], F32R) for i in range(2)] for n in ("w13_hi", "w13_lo"))
        w2_hi, w2_lo = ([sb(f"{n}{i}", [P, IT, H], F32R) for i in range(2)] for n in ("w2_hi", "w2_lo"))
        ident, half = sb("ident", [P, P]), sb("half", [P, 1])
        xn, xT = sb("xn", [P, H]), sb("xT", [P, KC, P])
        ln6, ln2, rstd = sb("ln6", [P, 6]), sb("ln2", [P, 2]), sb("rstd", [P, 1])
        level, top = sb("level", [P, NE]), sb("top", [P, 1])
        onehot = sb("onehot", [P, NE, NT])
        value, prob = sb("value", [P, NE]), sb("prob", [P, NE])
        total, m8 = sb("total", [P, 1]), sb("m8", [P, 8])
        above, equal, rank, keep, ones = (sb(n, [P, NE]) for n in ("above", "equal", "rank", "keep", "ones"))
        nabove = sb("nabove", [P, 1])
        gate = sb("gate", [P, 2, BLK * P])
        h_raw = sb("h_raw", [P, 2, BLK * P])
        h_hi, h_lo = (sb(n, [P, IT, BLK * P], F32R) for n in ("h_hi", "h_lo"))

        ps_h = ctx.enter_context(nc.psum_tensor("f1_ps_h", [P, 2, 2, BANK], F32))
        ps_y = ctx.enter_context(nc.psum_tensor("f1_ps_y", [P, 2, BANK], F32))
        ps_x = ctx.enter_context(nc.psum_tensor("f1_ps_x", [P, BANK], F32))
        ps_l = ctx.enter_context(nc.psum_tensor("f1_ps_l", [P, BANK], F32))

        (c_in, x_in, w_in, const_set, const_ok, chain, var_ok, rstd_ok, x_norm, xt_full, xt_ok, xt_high, xt_low,
         l_full, l_read, w_high, w_low, h_full, gate_ok, h_ok, h_high, h_split, y_full, y_read, stored, weight_sum,
         weight_ok) = (
            sem(n) for n in ("c_in", "x_in", "w_in", "const_set", "const_ok", "chain", "var_ok", "rstd_ok", "x_norm",
                             "xt_full", "xt_ok", "xt_high", "xt_low", "l_full", "l_read", "w_high", "w_low", "h_full",
                             "gate_ok", "h_ok", "h_high", "h_split", "y_full", "y_read", "stored",
                             "weight_sum", "weight_ok"))

        dve_passed, pe_passed, sp_passed = sem("dve_passed"), sem("pe_passed"), sem("sp_passed")

        def f(ap):
            return ap.bitcast(F32)

        block = ctx.enter_context(nc.Block())

        @block.sync
        def _(sp):
            sp.dma_start(acc[:, :, :], x.rearrange("t p h -> p t h")).then_inc(x_in, 16)
            sp.dma_start(wg_raw[:, :, :], wg).then_inc(c_in, 16)
            sp.dma_start(table_s[:, :], table[0].partition_broadcast(P)).then_inc(c_in, 16)
            sp.dma_start(steps_s[:, :], table[1].partition_broadcast(P)).then_inc(c_in, 16)
            with sp.Fori(0, NE) as e:
                sp.wait_ge(w_low, e * 2)
                stand(sp, sp_passed)
                sp.dma_start(w13_raw[:, :, :, :], w13[e]).then_inc(w_in, 16)
                sp.dma_start(w2_raw[:, :, :], w2[e]).then_inc(w_in, 16)
            sp.wait_ge(y_read, NE * TILES + 1)
            sp.dma_start(out.rearrange("t p h -> p t h"), acc[:, :, :]).then_inc(stored, 16)
            sp.wait_ge(stored, 16)

        @block.gpsimd
        def _(pool):
            nc.gpsimd.memset(half[:, :], -0.5).then_inc(const_ok, 1)
            nc.gpsimd.memset(ones[:, :], 1.0).then_inc(const_ok, 1)
            nc.gpsimd.memset(ident[:, :], 0.0).then_inc(const_set, 1)
            pool.wait_ge(const_set, 1)
            nc.gpsimd.affine_select(out=ident[:, :], in_=ident[:, :], compare_op=ALU.not_equal, fill=1.0, base=0,
                                    pattern=[[-1, P]], channel_multiplier=1).then_inc(const_ok, 1)
            pool.wait_ge(const_ok, 3)
            with pool.Fori(0, TILES) as t:
                pool.wait_ge(var_ok, t + 1)
                nc.gpsimd.tensor_tensor(rstd[:, :], ln2[:, 1:2], half[:, :], ALU.pow).then_inc(rstd_ok, 1)

            def weights(e, i):
                pool.wait_ge(w_in, e * 32 + 32)
                pool.wait_ge(w_high, e * 2 + 2)
                nc.gpsimd.tensor_tensor(w13_lo[i][:, :, :, :], w13_raw[:, :, :, :], f(w13_hi[i][:, :, :, :]),
                                        ALU.subtract).then_inc(w_low, 1)
                nc.gpsimd.tensor_tensor(w2_lo[i][:, :, :], w2_raw[:, :, :], f(w2_hi[i][:, :, :]),
                                        ALU.subtract).then_inc(w_low, 1)

            weights(0, 0)
            def experts(pair, more):
                for i in range(2):
                    e = pair * 2 + i
                    for blk in range(BLOCKS):
                        for m in range(IT):
                            n = (e * BLOCKS + blk) * IT + m
                            pool.wait_ge(h_high, n + 1)
                            nc.gpsimd.tensor_tensor(h_lo[:, m, :], h_raw[:, m % 2, :], f(h_hi[:, m, :]),
                                                    ALU.subtract).then_inc(h_split, 1)
                        if blk == 0 and i == 0:
                            weights(e + 1, 1)
                        if blk == 0 and i == 1 and more:
                            weights(e + 1, 0)

            with pool.Fori(0, NE // 2 - 1) as pair:
                experts(pair, True)
            experts(NE // 2 - 1, False)

        @block.tensor
        def _(pe):
            pe.wait_ge(const_ok, 3)
            pe.wait_ge(c_in, 48)
            with pe.Fori(0, TILES) as t:
                pe.wait_ge(x_norm, t + 1)
                for c in range(KC):
                    mm = nc.tensor.transpose(ps_x[:, c * P:(c + 1) * P], xn[:, c * P:(c + 1) * P], ident[:, :])
                mm.then_inc(xt_full, 1)
                pe.wait_ge(xt_ok, t + 1)
                pe.wait_ge(l_read, t)
                for c in range(KC):
                    mm = nc.tensor.matmul(ps_l[:, 0:NE], xT[:, c, :], wg_raw[:, c, :], start=c == 0, stop=c == KC - 1)
                mm.then_inc(l_full, 1)
            pe.wait_ge(xt_high, TILES)
            pe.wait_ge(xt_low, TILES)

            def split_mm(to, lhs, rhs, first, last):
                (lh, ll), (rh, rl) = lhs, rhs
                nc.tensor.matmul(to, lh, rh, start=first, stop=False)
                nc.tensor.matmul(to, ll, rh, start=False, stop=False)
                return nc.tensor.matmul(to, lh, rl, start=False, stop=last)

            with pe.Fori(0, NE // 2) as pair:
                for i in range(2):
                    e = pair * 2 + i
                    pe.wait_ge(w_low, e * 2 + 2)
                    stand(pe, pe_passed)
                    with pe.Fori(0, BLOCKS) as blk:
                        it = e * BLOCKS + blk
                        for m in range(IT):
                            n = it * IT + m
                            pe.wait_ge(h_ok, n)
                            for g in range(2):
                                for c in range(KC):
                                    mm = split_mm(ps_h[:, m % 2, g, :],
                                                  (w13_hi[i][:, g, c, m * P:(m + 1) * P], w13_lo[i][:, g, c, m * P:(m + 1) * P]),
                                                  (xT_hi[:, c, bass.ts(blk, BLK * P)], xT_lo[:, c, bass.ts(blk, BLK * P)]),
                                                  c == 0, c == KC - 1)
                            mm.then_inc(h_full, 1)
                        for q in range(BLK):
                            pe.wait_ge(y_read, it * BLK + q)
                            for m in range(IT):
                                if q == 0:
                                    pe.wait_ge(h_split, it * IT + m + 1)
                                k = slice(q * P, (q + 1) * P)
                                mm = split_mm(ps_y[:, q % 2, 0:H], (h_hi[:, m, k], h_lo[:, m, k]),
                                              (w2_hi[i][:, m, :], w2_lo[i][:, m, :]), m == 0, m == IT - 1)
                            mm.then_inc(y_full, 1)

        @block.scalar
        def _(act):
            with act.Fori(0, TILES) as t:
                act.wait_ge(xt_ok, t + 1)
                nc.scalar.copy(xT_hi[:, :, bass.ts(t, P)], xT[:, :, :]).then_inc(xt_high, 1)

            def weights(e, i):
                act.wait_ge(w_in, e * 32 + 32)
                nc.scalar.copy(w13_hi[i][:, :, :, :], w13_raw[:, :, :, :]).then_inc(w_high, 1)
                nc.scalar.copy(w2_hi[i][:, :, :], w2_raw[:, :, :]).then_inc(w_high, 1)

            weights(0, 0)
            def experts(pair, more):
                for i in range(2):
                    e = pair * 2 + i
                    for blk in range(BLOCKS):
                        for m in range(IT):
                            n = (e * BLOCKS + blk) * IT + m
                            act.wait_ge(h_full, n + 1)
                            if m < 2:
                                act.wait_ge(h_ok, (e * BLOCKS + blk) * IT + 1)
                            else:
                                act.wait_ge(h_ok, n)
                            nc.scalar.activation(gate[:, m % 2, :], ps_h[:, m % 2, 0, :], ACT.Silu).then_inc(gate_ok, 1)
                            act.wait_ge(h_ok, n + 2)
                            act.wait_ge(y_full, (e * BLOCKS + blk) * BLK)
                            nc.scalar.copy(h_hi[:, m, :], h_raw[:, m % 2, :]).then_inc(h_high, 1)
                        if blk == 0 and i == 0:
                            act.wait_ge(y_full, e * BLOCKS * BLK)
                            weights(e + 1, 1)
                        if blk == 0 and i == 1 and more:
                            act.wait_ge(y_full, e * BLOCKS * BLK)
                            weights(e + 1, 0)

            with act.Fori(0, NE // 2 - 1) as pair:
                experts(pair, True)
            experts(NE // 2 - 1, False)

        @block.vector
        def _(dve):
            nc.vector.memset(m8[:, :], 0.0).then_inc(h_ok, 1)
            nc.vector.memset(total[:, :], 0.0).then_inc(y_read, 1)
            dve.wait_ge(x_in, 16)
            dve.wait_ge(c_in, 48)
            dve.wait_ge(const_ok, 3)
            LINKS = 19
            with dve.Fori(0, TILES) as t:
                done = [0]

                def link(ins):
                    done[0] += 1
                    ins.then_inc(chain, 1)
                    dve.wait_ge(chain, t * LINKS + done[0])

                link(nc.vector.bn_stats(ln6[:, :], acc[:, bass.ds(t, 1), :].rearrange("p o h -> p (o h)")))
                stand(dve, dve_passed)
                link(nc.vector.bn_aggr(ln2[:, :], ln6[:, :]))
                nc.vector.tensor_scalar(ln2[:, 1:2], ln2[:, 1:2], EPS_LN, None, ALU.add).then_inc(var_ok, 1)
                dve.wait_ge(rstd_ok, t + 1)
                dve.wait_ge(xt_full, t)
                nc.vector.tensor_scalar(xn[:, :], acc[:, bass.ds(t, 1), :].rearrange("p o h -> p (o h)"), ln2[:, 0:1],
                                        rstd[:, :], ALU.subtract, ALU.mult).then_inc(x_norm, 1)
                dve.wait_ge(xt_full, t + 1)
                dve.wait_ge(xt_high, t)
                dve.wait_ge(l_full, t)
                nc.vector.tensor_copy(xT[:, :, :], ps_x[:, 0:H].rearrange("p (c s) -> p c s", c=KC)).then_inc(xt_ok, 1)
                dve.wait_ge(xt_high, t + 1)
                nc.vector.tensor_tensor(xT_lo[:, :, bass.ts(t, P)], xT[:, :, :], f(xT_hi[:, :, bass.ts(t, P)]),
                                        ALU.subtract).then_inc(xt_low, 1)
                dve.wait_ge(l_full, t + 1)
                link(nc.vector.tensor_scalar(level[:, :], ps_l[:, 0:NE], float(Q_IN), MAGIC, ALU.mult, ALU.add))
                nc.vector.tensor_scalar(level[:, :], level[:, :], MAGIC, None, ALU.subtract).then_inc(l_read, 1)
                dve.wait_ge(l_read, t + 1)
                link(nc.vector.tensor_reduce(top[:, :], level[:, :], AX.X, ALU.max))
                link(nc.vector.tensor_scalar(level[:, :], level[:, :], top[:, :], float(Q_MIN), ALU.subtract, ALU.max))
                link(nc.vector.tensor_tensor(onehot[:, :, :], level[:, :].unsqueeze(2).to_broadcast([P, NE, NT]),
                                             steps_s[:, :].unsqueeze(1).to_broadcast([P, NE, NT]), ALU.is_equal))
                link(nc.vector.tensor_tensor(onehot[:, :, :], onehot[:, :, :],
                                             table_s[:, :].unsqueeze(1).to_broadcast([P, NE, NT]), ALU.mult))
                link(nc.vector.tensor_reduce(value[:, :], onehot[:, :, :], AX.X, ALU.add))
                link(nc.vector.tensor_reduce(total[:, :], value[:, :], AX.X, ALU.add))
                link(nc.vector.reciprocal(total[:, :], total[:, :]))
                link(nc.vector.tensor_scalar(prob[:, :], value[:, :], total[:, :], None, ALU.mult))
                stand(dve, dve_passed)
                link(nc.vector.max(m8[:, :], value[:, :]))
                last = m8[:, TOP2 - 1:TOP2]
                link(nc.vector.tensor_scalar(above[:, :], value[:, :], last, None, ALU.is_gt))
                link(nc.vector.tensor_reduce(nabove[:, :], above[:, :], AX.X, ALU.add))
                link(nc.vector.tensor_scalar(equal[:, :], value[:, :], last, None, ALU.is_equal))
                link(nc.vector.tensor_tensor_scan(rank[:, :], ones[:, :], equal[:, :], nabove[:, 0:1], ALU.mult, ALU.add))
                link(nc.vector.scalar_tensor_tensor(keep[:, :], rank[:, :], float(TOP2), equal[:, :], ALU.is_le, ALU.mult))
                link(nc.vector.tensor_tensor(keep[:, :], above[:, :], keep[:, :], ALU.add))
                link(nc.vector.tensor_tensor(prob[:, :], prob[:, :], keep[:, :], ALU.mult))
                nc.vector.tensor_reduce(total[:, :], prob[:, :], AX.X, ALU.add).then_inc(weight_sum, 1)
                dve.wait_ge(weight_sum, 2 * t + 1)
                nc.vector.reciprocal(total[:, :], total[:, :]).then_inc(weight_sum, 1)
                dve.wait_ge(weight_sum, 2 * t + 2)
                nc.vector.tensor_scalar(weight[:, bass.ds(t, 1), :].rearrange("p o e -> p (o e)"), prob[:, :],
                                        total[:, :], None, ALU.mult).then_inc(weight_ok, 1)

            dve.wait_ge(weight_ok, TILES)
            with dve.Fori(0, NE // 2) as pair:
                for i in range(2):
                    e = pair * 2 + i
                    for blk in range(BLOCKS):
                        it = e * BLOCKS + blk
                        for m in range(IT):
                            n = it * IT + m
                            dve.wait_ge(gate_ok, n + 1)
                            if m < 2:
                                dve.wait_ge(h_split, it * IT)
                            else:
                                dve.wait_ge(h_split, n - 1)
                            nc.vector.tensor_tensor(h_raw[:, m % 2, :], gate[:, m % 2, :], ps_h[:, m % 2, 1, :],
                                                    ALU.mult).then_inc(h_ok, 1)
                        for q in range(BLK):
                            t = blk * BLK + q
                            dve.wait_ge(y_full, it * BLK + q + 1)
                            nc.vector.scalar_tensor_tensor(
                                acc[:, t, :], ps_y[:, q % 2, 0:H],
                                weight[:, t, bass.ds(e, 1)], acc[:, t, :], ALU.mult, ALU.add).then_inc(y_read, 1)


def network(nc, x, mask_q, mask_k, ctxT, wq0, wkv0, wo0, bias0, qn, kn, wa, wb, ww, bias_f, alibi, wq1, wkv1, wo1,
            wg, w13, w2, table, out):
    def rows(name):
        return nc.dram_tensor(name, (B, S, H), F32, kind="Internal").ap()

    def tiles(a):
        return a.rearrange("b (t p) h -> (b t) p h", p=P)

    x1, x2, x3 = rows("x1"), rows("x2"), rows("x3")
    first_attention(nc, x, x1, ctxT, mask_q, wq0, wkv0, wo0, bias0, qn, kn)
    first_ffn(nc, tiles(x1), tiles(x2), wa, wb, ww, bias_f)
    second_attention(nc, x2, x3, ctxT, mask_k, alibi, wq1, wkv1, wo1)
    second_ffn(nc, tiles(x3), tiles(out), wg, w13, w2, table)


def _sliced(np, w, kc):
    return np.ascontiguousarray(w.reshape(kc, w.shape[0] // kc, -1).transpose(1, 0, 2))


def _grouped(np, w, groups):
    n = w.shape[1] // groups
    return w.reshape(KC, P, groups, n).transpose(2, 1, 0, 3)


def kernel(**inputs):
    import numpy as np
    import concourse.bacc as _bacc
    from concourse import mybir as _mybir
    from concourse.bass_utils import run_bass_kernel_spmd as _run

    a = {k: np.asarray(v) for k, v in inputs.items()}
    f32 = np.float32

    ctxT = np.zeros((B, H, SKP), f32)
    ctxT[:, :, :SK] = a["ctx_2048"].transpose(0, 2, 1)
    w1, w3, w2 = a["L1_ffn_w1"], a["L1_ffn_w3"], a["L1_ffn_w2"]
    w13 = np.zeros((NE, 2, H, IT * P), f32)
    w13[:, 0, :, :INNER] = w1.transpose(0, 2, 1)
    w13[:, 1, :, :INNER] = w3.transpose(0, 2, 1)
    w2T = np.zeros((NE, IT * P, H), f32)
    w2T[:, :INNER] = w2.transpose(0, 2, 1)
    wo1 = np.repeat(a["L1_xattn_Wo"].reshape(G1, HPG1, 1, HD1, H), 2, axis=2)

    slopes = f32(2.0 ** -0.5) ** np.arange(1, NH1 + 1, dtype=f32)
    alibi = np.zeros((S, NH1, 2), f32)
    alibi[:, :, 0] = slopes
    alibi[:, :, 1] = -slopes * np.arange(S, dtype=f32)[:, None]
    logits = np.arange(Q_MIN, 1)
    table = np.stack([np.floor(np.exp(logits / float(Q_IN)) * 65536.0), logits]).astype(f32)

    arrays = {
        "x": a["x"],
        "mask_q": a["mask_1xSxS2_ff0"].reshape(S, SK),
        "mask_k": a["mask_BxS2_bf1"].view(np.uint8),
        "ctxT": ctxT.reshape(B, KC, P, SKP).transpose(0, 2, 1, 3).reshape(B, P, KC * SKP),
        "wq0": _grouped(np, a["L0_xattn_Wq"], G0),
        "wkv0": np.concatenate([_grouped(np, a["L0_xattn_Wk"], G0), _grouped(np, a["L0_xattn_Wv"], G0)], axis=3),
        "wo0": a["L0_xattn_Wo"].reshape(G0, HPG0, HD0, H).transpose(0, 2, 1, 3),
        "bias0": np.concatenate([a["L0_xattn_" + n].reshape(G0, -1) for n in ("bq", "bk", "bv")], axis=1),
        "qn": a["L0_xattn_qn_w"].reshape(HD0, 1),
        "kn": a["L0_xattn_kn_w"].reshape(HD0, 1),
        "wa": _sliced(np, a["L0_ffn_A"].reshape(AR, H).T, KC),
        "wb": _sliced(np, a["L0_ffn_B"].transpose(0, 2, 1).reshape(AR, H), AC),
        "ww": _sliced(np, a["L0_ffn_W"].T, KC),
        "bias_f": a["L0_ffn_bias"],
        "alibi": alibi,
        "wq1": _sliced(np, a["L1_xattn_Wq"], KC),
        "wkv1": _sliced(np, np.concatenate([a["L1_xattn_Wk"], a["L1_xattn_Wv"]], axis=1), KC),
        "wo1": wo1.transpose(0, 2, 3, 1, 4).reshape(P, HPG1, H),
        "wg": _sliced(np, a["L1_ffn_w_gate"].T, KC),
        "w13": w13.reshape(NE, 2, KC, P, IT * P).transpose(0, 3, 1, 2, 4),
        "w2": w2T.reshape(NE, IT, P, H).transpose(0, 2, 1, 3),
        "table": table,
    }
    nc = _bacc.Bacc("TRN2", target_bir_lowering=False, num_devices=1)
    feeds, args = {}, {}
    for name, array in arrays.items():
        array = np.ascontiguousarray(array)
        feeds[f"in_{name}"] = array
        args[name] = nc.dram_tensor(f"in_{name}", array.shape, _mybir.dt.from_np(array.dtype), kind="ExternalInput").ap()
    args["out"] = nc.dram_tensor("out_0", (B, S, H), F32, kind="ExternalOutput").ap()
    network(nc, **args)
    return _run(nc, [feeds], core_ids=[0]).results[0]["out_0"]
```

```python
from contextlib import ExitStack

import concourse.bass as bass
from concourse import mybir

ALU = mybir.AluOpType
ACT = mybir.ActivationFunctionType
AX = mybir.AxisListType
F32 = mybir.dt.float32
F32R = mybir.dt.float32r

P = 128
B, S, H = 8, 256, 256
KC = H // P
QT = S // P
SK = 1601
KT = -(-SK // P)
SKP = KT * P
CHUNKS = 4
CW = 402
SKC = CHUNKS * CW
BANK = 512
NEG = -1.0e30
KGROUPS = [range(0, 4), range(4, 7), range(7, 10), range(10, 13)]
HD0, G0, HPG0 = 128, 4, 4
EPS_RMS, EPS_LN = 1e-6, 1e-5


class Ring:

    def __init__(self, steps, kinds, size):
        self.size = size
        lists = ([s for s in steps if s[-1]], steps, [s for s in steps if not s[-1]])
        self.at = [{s: i for i, s in enumerate(s for s in part if s[0] in kinds)} for part in lists]

    def uses(self, part, bank):
        return len(range(bank, len(self.at[part]), self.size))

    def bank(self, part, step):
        return self.at[part][step] % self.size

    def tenants(self, part, b, step):
        i = self.at[part][step]
        bank, n = i % self.size, i // self.size
        return n if part == 0 else self.uses(0, bank) + b * self.uses(1, bank) + n

    def last(self, part, steps):
        return {self.bank(part, s): s for s in sorted(steps, key=self.at[part].get)}.values()

    def before(self, part, b, step=None):
        n = 0 if step is None else self.at[part][step]
        return n if part == 0 else len(self.at[0]) + b * len(self.at[1]) + n


def stand(eng, passed):
    eng.sem_inc(passed, 1)


def with_negated(steps):
    out, waiting = [], []
    for s in steps:
        out.append(s)
        if s[0] == "max":
            waiting.append(("neg", *s[1:]))
        if waiting and (s[0] == "turn" or s[0] == "max" and s[1] < 2 and s[3]):
            out.append(waiting.pop())
    assert not waiting
    return out


def first_plan():
    tiles, per = G0 * HPG0 * QT, HPG0 * QT
    slots = [[] for _ in range(tiles + 2)]
    for g in range(G0):
        nxt, to = divmod(g + 1, G0)
        at = g * per
        kv = [("kv", to, i, nxt) for i in range(7)]
        qp = [("qp", to, i, nxt) for i in range(QT)]
        slots[at + 1 if g == 0 else at - 1] += qp + [("qstat", to, 0, nxt)]
        slots[at + 1] += kv[:3]
        slots[at + 3] += kv[3:] + [("kstat", to, 0, nxt), ("vh", to, 0, nxt)]
        slots[at + 5] += [("qt", to, i, nxt) for i in range(QT)] + [("kt", to, i, nxt) for i in range(4)]
        slots[at + per + 1].insert(0, ("wo", g, 0, 0))
    slots[tiles - per - 2] += [("ln", 0, 0, 1), ("xt", 0, 0, 1)]
    slots[tiles - per - 1].insert(0, ("ctx", 0, 0, 1))
    slots[tiles - per] += [("ctx", 0, 1, 1)]

    first = {tiles - 2: 0, tiles: 1, tiles + 1: 2}
    steps = []
    for t in range(tiles + 2):
        pair = t // 2 - 1
        early, late = [], slots[t]
        if t < tiles:
            early = [w for w in late if w[0] in ("wo", "kv", "qp", "qt", "kt")][:7]
            late = [w for w in late if w not in early]
        if t % 2 == 0 and pair >= 0:
            steps.append(("rinv", pair, 0, 0))
        if t + 1 < tiles:
            steps.append(("exp", t + 1, 0, 0))
        if t + 2 < tiles:
            steps.append(("max", t + 2, 0, 0))
        elif tiles - 1 <= t <= tiles:
            steps.append(("max", t - tiles + 1, 0, 1))
        if t == tiles:
            steps.append(("exp", 0, 0, 1))
        if t % 2 == 0 and pair >= 0:
            steps += [("pv", pair, j, 0) for j in range(4)] + [("row", pair, 0, 0)]
        steps += early
        scores = []
        if t + 3 < tiles:
            scores = [("scores", t + 3, j, 0) for j in range(2)]
        elif t in first:
            scores = [("scores", first[t], j, 1) for j in range(2)]
        if t < tiles:
            steps += [("turn", t, j, 0) for j in range(3)] + scores[:1] + [("turn", t, 3, 0)] + scores[1:]
        else:
            steps += scores
        if t % 2 == 0 and pair >= 0:
            steps += [("norm", pair, 0, 0)]
        steps += late
    return with_negated(steps)


def first_attention(nc, x, out, ctxT, mask, wq, wkv, wo, bias, qn, kn):
    steps = first_plan()
    TURN_BANKS, PROBS = 3, 3
    ring = Ring(steps, ("xt", "kv", "qp", "kt", "qt", "turn", "row", "wo"), TURN_BANKS)
    highs = Ring(steps, ("kt", "qt", "turn"), 1)
    TILES, PAIRS = G0 * HPG0 * QT, G0 * HPG0
    assert wq.shape[0] == G0
    C = 1

    with ExitStack() as ctx:
        def sb(name, shape, dt=F32):
            return ctx.enter_context(nc.sbuf_tensor("a0_" + name, shape, dt))

        def sem(name):
            return ctx.enter_context(nc.semaphore("a0_" + name))

        ctx_hi, ctx_lo = (sb(n, [P, KC, SKP], F32R) for n in ("ctx_hi", "ctx_lo"))
        wkv_raw = sb("wkv_raw", [P, KC, 2 * HD0])
        wkv_hi, wkv_lo = (sb(n, [P, KC, 2 * HD0], F32R) for n in ("wkv_hi", "wkv_lo"))
        wq_g = sb("wq_g", [P, KC, HPG0 * HD0])
        wo_g = sb("wo_g", [P, HPG0, H])
        bias_g = sb("bias_g", [P, HPG0 * HD0 + 2 * HD0])
        maskt = sb("mask", [P, QT, SKC])
        k_hi, k_lo = ([sb(f"{n}{i}", [P, SKP], F32R) for i in range(2)] for n in ("k_hi", "k_lo"))
        v_hi, v_lo = ([sb(f"{n}{i}", [P, KT, HD0], F32R) for i in range(2)] for n in ("v_hi", "v_lo"))
        q_hi, q_lo = ([sb(f"{n}{i}", [P, HPG0, S], F32R) for i in range(2)] for n in ("q_hi", "q_lo"))
        prob = [sb(f"prob{i}", [P, SKP]) for i in range(PROBS)]
        pt_hi, pt_lo = (sb(n, [P, KT, S], F32R) for n in ("pt_hi", "pt_lo"))
        kv_raw = sb("kv_raw", [P, KT, 2 * HD0])
        square = sb("square", [P, KT * HD0])
        q_raw = sb("q_raw", [P, QT, HPG0 * HD0])
        heads = sb("heads", [P, HPG0, S])
        x_in = sb("x_in", [P, QT, H])
        x_out = sb("x_out", [P, QT, H])
        xT = sb("xT", [P, KC, S])
        rows = sb("rows", [P, S])
        ident = sb("ident", [P, P])
        qn_s, kn_s = sb("qn_s", [P, 1]), sb("kn_s", [P, 1])
        half = sb("half", [P, 16])
        top = sb("top", [P, 4, 2])
        negmax = sb("negmax", [P, 4])
        total = sb("total", [P, 4])
        inv = sb("inv", [P, 2, 2])
        kvar, krstd = sb("kvar", [P, KT]), sb("krstd", [P, KT])
        qvar, qrstd = sb("qvar", [P, QT * HPG0]), sb("qrstd", [P, QT * HPG0])
        ln6, ln2, lnr = sb("ln6", [P, QT, 6]), sb("ln2", [P, QT, 2]), sb("lnr", [P, QT])

        ps_s = ctx.enter_context(nc.psum_tensor("a0_ps_s", [P, CHUNKS, BANK], F32))
        ps_t = ctx.enter_context(nc.psum_tensor("a0_ps_t", [P, TURN_BANKS, BANK], F32))
        ps_o = ctx.enter_context(nc.psum_tensor("a0_ps_o", [P, BANK], F32))

        (const_in, mask_in, const_set, const_ok, qn_scaled, ctx_in, x_in_s, wkv_in, wq_in, wo_in, ctx_high, ctx_split,
         wkv_high, wkv_split, ln_step, ln_var, ln_rstd, x_norm, bank_full, scores_full, scored, negmax_ok, exp_ok,
         high_ok, pv_done, taken, inv_ok, k_square, k_sum, k_var, k_rstd, k_norm, q_square, q_sum, q_var,
         q_rstd, q_norm, v_high, v_split, x_done, x_stored, dve_passed, pool_passed, sp_passed) = (
            sem(n) for n in ("const_in", "mask_in", "const_set", "const_ok", "qn_scaled", "ctx_in", "x_in_s", "wkv_in", "wq_in",
                             "wo_in", "ctx_high", "ctx_split", "wkv_high", "wkv_split", "ln_step", "ln_var",
                             "ln_rstd", "x_norm", "bank_full", "scores_full", "scored", "negmax_ok", "exp_ok",
                             "high_ok", "pv_done", "taken", "inv_ok", "k_square", "k_sum", "k_var",
                             "k_rstd", "k_norm", "q_square", "q_sum", "q_var", "q_rstd", "q_norm", "v_high",
                             "v_split", "x_done", "x_stored", "dve_passed", "pool_passed", "sp_passed"))
        bank_free = [sem(f"bank_free{i}") for i in range(TURN_BANKS)]

        def f(ap):
            return ap.bitcast(F32)

        def is_free(eng, part, b, step, done):
            bank = ring.bank(part, step)
            eng.wait_ge(bank_free[bank], ring.tenants(part, b, step) + done + C)
            return ps_t[:, bank, :]

        def is_full(eng, part, b, step):
            eng.wait_ge(bank_full, ring.before(part, b, step) + 1 + C)
            return ps_t[:, ring.bank(part, step), :]

        def all_full(eng, part, b):
            eng.wait_ge(bank_full, ring.before(part, b) + C)

        def batches(eng, body):
            body(0, -1, [s for s in steps if s[-1]])
            if B > 1:
                with eng.Fori(0, B - 1) as b:
                    body(1, b, steps)
            body(2, B - 1, [s for s in steps if not s[-1]])

        def groups(part):
            return [(g, 0) for g in range(1, G0) if part] + [(0, 1)] * (part < 2)

        block = ctx.enter_context(nc.Block())

        @block.sync
        def _(sp):
            sp.sem_inc(x_stored, C)
            with nc.allow_non_contiguous_dma("one number a partition"):
                sp.dma_start(qn_s[:, :], qn).then_inc(const_in, 16)
                sp.dma_start(kn_s[:, :], kn).then_inc(const_in, 16)

            def batch(part, b, _):
                def output_weights(n):
                    if n == 0:
                        all_full(sp, part, b)
                    else:
                        is_full(sp, part, b, ("wo", n - 1, 0, 0))
                    sp.dma_start(wo_g[:, :, :], wo[n]).then_inc(wo_in, 16)

                for g, nxt in groups(part):
                    n = (b + nxt) * G0 + g
                    sp.wait_ge(wkv_split, n + C)
                    sp.dma_start(wkv_raw[:, :, :], wkv[g]).then_inc(wkv_in, 16)
                    if part:
                        if g == 1:
                            sp.wait_ge(k_sum, n + C)
                        else:
                            before = (g - 1) % G0
                            is_free(sp, part, b, ("kv", before, 6, 0), 1)
                    sp.dma_start(wq_g[:, :, :], wq[g]).then_inc(wq_in, 16)
                    sp.dma_start(bias_g[:, :], bias[g].partition_broadcast(P)).then_inc(wq_in, 16)
                    if g:
                        stand(sp, sp_passed)
                        output_weights(g - 1)
                if part < 2:
                    if part:
                        is_free(sp, part, b, ("wo", 0, 0, 0), 1)
                        stand(sp, sp_passed)
                    sp.dma_start(x_in[:, :, :], x[b + 1].rearrange("(t p) h -> p t h", p=P)).then_inc(x_in_s, 16)
                    if part:
                        is_full(sp, part, b, ("kt", G0 - 1, 3, 0))
                        stand(sp, sp_passed)
                        sp.wait_ge(v_split, (b + 1) * G0 + C)
                        stand(sp, sp_passed)
                    sp.dma_start(kv_raw[:, :, :].rearrange("p k d -> p (k d)"), ctxT[b + 1]).then_inc(ctx_in, 16)
                if part == 0:
                    sp.wait_ge(const_set, 1)
                    sp.dma_start(maskt[:, :, 0:SK], mask.rearrange("(t p) k -> p t k", p=P)).then_inc(mask_in, 16)
                if part:
                    output_weights(G0 - 1)
                    sp.wait_ge(x_done, b + 1)
                    stand(sp, sp_passed)
                    sp.dma_start(out[b].rearrange("(t p) h -> p t h", p=P), x_out[:, :, :]).then_inc(x_stored, 16)

            batches(sp, batch)
            sp.wait_ge(x_stored, 16 * B + C)

        @block.gpsimd
        def _(pool):
            for s in (wkv_split, v_split):
                pool.sem_inc(s, C)
            nc.gpsimd.memset(maskt[:, :, :], NEG).then_inc(const_set, 1)
            nc.gpsimd.memset(half[:, :], -0.5).then_inc(const_ok, 1)
            for t in prob:
                nc.gpsimd.memset(t[:, SKC:], 0.0).then_inc(const_ok, 1)
            nc.gpsimd.memset(ident[:, :], 0.0).then_inc(const_set, 1)
            pool.wait_ge(const_set, 2)
            nc.gpsimd.affine_select(out=ident[:, :], in_=ident[:, :], compare_op=ALU.not_equal, fill=1.0, base=0,
                                    pattern=[[-1, P]], channel_multiplier=1).then_inc(const_ok, 1)
            pool.wait_ge(const_ok, 2 + PROBS)

            def batch(part, b, _):
                for g, nxt in groups(part):
                    n = (b + nxt) * G0 + g
                    pool.wait_ge(wkv_in, n * 16 + 16)
                    if g == 1:
                        all_full(pool, part, b)
                    elif part:
                        is_full(pool, part, b, ("kv", (g - 1) % G0, 6, 0))
                    stand(pool, pool_passed)
                    nc.gpsimd.tensor_scalar(wkv_hi[:, :, :], wkv_raw[:, :, :], 1.0, None, ALU.mult).then_inc(wkv_high, 1)
                    pool.wait_ge(wkv_high, n + 1)
                    nc.gpsimd.tensor_tensor(wkv_lo[:, :, :], wkv_raw[:, :, :], f(wkv_hi[:, :, :]),
                                            ALU.subtract).then_inc(wkv_split, 1)
                    if g == 0:
                        pool.wait_ge(ln_var, (b + 1) * QT + QT)
                        nc.gpsimd.tensor_tensor(lnr[:, :], ln2[:, :, 1], half[:, 0:QT], ALU.pow).then_inc(ln_rstd, 1)
                    is_free(pool, part, b, ("qp", g, 1, nxt), 1)
                    pool.wait_ge(k_sum, n + C)
                    q3 = q_raw[:, :, :].rearrange("p t (h d) -> p (t h) d", d=HD0)
                    nc.gpsimd.tensor_tensor(square[:, 0:QT * HPG0 * HD0].rearrange("p (k d) -> p k d", d=HD0), q3, q3,
                                            ALU.mult).then_inc(q_square, 1)
                    pool.wait_ge(q_var, n + 1)
                    nc.gpsimd.tensor_tensor(qrstd[:, :], qvar[:, :], half[:, 0:QT * HPG0], ALU.pow).then_inc(q_rstd, 1)
                    pool.wait_ge(q_rstd, n + 1)
                    nc.gpsimd.tensor_tensor(q3, q3, qrstd[:, :].unsqueeze(2).to_broadcast([P, QT * HPG0, HD0]),
                                            ALU.mult).then_inc(q_norm, 1)
                    is_free(pool, part, b, ("kv", g, 6, nxt), 1)
                    k3 = kv_raw[:, :, 0:HD0]
                    nc.gpsimd.tensor_tensor(square[:, :].rearrange("p (k d) -> p k d", d=HD0), k3, k3,
                                            ALU.mult).then_inc(k_square, 1)
                    pool.wait_ge(k_var, n + 1)
                    nc.gpsimd.tensor_tensor(krstd[:, :], kvar[:, :], half[:, 0:KT], ALU.pow).then_inc(k_rstd, 1)
                    pool.wait_ge(k_rstd, n + 1)
                    nc.gpsimd.tensor_tensor(k3, k3, krstd[:, :].unsqueeze(2).to_broadcast([P, KT, HD0]),
                                            ALU.mult).then_inc(k_norm, 1)
                    pool.wait_ge(v_high, n + 1)
                    nc.gpsimd.tensor_tensor(v_lo[g % 2][:, :, :], kv_raw[:, :, HD0:], f(v_hi[g % 2][:, :, :]),
                                            ALU.subtract).then_inc(v_split, 1)

            batches(pool, batch)

        @block.tensor
        def _(pe):
            for s in (bank_full, pv_done):
                pe.sem_inc(s, C)
            pe.wait_ge(const_ok, 2 + PROBS)

            def split_mm(to, lhs, rhs, first=True, last=True):
                (lh, ll), (rh, rl) = lhs, rhs
                nc.tensor.matmul(to, lh, rh, start=first, stop=False)
                nc.tensor.matmul(to, ll, rh, start=False, stop=False)
                return nc.tensor.matmul(to, lh, rl, start=False, stop=last)

            def batch(part, b, order):
                for step in order:
                    kind, n, j, nxt = step
                    nb = b + nxt
                    if kind in ("xt", "kv", "qp", "kt", "qt", "turn", "row", "wo"):
                        ps = is_free(pe, part, b, step, 0)
                    if kind == "xt":
                        pe.wait_ge(x_norm, nb * QT + QT)
                        for c in range(KC):
                            for q in range(QT):
                                mm = nc.tensor.transpose(ps[:, c * S + q * P:c * S + (q + 1) * P],
                                                         q_raw[:, q, c * P:(c + 1) * P], ident[:, :])
                        mm.then_inc(bank_full, 1)
                    elif kind == "kv":
                        if j == 0:
                            pe.wait_ge(wkv_split, nb * G0 + n + 1 + C)
                            if n == 0:
                                pe.wait_ge(ctx_split, nb * KC + KC)
                        for i in range(min(2, KT - 2 * j)):
                            k = slice((2 * j + i) * P, (2 * j + i + 1) * P)
                            for c in range(KC):
                                mm = split_mm(ps[:, i * 2 * HD0:(i + 1) * 2 * HD0], (ctx_hi[:, c, k], ctx_lo[:, c, k]),
                                              (wkv_hi[:, c, :], wkv_lo[:, c, :]), c == 0, c == KC - 1)
                        mm.then_inc(bank_full, 1)
                    elif kind == "qp":
                        if n == 0:
                            is_free(pe, part, b, ("xt", 0, 0, nxt), 1)
                        pe.wait_ge(wq_in, (nb * G0 + n) * 32 + 32)
                        for c in range(KC):
                            mm = nc.tensor.matmul(ps, xT[:, c, j * P:(j + 1) * P], wq_g[:, c, :],
                                                  start=c == 0, stop=c == KC - 1)
                        mm.then_inc(bank_full, 1)
                    elif kind == "kt":
                        pe.wait_ge(k_norm, nb * G0 + n + 1)
                        for i, k in enumerate(KGROUPS[j]):
                            mm = nc.tensor.transpose(ps[:, i * P:(i + 1) * P], kv_raw[:, k, 0:HD0], ident[:, :])
                        mm.then_inc(bank_full, 1)
                    elif kind == "qt":
                        pe.wait_ge(q_norm, nb * G0 + n + 1)
                        for i in range(HPG0):
                            mm = nc.tensor.transpose(ps[:, i * P:(i + 1) * P], q_raw[:, j, i * HD0:(i + 1) * HD0],
                                                     ident[:, :])
                        mm.then_inc(bank_full, 1)
                    elif kind == "scores":
                        g, at = divmod(n, HPG0 * QT)
                        head, q = divmod(at, QT)
                        if at == 0 and j == 0:
                            turned = [("kt", g, i, nxt) for i in range(4)] + [("qt", g, i, nxt) for i in range(QT)]
                            for s in ring.last(part, turned):
                                is_free(pe, part, b, s, 1)
                        q = slice(q * P, (q + 1) * P)
                        pe.wait_ge(scored, (nb * TILES + n) * 2 + j + C)
                        for c in (2 * j, 2 * j + 1):
                            k = slice(c * CW, (c + 1) * CW)
                            mm = split_mm(ps_s[:, c, 0:CW], (q_hi[g % 2][:, head, q], q_lo[g % 2][:, head, q]),
                                          (k_hi[g % 2][:, k], k_lo[g % 2][:, k]))
                        mm.then_inc(scores_full, 1)
                    elif kind == "turn":
                        pe.wait_ge(exp_ok, b * TILES + n + 1)
                        for i, k in enumerate(KGROUPS[j]):
                            mm = nc.tensor.transpose(ps[:, i * P:(i + 1) * P], prob[n % PROBS][:, k * P:(k + 1) * P],
                                                     ident[:, :])
                        mm.then_inc(bank_full, 1)
                    elif kind == "pv":
                        g = n // HPG0
                        if j == 0:
                            pe.wait_ge(taken, b * PAIRS + n + C)
                            if n % HPG0 == 0:
                                pe.wait_ge(v_split, b * G0 + g + 1 + C)
                        is_free(pe, part, b, ("turn", 2 * n + 1, j, 0), 1)
                        for k in KGROUPS[j]:
                            mm = split_mm(ps_o[:, 0:S], (v_hi[g % 2][:, k, :], v_lo[g % 2][:, k, :]),
                                          (pt_hi[:, k, :], pt_lo[:, k, :]), k == 0, k == KT - 1)
                        mm.then_inc(pv_done, 1)
                    elif kind == "row":
                        pe.wait_ge(inv_ok, b * PAIRS + n + 1)
                        for q in range(QT):
                            mm = nc.tensor.matmul(ps[:, q * P:(q + 1) * P],
                                                  inv[:, n % 2, q:q + 1].to_broadcast([P, P]), ident[:, :],
                                                  start=True, stop=True)
                        mm.then_inc(bank_full, 1)
                    elif kind == "wo":
                        pe.wait_ge(taken, b * PAIRS + (n + 1) * HPG0 + C)
                        pe.wait_ge(wo_in, (b * G0 + n) * 16 + 16)
                        for q in range(QT):
                            for i in range(HPG0):
                                mm = nc.tensor.matmul(ps[:, q * H:(q + 1) * H], heads[:, i, q * P:(q + 1) * P],
                                                      wo_g[:, i, :], start=i == 0, stop=i == HPG0 - 1)
                        mm.then_inc(bank_full, 1)

            batches(pe, batch)

        @block.scalar
        def _(act):
            def batch(part, b, order):
                for step in order:
                    kind, n, j, nxt = step
                    nb = b + nxt
                    if kind == "ctx":
                        act.wait_ge(ctx_in, nb * 16 + 16)
                        if part:
                            is_full(act, part, b, ("kv", G0 - 1, 6, 0))
                        nc.scalar.copy(ctx_hi[:, j, :], kv_raw[:, :, :].rearrange("p k d -> p (k d)")[
                            :, j * SKP:(j + 1) * SKP]).then_inc(ctx_high, 1)
                    elif kind == "vh":
                        is_free(act, part, b, ("kv", n, 6, nxt), 1)
                        if part:
                            act.wait_ge(pv_done, nb * PAIRS * 4 + (n - 1) * HPG0 * 4 + C)
                        nc.scalar.copy(v_hi[n % 2][:, :, :], kv_raw[:, :, HD0:]).then_inc(v_high, 1)
                    elif kind in ("kt", "qt", "turn"):
                        ps = is_full(act, part, b, step)
                        w = len(KGROUPS[j])
                        k0 = KGROUPS[j][0]
                        if kind != "turn" and part:
                            act.wait_ge(scored, (nb * TILES + (n - 1) * HPG0 * QT) * 2 + C + 1)
                        if kind == "kt":
                            if part == 0:
                                act.wait_ge(const_in, 32)
                            nc.scalar.activation(k_hi[n % 2][:, k0 * P:(k0 + w) * P], ps[:, 0:w * P], ACT.Identity,
                                                 bias=0.0, scale=kn_s[:, :]).then_inc(high_ok, 1)
                        elif kind == "qt":
                            if part == 0:
                                act.wait_ge(qn_scaled, 1)
                            nc.scalar.activation(q_hi[n % 2][:, :, j * P:(j + 1) * P],
                                                 ps.rearrange("p (h s) -> p h s", h=HPG0), ACT.Identity, bias=0.0,
                                                 scale=qn_s[:, :]).then_inc(high_ok, 1)
                        else:
                            pair, q = divmod(n, QT)
                            if q == 0:
                                act.wait_ge(pv_done, (b * PAIRS + pair - 1) * 4 + j + 1 + C if pair
                                            else b * PAIRS * 4 + C)
                            nc.scalar.copy(pt_hi[:, k0:k0 + w, q * P:(q + 1) * P],
                                           ps[:, 0:w * P].rearrange("p (k s) -> p k s", k=w)).then_inc(high_ok, 1)
                    elif kind == "exp":
                        act.wait_ge(negmax_ok, nb * TILES + n + 1)
                        nc.scalar.activation(prob[n % PROBS][:, 0:SKC], prob[n % PROBS][:, 0:SKC], ACT.Exp,
                                             bias=negmax[:, n % 4:n % 4 + 1], scale=1.0,
                                             accum_out=total[:, n % 4:n % 4 + 1]).then_inc(exp_ok, 1)
                    elif kind == "row":
                        ps = is_full(act, part, b, step)
                        act.wait_ge(taken, b * PAIRS + n + C)
                        nc.scalar.copy(rows[:, :], ps[:, 0:S]).then_inc(bank_free[ring.bank(part, step)], 1)

            batches(act, batch)

        @block.vector
        def _(dve):
            for s in (*bank_free, k_sum, taken):
                dve.sem_inc(s, C)
            dve.sem_inc(scored, C + 1)
            dve.wait_ge(const_in, 32)
            nc.vector.tensor_scalar(qn_s[:, :], qn_s[:, :], float(HD0) ** -0.5, None, ALU.mult).then_inc(qn_scaled, 1)
            dve.wait_ge(qn_scaled, 1)

            def batch(part, b, order):
                for step in order:
                    kind, n, j, nxt = step
                    nb = b + nxt
                    free = bank_free[ring.bank(part, step)] if step in ring.at[part] else None
                    if kind == "ln":
                        dve.wait_ge(x_in_s, nb * 16 + 16)
                        for q in range(QT):
                            nc.vector.bn_stats(ln6[:, q, :], x_in[:, q, :]).then_inc(ln_step, 1)
                            dve.wait_ge(ln_step, (nb * QT + q) * 2 + 1)
                            stand(dve, dve_passed)
                            nc.vector.bn_aggr(ln2[:, q, :], ln6[:, q, :]).then_inc(ln_step, 1)
                            dve.wait_ge(ln_step, (nb * QT + q) * 2 + 2)
                            nc.vector.tensor_scalar(ln2[:, q, 1:2], ln2[:, q, 1:2], EPS_LN, None,
                                                    ALU.add).then_inc(ln_var, 1)
                        dve.wait_ge(ln_rstd, nb + 1)
                        if part:
                            is_full(dve, part, b, ("qt", G0 - 1, 1, 0))
                        for q in range(QT):
                            nc.vector.tensor_scalar(q_raw[:, q, 0:H], x_in[:, q, :], ln2[:, q, 0:1], lnr[:, q:q + 1],
                                                    ALU.subtract, ALU.mult).then_inc(x_norm, 1)
                    elif kind == "ctx":
                        dve.wait_ge(ctx_high, nb * KC + j + 1)
                        nc.vector.tensor_tensor(ctx_lo[:, j, :], kv_raw[:, :, :].rearrange("p k d -> p (k d)")[
                            :, j * SKP:(j + 1) * SKP], f(ctx_hi[:, j, :]), ALU.subtract).then_inc(ctx_split, 1)
                    elif kind == "xt":
                        ps = is_full(dve, part, b, step)
                        nc.vector.tensor_copy(xT[:, :, :].rearrange("p c s -> p (c s)"), ps).then_inc(free, 1)
                    elif kind == "kv":
                        ps = is_full(dve, part, b, step)
                        if j == 0:
                            dve.wait_ge(wq_in, (nb * G0 + n) * 32 + 32)
                            dve.wait_ge(v_split, nb * G0 + n + C)
                            if n == 0:
                                dve.wait_ge(ctx_split, nb * KC + KC)
                        w = min(2, KT - 2 * j)
                        nc.vector.tensor_tensor(kv_raw[:, 2 * j:2 * j + w, :],
                                                ps[:, 0:w * 2 * HD0].rearrange("p (k d) -> p k d", k=w),
                                                bias_g[:, HPG0 * HD0:].unsqueeze(1).to_broadcast([P, w, 2 * HD0]),
                                                ALU.add).then_inc(free, 1)
                    elif kind == "qp":
                        ps = is_full(dve, part, b, step)
                        nc.vector.tensor_tensor(q_raw[:, j, :], ps, bias_g[:, 0:HPG0 * HD0],
                                                ALU.add).then_inc(free, 1)
                    elif kind == "kstat":
                        dve.wait_ge(k_square, nb * G0 + n + 1)
                        nc.vector.tensor_reduce(kvar[:, :], square[:, :].rearrange("p (k d) -> p k d", d=HD0), AX.X,
                                                ALU.add).then_inc(k_sum, 1)
                        dve.wait_ge(k_sum, nb * G0 + n + 1 + C)
                        nc.vector.tensor_scalar(kvar[:, :], kvar[:, :], 1.0 / HD0, EPS_RMS, ALU.mult,
                                                ALU.add).then_inc(k_var, 1)
                    elif kind == "qstat":
                        dve.wait_ge(q_square, nb * G0 + n + 1)
                        nc.vector.tensor_reduce(qvar[:, :], square[:, 0:QT * HPG0 * HD0].rearrange(
                            "p (k d) -> p k d", d=HD0), AX.X, ALU.add).then_inc(q_sum, 1)
                        dve.wait_ge(q_sum, nb * G0 + n + 1)
                        nc.vector.tensor_scalar(qvar[:, :], qvar[:, :], 1.0 / HD0, EPS_RMS, ALU.mult,
                                                ALU.add).then_inc(q_var, 1)
                    elif kind in ("kt", "qt", "turn"):
                        ps = ps_t[:, ring.bank(part, step), :]
                        dve.wait_ge(high_ok, highs.before(part, b, step) + 1)
                        w, k0 = len(KGROUPS[j]), KGROUPS[j][0]
                        if kind == "kt":
                            k = slice(k0 * P, (k0 + w) * P)
                            nc.vector.scalar_tensor_tensor(k_lo[n % 2][:, k], ps[:, 0:w * P], kn_s[:, :],
                                                           f(k_hi[n % 2][:, k]), ALU.mult,
                                                           ALU.subtract).then_inc(free, 1)
                        elif kind == "qt":
                            q = slice(j * P, (j + 1) * P)
                            nc.vector.scalar_tensor_tensor(q_lo[n % 2][:, :, q], ps.rearrange("p (h s) -> p h s", h=HPG0),
                                                           qn_s[:, :], f(q_hi[n % 2][:, :, q]), ALU.mult,
                                                           ALU.subtract).then_inc(free, 1)
                        else:
                            q = slice(n % QT * P, (n % QT + 1) * P)
                            nc.vector.tensor_tensor(pt_lo[:, k0:k0 + w, q],
                                                    ps[:, 0:w * P].rearrange("p (k s) -> p k s", k=w),
                                                    f(pt_hi[:, k0:k0 + w, q]), ALU.subtract).then_inc(free, 1)
                    elif kind == "max":
                        if n >= PROBS:
                            is_full(dve, part, b, ("turn", n - PROBS, 3, 0))
                        elif nxt and part:
                            is_full(dve, part, b, ("turn", TILES - 2 + n, 3, 0))
                        else:
                            all_full(dve, part, b)
                        if part == 0 and n == 0:
                            dve.wait_ge(mask_in, 16)
                        for c in range(2):
                            dve.wait_ge(scores_full, (nb * TILES + n) * 2 + c + 1)
                            stand(dve, dve_passed)
                            k = slice(2 * c * CW, (2 * c + 2) * CW)
                            nc.vector.tensor_tensor_reduce(
                                prob[n % PROBS][:, k].rearrange("p (c k) -> p c k", c=2), ps_s[:, 2 * c:2 * c + 2, 0:CW],
                                maskt[:, n % QT, k].rearrange("p (c k) -> p c k", c=2), 1.0, -3.4e38, ALU.add,
                                ALU.max, top[:, n % 4, c:c + 1]).then_inc(scored, 1)
                    elif kind == "neg":
                        dve.wait_ge(scored, (nb * TILES + n) * 2 + 3 + C)
                        nc.vector.tensor_reduce(negmax[:, n % 4:n % 4 + 1], top[:, n % 4, :], AX.X, ALU.max,
                                                negate=True).then_inc(negmax_ok, 1)
                    elif kind == "rinv":
                        dve.wait_ge(exp_ok, b * TILES + 2 * n + 2)
                        if n >= 2:
                            is_full(dve, part, b, ("row", n - 2, 0, 0))
                        else:
                            all_full(dve, part, b)
                        nc.vector.reciprocal(inv[:, n % 2, :], total[:, 2 * n % 4:2 * n % 4 + 2]).then_inc(inv_ok, 1)
                    elif kind == "norm":
                        dve.wait_ge(pv_done, (b * PAIRS + n) * 4 + 4 + C)
                        if n % HPG0 == 0:
                            if n:
                                is_full(dve, part, b, ("wo", n // HPG0 - 1, 0, 0))
                            else:
                                all_full(dve, part, b)
                        is_free(dve, part, b, ("row", n, 0, 0), 1)
                        nc.vector.tensor_tensor(heads[:, n % HPG0, :], ps_o[:, 0:S], rows[:, :],
                                                ALU.mult).then_inc(taken, 1)
                    elif kind == "wo":
                        ps = is_full(dve, part, b, step)
                        if n == 0:
                            dve.wait_ge(x_stored, b * 16 + C)
                        else:
                            is_free(dve, part, b, ("wo", n - 1, 0, 0), 1)
                        y = ps.rearrange("p (t h) -> p t h", t=QT)
                        nc.vector.tensor_tensor(x_out[:, :, :], y, (x_out if n else x_in)[:, :, :],
                                                ALU.add).then_inc(free, 1)
                        if n == G0 - 1:
                            is_free(dve, part, b, step, 1)
                            dve.sem_inc(x_done, 1)

            batches(dve, batch)


NA, R, TOPK = 64, 16, 4
AR = NA * R
AC = AR // P


def first_ffn(nc, x, out, wa, wb, ww, bias):
    TILES = B * S // P
    PER = 8
    C, CC = 1, 2
    ORDER = [(kind, (s + ahead) % PER, (s + ahead) // PER) for s in range(PER)
             for kind, ahead in (("stat", 3), ("zt", 0), ("norm", 3), ("a", 2), ("pick", 1), ("wb", 0), ("xt", 3),
                                 ("sum", 0))]

    with ExitStack() as ctx:
        def sb(name, shape, dt=F32):
            return ctx.enter_context(nc.sbuf_tensor("f0_" + name, shape, dt))

        def sem(name):
            return ctx.enter_context(nc.semaphore("f0_" + name))

        wa_raw, wb_raw, ww_raw = sb("wa_raw", [P, KC, AR]), sb("wb_raw", [P, AC, H]), sb("ww_raw", [P, KC, H])
        wa_hi, wa_lo = (sb(n, [P, KC, AR], F32R) for n in ("wa_hi", "wa_lo"))
        wb_hi, wb_lo = (sb(n, [P, AC, H], F32R) for n in ("wb_hi", "wb_lo"))
        ww_hi, ww_lo = (sb(n, [P, KC, H], F32R) for n in ("ww_hi", "ww_lo"))
        bias_s = sb("bias", [P, H])
        ident, half = sb("ident", [P, P]), sb("half", [P, 1])
        ones = sb("ones", [P, NA])
        xs = sb("xs", [P, PER, H])
        xn = sb("xn", [P, 2, H])
        xT_hi, xT_lo = (sb(n, [P, PER, KC, P], F32R) for n in ("xT_hi", "xT_lo"))
        sq = sb("sq", [P, 2, AR])
        norms = sb("norms", [P, NA])
        m8 = sb("m8", [P, 8])
        above, equal, rank, keep = (sb(n, [P, NA]) for n in ("above", "equal", "rank", "keep"))
        nabove = sb("nabove", [P, 1])
        picked = sb("picked", [P, 2, NA])
        masked = sb("masked", [P, 2, AR])
        v = sb("v", [P, 2, R])
        z = sb("z", [P, 2, AR])
        zT_hi, zT_lo = (sb(n, [P, AC, P], F32R) for n in ("zT_hi", "zT_lo"))
        y = sb("y", [P, PER, H])
        ln6, ln2, rstd = sb("ln6", [P, 6]), sb("ln2", [P, 2, 2]), sb("rstd", [P, 2])

        ps_v = ctx.enter_context(nc.psum_tensor("f0_ps_v", [P, 2, 2 * BANK], F32))
        ps_z = ctx.enter_context(nc.psum_tensor("f0_ps_z", [P, 2, BANK], F32))
        ps_x = ctx.enter_context(nc.psum_tensor("f0_ps_x", [P, BANK], F32))
        ps_y = ctx.enter_context(nc.psum_tensor("f0_ps_y", [P, BANK], F32))

        (w_in, const_set, const_ok, w_high, w_split, var_ok, rstd_ok, x_norm, xt_full, xt_high, xt_low,
         v_full, squared, v_used, picked_ok, z_ok, zt_full, zt_high, zt_low, y_full, y_read, y_ok, stored) = (
            sem(n) for n in ("w_in", "const_set", "const_ok", "w_high", "w_split", "var_ok", "rstd_ok",
                             "x_norm", "xt_full", "xt_high", "xt_low", "v_full", "squared", "v_used", "picked_ok",
                             "z_ok", "zt_full", "zt_high", "zt_low", "y_full", "y_read", "y_ok", "stored"))

        dve_passed, sp_passed = sem("dve_passed"), sem("sp_passed")
        norm_link, pick_link = sem("norm_link"), sem("pick_link")
        x_in = [sem(f"x_in{n}") for n in range(PER)]

        def f(ap):
            return ap.bitcast(F32)

        def turns(eng, body):
            body(-1, [o for o in ORDER if o[2]])
            with eng.Fori(0, TILES // PER - 1) as i:
                body(i, ORDER)
            body(TILES // PER - 1, [o for o in ORDER if not o[2]])

        block = ctx.enter_context(nc.Block())

        @block.sync
        def _(sp):
            sp.sem_inc(stored, C)
            sp.dma_start(wa_raw[:, :, :], wa).then_inc(w_in, 16)
            sp.dma_start(wb_raw[:, :, :], wb).then_inc(w_in, 16)
            sp.dma_start(ww_raw[:, :, :], ww).then_inc(w_in, 16)
            sp.dma_start(bias_s[:, :], bias.partition_broadcast(P)).then_inc(w_in, 16)
            for n in range(PER):
                sp.dma_start(xs[:, n, :], x[n]).then_inc(x_in[n], 16)
            with sp.Fori(1, TILES // PER) as i:
                for n in range(PER):
                    sp.wait_ge(y_ok, (i - 1) * PER + n + 1)
                    stand(sp, sp_passed)
                    sp.dma_start(out[(i - 1) * PER + n], y[:, n, :]).then_inc(stored, 16)
                    sp.dma_start(xs[:, n, :], x[i * PER + n]).then_inc(x_in[n], 16)
            for n in range(PER):
                sp.wait_ge(y_ok, TILES - PER + n + 1)
                sp.dma_start(out[TILES - PER + n], y[:, n, :]).then_inc(stored, 16)
            sp.wait_ge(stored, 16 * TILES + C)

        @block.gpsimd
        def _(pool):
            nc.gpsimd.memset(half[:, :], -0.5).then_inc(const_ok, 1)
            nc.gpsimd.memset(ones[:, :], 1.0).then_inc(const_ok, 1)
            nc.gpsimd.memset(ident[:, :], 0.0).then_inc(const_set, 1)
            pool.wait_ge(const_set, 1)
            nc.gpsimd.affine_select(out=ident[:, :], in_=ident[:, :], compare_op=ALU.not_equal, fill=1.0, base=0,
                                    pattern=[[-1, P]], channel_multiplier=1).then_inc(const_ok, 1)
            pool.wait_ge(const_ok, 3)
            with pool.Fori(0, TILES // PER) as i:
                for n in range(PER):
                    pool.wait_ge(var_ok, i * PER + n + 1)
                    nc.gpsimd.tensor_tensor(rstd[:, n % 2:n % 2 + 1], ln2[:, n % 2, 1:2], half[:, :],
                                            ALU.pow).then_inc(rstd_ok, 1)

        @block.tensor
        def _(pe):
            pe.sem_inc(zt_full, 2 * CC)
            pe.sem_inc(xt_full, CC)
            pe.sem_inc(y_full, PER)
            pe.wait_ge(const_ok, 3)
            pe.wait_ge(w_split, 3)

            def turn(i, order):
                for kind, n, nxt in order:
                    p, t = n % 2, (i + nxt) * PER + n
                    if kind == "xt":
                        pe.wait_ge(x_norm, t + 1)
                        pe.wait_ge(xt_low, t + C)
                        for c in range(KC):
                            mm = nc.tensor.transpose(ps_x[:, c * P:(c + 1) * P], xn[:, p, c * P:(c + 1) * P], ident[:, :])
                        mm.then_inc(xt_full, 1)
                    elif kind == "a":
                        pe.wait_ge(xt_low, t + 1 + C)
                        pe.wait_ge(v_used, t - 1 + CC)
                        for q in range(2):
                            for c in range(KC):
                                for k, (l, r) in enumerate(((xT_hi, wa_hi), (xT_lo, wa_hi), (xT_hi, wa_lo))):
                                    mm = nc.tensor.matmul(ps_v[:, p, q * BANK:(q + 1) * BANK], l[:, n, c, :],
                                                          r[:, c, q * BANK:(q + 1) * BANK],
                                                          start=c == 0 and k == 0, stop=c == KC - 1 and k == 2)
                        mm.then_inc(v_full, 1)
                    elif kind == "zt":
                        pe.wait_ge(z_ok, t + 1)
                        for q in range(2):
                            pe.wait_ge(zt_low, t * 2 + q - 1 + CC)
                            for k in range(4):
                                mm = nc.tensor.transpose(ps_z[:, q, k * P:(k + 1) * P],
                                                         z[:, p, (4 * q + k) * P:(4 * q + k + 1) * P], ident[:, :])
                            mm.then_inc(zt_full, 1)
                    elif kind == "wb":
                        pe.wait_ge(y_read, t + C)
                        for c in range(KC):
                            for k, (l, r) in enumerate(((xT_hi, ww_hi), (xT_lo, ww_hi), (xT_hi, ww_lo))):
                                nc.tensor.matmul(ps_y[:, 0:H], l[:, n, c, :], r[:, c, :],
                                                 start=c == 0 and k == 0, stop=False)
                        for a in range(AC):
                            if a % 4 == 0:
                                pe.wait_ge(zt_low, t * 2 + a // 4 + 1 + CC)
                            for k, (l, r) in enumerate(((zT_hi, wb_hi), (zT_lo, wb_hi), (zT_hi, wb_lo))):
                                mm = nc.tensor.matmul(ps_y[:, 0:H], l[:, a, :], r[:, a, :], start=False,
                                                      stop=a == AC - 1 and k == 2)
                        mm.then_inc(y_full, 1)

            turns(pe, turn)

        @block.scalar
        def _(act):
            act.wait_ge(w_in, 64)
            for hi, raw in ((wa_hi, wa_raw), (wb_hi, wb_raw), (ww_hi, ww_raw)):
                nc.scalar.copy(hi[:, :, :], raw[:, :, :]).then_inc(w_high, 1)

            def turn(i, order):
                for kind, n, nxt in order:
                    p, t = n % 2, (i + nxt) * PER + n
                    if kind == "xt":
                        act.wait_ge(xt_full, t + 1 + CC)
                        act.wait_ge(y_full, t + 1)
                        nc.scalar.copy(xT_hi[:, n, :, :], ps_x[:, 0:H].rearrange("p (c s) -> p c s", c=KC)).then_inc(
                            xt_high, 1)
                    elif kind == "a":
                        act.wait_ge(v_full, t + 1)
                        nc.scalar.square(sq[:, p, :], ps_v[:, p, :]).then_inc(squared, 1)
                    elif kind == "zt":
                        act.wait_ge(y_full, t + PER)
                        for q in range(2):
                            act.wait_ge(zt_full, t * 2 + q + 1 + 2 * CC)
                            nc.scalar.copy(zT_hi[:, 4 * q:4 * q + 4, :], ps_z[:, q, :].rearrange(
                                "p (a s) -> p a s", a=4)).then_inc(zt_high, 1)

            turns(act, turn)

        @block.vector
        def _(dve):
            for s in (xt_low, y_read):
                dve.sem_inc(s, C)
            dve.sem_inc(v_used, CC)
            dve.sem_inc(zt_low, CC)
            for n, (lo, hi, raw) in enumerate(((wa_lo, wa_hi, wa_raw), (wb_lo, wb_hi, wb_raw), (ww_lo, ww_hi, ww_raw))):
                dve.wait_ge(w_high, n + 1)
                nc.vector.tensor_tensor(lo[:, :, :], raw[:, :, :], f(hi[:, :, :]), ALU.subtract).then_inc(w_split, 1)
            dve.wait_ge(w_in, 64)
            dve.wait_ge(const_ok, 3)

            NORM_LINKS, PICK_LINKS = 2, 9

            def turn(i, order):
                def link(ins, sem, n):
                    ins.then_inc(sem, 1)
                    dve.wait_ge(sem, n)

                for kind, n, nxt in order:
                    p, t = n % 2, (i + nxt) * PER + n
                    if kind == "stat":
                        dve.wait_ge(x_in[n], (i + nxt) * 16 + 16)
                        link(nc.vector.bn_stats(ln6[:, :], xs[:, n, :]), norm_link, t * NORM_LINKS + 1)
                        stand(dve, dve_passed)
                        link(nc.vector.bn_aggr(ln2[:, p, :], ln6[:, :]), norm_link, t * NORM_LINKS + 2)
                        nc.vector.tensor_scalar(ln2[:, p, 1:2], ln2[:, p, 1:2], EPS_LN, None, ALU.add).then_inc(var_ok, 1)
                    elif kind == "norm":
                        dve.wait_ge(rstd_ok, t + 1)
                        dve.wait_ge(xt_full, t - 1 + CC)
                        nc.vector.tensor_scalar(xn[:, p, :], xs[:, n, :], ln2[:, p, 0:1], rstd[:, p:p + 1],
                                                ALU.subtract, ALU.mult).then_inc(x_norm, 1)
                    elif kind == "xt":
                        dve.wait_ge(xt_high, t + 1)
                        nc.vector.tensor_tensor(xT_lo[:, n, :, :], ps_x[:, 0:H].rearrange("p (c s) -> p c s", c=KC),
                                                f(xT_hi[:, n, :, :]), ALU.subtract).then_inc(xt_low, 1)
                    elif kind == "pick":
                        at = t * PICK_LINKS
                        last = m8[:, TOPK - 1:TOPK]
                        dve.wait_ge(squared, t + 1)
                        link(nc.vector.tensor_reduce(norms[:, :], sq[:, p, :].rearrange("p (a r) -> p a r", r=R), AX.X,
                                                     ALU.add), pick_link, at + 1)
                        stand(dve, dve_passed)
                        link(nc.vector.max(m8[:, :], norms[:, :]), pick_link, at + 2)
                        link(nc.vector.tensor_scalar(above[:, :], norms[:, :], last, None, ALU.is_gt), pick_link, at + 3)
                        link(nc.vector.tensor_reduce(nabove[:, :], above[:, :], AX.X, ALU.add), pick_link, at + 4)
                        link(nc.vector.tensor_scalar(equal[:, :], norms[:, :], last, None, ALU.is_equal),
                             pick_link, at + 5)
                        link(nc.vector.tensor_tensor_scan(rank[:, :], ones[:, :], equal[:, :], nabove[:, 0:1],
                                                          ALU.mult, ALU.add), pick_link, at + 6)
                        link(nc.vector.tensor_scalar(keep[:, :], rank[:, :], float(TOPK), None, ALU.is_le),
                             pick_link, at + 7)
                        link(nc.vector.tensor_tensor(keep[:, :], keep[:, :], equal[:, :], ALU.mult), pick_link, at + 8)
                        link(nc.vector.tensor_tensor(picked[:, p, :], above[:, :], keep[:, :], ALU.add),
                             pick_link, at + 9)
                        nc.vector.tensor_tensor(masked[:, p, :].rearrange("p (a r) -> p a r", r=R),
                                                ps_v[:, p, :].rearrange("p (a r) -> p a r", r=R),
                                                picked[:, p, :].unsqueeze(2).to_broadcast([P, NA, R]),
                                                ALU.mult).then_inc(v_used, 1)
                        dve.wait_ge(v_used, t + 1 + CC)
                        nc.vector.tensor_reduce(v[:, p, :], masked[:, p, :].rearrange("p (a r) -> p r a", r=R), AX.X,
                                                ALU.add).then_inc(picked_ok, 1)
                        dve.wait_ge(picked_ok, t + 1)
                        dve.wait_ge(zt_full, 2 * (t - 1) + 2 * CC)
                        nc.vector.scalar_tensor_tensor(z[:, p, :].rearrange("p (a r) -> p a r", r=R),
                                                       picked[:, p, :].unsqueeze(2).to_broadcast([P, NA, R]),
                                                       1.0 / TOPK ** 2, v[:, p, :].unsqueeze(1).to_broadcast([P, NA, R]),
                                                       ALU.mult, ALU.mult).then_inc(z_ok, 1)
                    elif kind == "zt":
                        for q in range(2):
                            dve.wait_ge(zt_high, t * 2 + q + 1)
                            nc.vector.tensor_tensor(zT_lo[:, 4 * q:4 * q + 4, :],
                                                    ps_z[:, q, :].rearrange("p (a s) -> p a s", a=4),
                                                    f(zT_hi[:, 4 * q:4 * q + 4, :]), ALU.subtract).then_inc(zt_low, 1)
                    elif kind == "sum":
                        dve.wait_ge(y_full, t + 1 + PER)
                        if n == 0:
                            dve.wait_ge(stored, 16 * PER * i + C)
                        nc.vector.tensor_tensor(y[:, n, :], ps_y[:, 0:H], bias_s[:, :], ALU.add).then_inc(y_read, 1)
                        dve.wait_ge(y_read, t + 1 + C)
                        nc.vector.tensor_tensor(y[:, n, :], y[:, n, :], xs[:, n, :], ALU.add).then_inc(y_ok, 1)

            turns(dve, turn)


HD1, NH1, G1, HPG1 = 16, 16, 4, 4
PAD = -3.0e38


def second_plan():
    tiles, per = NH1 * QT, HPG1 * QT

    def turns(g):
        nxt, g = divmod(g, G1)
        kt, qt = [("kt", g, j, nxt) for j in range(4)], [("qt", g, j, nxt) for j in range(QT)]
        return {0: qt[:1], 1: kt[:1], 2: kt[1:2], 3: qt[1:], 4: kt[2:]}

    scores = {tiles - 2: [("scores", 0, 0, 1)], tiles: [("scores", 1, 0, 1)], tiles + 1: [("scores", 2, 0, 1)]}
    maxima = {tiles - 2: [("mask", 0, 0, 1)], tiles - 1: [("max", 0, 0, 1)], tiles: [("max", 1, 0, 1)]}
    steps = []
    for t in range(tiles + 2):
        g, at = divmod(t, per)
        work = turns(g + 1).get(at, []) if g < G1 else []
        if g == G1 // 2:
            work = work + {0: [("ln", 0, 0, 1), ("xt", 0, 0, 1)], 1: [("qp", 0, 0, 1)], 2: [("kv", 0, 0, 1)],
                           4: [("kv", 0, 1, 1)], 6: [("kv", 0, 2, 1)], 7: [("kv", 0, 3, 1)]}.get(at, [])
        head = t // 2 - 1
        pv = [("pv", head, 2 * (t % 2) + j, 0) for j in range(2)] if head >= 0 else []
        take = [("take", head, 0, 0)] if t % 2 and pv else []
        if t + 1 < tiles:
            steps.append(("exp", t + 1, 0, 0))
        if t + 2 < tiles:
            steps.append(("max", t + 2, 0, 0))
        if t == tiles:
            steps += [("exp", 0, 0, 1)]
        steps += pv + work
        steps += [("rows", t - tiles, 0, 0)] if t >= tiles else []
        if t < tiles:
            steps += [("turn", t, j, 0) for j in range(3)]
        steps += [("scores", t + 3, 0, 0)] if t + 3 < tiles else scores.get(t, [])
        steps += take
        if t < tiles:
            steps.append(("turn", t, 3, 0))
        if t == tiles - 1:
            steps.append(("inv", 0, 0, 0))
        steps += maxima.get(t, [])
    return with_negated(steps + [("wo", 0, 0, 0), ("wo", 1, 0, 0)])


def second_attention(nc, x, out, ctxT, mask, alibi, wq, wkv, wo):
    steps = second_plan()
    TURN_BANKS, PROBS = 3, 3
    ring = Ring(steps, ("xt", "kv", "qp", "kt", "qt", "turn", "rows", "wo"), TURN_BANKS)
    TILES = NH1 * QT
    ROWS = 4 * HD1
    C = 1

    with ExitStack() as ctx:
        def sb(name, shape, dt=F32):
            return ctx.enter_context(nc.sbuf_tensor("a1_" + name, shape, dt))

        def sem(name):
            return ctx.enter_context(nc.semaphore("a1_" + name))

        ctx_s = sb("ctx", [P, KC, SKP])
        wkv_s, wq_s, wo_s = sb("wkv", [P, KC, P]), sb("wq", [P, KC, H]), sb("wo", [P, HPG1, H])
        mask8 = sb("mask8", [P, SK], mybir.dt.uint8)
        maskt = sb("mask", [P, SKC])
        kv_raw = sb("kv_raw", [P, KT, P])
        k_rows = [sb(f"k_rows{i}", [P, KT, P]) for i in range(2)]
        q_rows = sb("q_rows", [P, QT, NH1, P])
        kk = [sb(f"kk{i}", [P, SKP], F32R) for i in range(2)]
        qq = [sb(f"qq{i}", [P, HPG1, S], F32R) for i in range(2)]
        vv = sb("vv", [P, KT, G1, 2, HD1], F32R)
        q_raw = sb("q_raw", [P, QT, H])
        alibi_s = sb("alibi", [P, QT, NH1, 2])
        place = sb("place", [P, KT])
        prob = [sb(f"prob{i}", [P, SKP]) for i in range(PROBS)]
        pt_hi, pt_lo = ([sb(f"{n}{i}", [P, KT, S], F32R) for i in range(2)] for n in ("pt_hi", "pt_lo"))
        heads = sb("heads", [P, HPG1, S])
        x_in, x_res, x_out, xn = (sb(n, [P, QT, H]) for n in ("x_in", "x_res", "x_out", "xn"))
        xT = sb("xT", [P, KC, S])
        ident, half = sb("ident", [P, P]), sb("half", [P, QT])
        top, negmax = sb("top", [P, 4, 2]), sb("negmax", [P, 4])
        total, inv = sb("total", [P, QT * HPG1 * G1]), sb("inv", [P, QT * HPG1 * G1])
        inv_rows = sb("inv_rows", [P, QT * HPG1 * G1, P // G1])
        ln6, ln2, lnr = sb("ln6", [P, QT, 6]), sb("ln2", [P, QT, 2]), sb("lnr", [P, QT])

        ps_s = ctx.enter_context(nc.psum_tensor("a1_ps_s", [P, CHUNKS, BANK], F32))
        ps_t = ctx.enter_context(nc.psum_tensor("a1_ps_t", [P, TURN_BANKS, BANK], F32))
        ps_o = ctx.enter_context(nc.psum_tensor("a1_ps_o", [P, BANK], F32))

        (w_in, al_in, const_set, const_ok, ctx_in, ctx_used, x_in_s, x_kept, mask_in, mask_ok, ln_step, ln_var,
         ln_rstd, x_norm, al_step, q_high, q_low, v_high, v_split, k_high, k_low, bank_full, scores_full, scored,
         negmax_ok, exp_ok, high_ok, pv_done, taken, inv_step, inv_ok, x_done, x_stored, dve_passed, pool_passed,
         sp_passed) = (
            sem(n) for n in ("w_in", "al_in", "const_set", "const_ok", "ctx_in", "ctx_used", "x_in_s", "x_kept",
                             "mask_in", "mask_ok", "ln_step", "ln_var", "ln_rstd", "x_norm", "al_step", "q_high",
                             "q_low", "v_high", "v_split", "k_high", "k_low", "bank_full", "scores_full", "scored",
                             "negmax_ok", "exp_ok", "high_ok", "pv_done", "taken", "inv_step", "inv_ok", "x_done",
                             "x_stored", "dve_passed", "pool_passed", "sp_passed"))
        bank_free = [sem(f"bank_free{i}") for i in range(TURN_BANKS)]

        def f(ap):
            return ap.bitcast(F32)

        def r(ap):
            return ap.bitcast(F32R)

        def is_free(eng, part, b, step, done):
            bank = ring.bank(part, step)
            eng.wait_ge(bank_free[bank], ring.tenants(part, b, step) + done + C)
            return ps_t[:, bank, :]

        def is_full(eng, part, b, step):
            eng.wait_ge(bank_full, ring.before(part, b, step) + 1 + C)
            return ps_t[:, ring.bank(part, step), :]

        def batches(eng, body):
            body(0, -1, [s for s in steps if s[-1]])
            if B > 1:
                with eng.Fori(0, B - 1) as b:
                    body(1, b, steps)
            body(2, B - 1, [s for s in steps if not s[-1]])

        block = ctx.enter_context(nc.Block())

        @block.sync
        def _(sp):
            sp.sem_inc(x_stored, C)
            for t, src in ((wkv_s, wkv), (wq_s, wq), (wo_s, wo)):
                sp.dma_start(t[:, :, :], src).then_inc(w_in, 16)
            sp.dma_start(alibi_s[:, :, :, :], alibi.rearrange("(t p) h c -> p t h c", p=P)).then_inc(al_in, 16)

            def batch(part, b, _):
                if part < 2:
                    sp.wait_ge(x_kept, b + 1 + C)
                    stand(sp, sp_passed)
                    sp.dma_start(x_in[:, :, :], x[b + 1].rearrange("(t p) h -> p t h", p=P)).then_inc(x_in_s, 16)
                    sp.wait_ge(ctx_used, b + 1 + C)
                    stand(sp, sp_passed)
                    sp.dma_start(ctx_s[:, :, :].rearrange("p c k -> p (c k)"), ctxT[b + 1]).then_inc(ctx_in, 16)
                    sp.wait_ge(mask_ok, b + 1 + C)
                    stand(sp, sp_passed)
                    sp.dma_start(mask8[:, :], mask[b + 1].partition_broadcast(P)).then_inc(mask_in, 16)
                if part:
                    sp.wait_ge(x_done, b + 1 + C)
                    stand(sp, sp_passed)
                    sp.dma_start(out[b].rearrange("(t p) h -> p t h", p=P), x_out[:, :, :]).then_inc(x_stored, 16)

            batches(sp, batch)
            sp.wait_ge(x_stored, 16 * B + C)

        @block.gpsimd
        def _(pool):
            for s in (x_kept, ctx_used, q_low, v_split, k_low):
                pool.sem_inc(s, C)
            nc.gpsimd.memset(half[:, :], -0.5).then_inc(const_ok, 1)
            for t in prob:
                nc.gpsimd.memset(t[:, SKC:], 0.0).then_inc(const_ok, 1)
            nc.gpsimd.memset(ident[:, :], 0.0).then_inc(const_set, 1)
            nc.gpsimd.memset(q_rows[:, :, :, :], 0.0).then_inc(const_set, 1)
            for t in k_rows:
                nc.gpsimd.memset(t[:, :, :], 0.0).then_inc(const_set, 1)
            nc.gpsimd.iota(place[:, :], pattern=[[P, KT]], base=0, channel_multiplier=1,
                           allow_small_or_imprecise_dtypes=True).then_inc(const_set, 1)
            pool.wait_ge(const_set, 5)
            nc.gpsimd.affine_select(out=ident[:, :], in_=ident[:, :], compare_op=ALU.not_equal, fill=1.0, base=0,
                                    pattern=[[-1, P]], channel_multiplier=1).then_inc(const_ok, 1)
            for t in k_rows:
                nc.gpsimd.tensor_scalar(t[:, :, ROWS:ROWS + 2], place[:, :].unsqueeze(2).to_broadcast([P, KT, 2]),
                                        1.0, None, ALU.mult).then_inc(const_ok, 1)
                nc.gpsimd.memset(t[:, :, ROWS + 2:ROWS + 4], 1.0).then_inc(const_ok, 1)
            pool.wait_ge(al_in, 16)
            for q in range(QT):
                hi, lo = q_rows[:, q, :, ROWS:ROWS + 4:2], q_rows[:, q, :, ROWS + 1:ROWS + 4:2]
                nc.gpsimd.tensor_scalar(r(hi), alibi_s[:, q, :, :], 1.0, None, ALU.mult).then_inc(al_step, 1)
                pool.wait_ge(al_step, q + 1)
                nc.gpsimd.tensor_tensor(lo, alibi_s[:, q, :, :], hi, ALU.subtract).then_inc(const_ok, 1)
            pool.wait_ge(const_ok, 8 + PROBS)

            def keys(b, g):
                stand(pool, pool_passed)
                t = k_rows[g % 2]
                src = kv_raw[:, :, g * HD1:(g + 1) * HD1]
                for i in (0, 2):
                    nc.gpsimd.tensor_scalar(r(t[:, :, i * HD1:(i + 1) * HD1]), src, 1.0, None,
                                            ALU.mult).then_inc(k_high, 1)
                pool.wait_ge(k_high, (b * G1 + g) * 2 + 2)
                for i in (1, 3):
                    nc.gpsimd.tensor_tensor(t[:, :, i * HD1:(i + 1) * HD1], src, t[:, :, 0:HD1],
                                            ALU.subtract).then_inc(k_low, 1)

            def batch(part, b, _):
                if part:
                    pool.wait_ge(x_done, b + C)
                    stand(pool, pool_passed)
                    nc.gpsimd.tensor_scalar(x_res[:, :, :], x_in[:, :, :], 1.0, None, ALU.mult).then_inc(x_kept, 1)
                    is_full(pool, part, b, ("kt", 1, 3, 0))
                    keys(b, 3)
                if part == 2:
                    return
                nb = b + 1
                pool.wait_ge(ln_var, nb * QT + QT)
                nc.gpsimd.tensor_tensor(lnr[:, :], ln2[:, :, 1], half[:, :], ALU.pow).then_inc(ln_rstd, 1)
                is_free(pool, part, b, ("qp", 0, 0, 1), 1)
                if part:
                    is_full(pool, part, b, ("qt", 3, 1, 0))
                stand(pool, pool_passed)
                for q in range(QT):
                    src = q_raw[:, q, :].rearrange("p (h d) -> p h d", h=NH1)
                    hi = q_rows[:, q, :, 0:HD1]
                    nc.gpsimd.tensor_scalar(r(hi), src, 1.0, None, ALU.mult).then_inc(q_high, 1)
                    nc.gpsimd.tensor_scalar(r(q_rows[:, q, :, HD1:2 * HD1]), src, 1.0, None,
                                            ALU.mult).then_inc(q_high, 1)
                    pool.wait_ge(q_high, (nb * QT + q) * 2 + 2)
                    for i in (2, 3):
                        nc.gpsimd.tensor_tensor(q_rows[:, q, :, i * HD1:(i + 1) * HD1], src, hi,
                                                ALU.subtract).then_inc(q_low, 1)
                is_free(pool, part, b, ("kv", 0, 3, 1), 1)
                pool.sem_inc(ctx_used, 1)
                for g in range(3):
                    if part:
                        is_full(pool, part, b, ("kt", g + 2, 3, 0) if g < 2 else ("kt", 0, 3, 1))
                    elif g == 2:
                        is_full(pool, part, b, ("kt", 0, 3, 1))
                    keys(nb, g)
                pool.wait_ge(pv_done, nb * NH1 * 4 + C)
                stand(pool, pool_passed)
                for i in range(G1):
                    v = kv_raw[:, :, P // 2 + i * HD1:P // 2 + (i + 1) * HD1]
                    nc.gpsimd.tensor_scalar(vv[:, :, i, 0, :], v, 1.0, None, ALU.mult).then_inc(v_high, 1)
                pool.wait_ge(v_high, nb * G1 + G1)
                for i in range(G1):
                    v = kv_raw[:, :, P // 2 + i * HD1:P // 2 + (i + 1) * HD1]
                    nc.gpsimd.tensor_tensor(vv[:, :, i, 1, :], v, f(vv[:, :, i, 0, :]),
                                            ALU.subtract).then_inc(v_split, 1)

            batches(pool, batch)

        @block.tensor
        def _(pe):
            for s in (bank_full, pv_done):
                pe.sem_inc(s, C)
            pe.wait_ge(const_ok, 8 + PROBS)
            pe.wait_ge(w_in, 48)

            def batch(part, b, order):
                for step in order:
                    kind, n, j, nxt = step
                    nb = b + nxt
                    if kind in ("xt", "qp", "kv", "kt", "qt", "turn", "rows", "wo"):
                        ps = is_free(pe, part, b, step, 0)
                    if kind == "xt":
                        pe.wait_ge(x_norm, nb * QT + QT)
                        for c in range(KC):
                            for q in range(QT):
                                mm = nc.tensor.transpose(ps[:, c * S + q * P:c * S + (q + 1) * P],
                                                         xn[:, q, c * P:(c + 1) * P], ident[:, :])
                        mm.then_inc(bank_full, 1)
                    elif kind == "qp":
                        is_free(pe, part, b, ("xt", 0, 0, nxt), 1)
                        for q in range(QT):
                            for c in range(KC):
                                mm = nc.tensor.matmul(ps[:, q * H:(q + 1) * H], xT[:, c, q * P:(q + 1) * P],
                                                      wq_s[:, c, :], start=c == 0, stop=c == KC - 1)
                        mm.then_inc(bank_full, 1)
                    elif kind == "kv":
                        if j == 0:
                            pe.wait_ge(ctx_in, nb * 16 + 16)
                        for i, k in enumerate(KGROUPS[j]):
                            for c in range(KC):
                                mm = nc.tensor.matmul(ps[:, i * P:(i + 1) * P], ctx_s[:, c, k * P:(k + 1) * P],
                                                      wkv_s[:, c, :], start=c == 0, stop=c == KC - 1)
                        mm.then_inc(bank_full, 1)
                    elif kind == "kt":
                        pe.wait_ge(k_low, (nb * G1 + n) * 2 + 2 + C)
                        for i, k in enumerate(KGROUPS[j]):
                            mm = nc.tensor.transpose(ps[:, i * P:(i + 1) * P], k_rows[n % 2][:, k, :], ident[:, :])
                        mm.then_inc(bank_full, 1)
                    elif kind == "qt":
                        pe.wait_ge(q_low, (nb * QT + QT) * 2 + C)
                        for i in range(HPG1):
                            mm = nc.tensor.transpose(ps[:, i * P:(i + 1) * P], q_rows[:, j, n * HPG1 + i, :],
                                                     ident[:, :])
                        mm.then_inc(bank_full, 1)
                    elif kind == "scores":
                        head, q = divmod(n, QT)
                        g = head // HPG1
                        if n % (HPG1 * QT) == 0:
                            turned = [("kt", g, i, nxt) for i in range(4)] + [("qt", g, i, nxt) for i in range(QT)]
                            for s in ring.last(part, turned):
                                is_free(pe, part, b, s, 1)
                        for c in range(CHUNKS):
                            if c % 2 == 0:
                                pe.wait_ge(scored, (nb * TILES + n) * 2 + c // 2 + C)
                            mm = nc.tensor.matmul(ps_s[:, c, 0:CW], qq[g % 2][:, head % HPG1, q * P:(q + 1) * P],
                                                  kk[g % 2][:, c * CW:(c + 1) * CW], start=True, stop=True)
                            if c % 2:
                                mm.then_inc(scores_full, 1)
                    elif kind == "turn":
                        pe.wait_ge(exp_ok, b * TILES + n + 1)
                        for i, k in enumerate(KGROUPS[j]):
                            mm = nc.tensor.transpose(ps[:, i * P:(i + 1) * P], prob[n % PROBS][:, k * P:(k + 1) * P],
                                                     ident[:, :])
                        mm.then_inc(bank_full, 1)
                    elif kind == "pv":
                        if j == 0:
                            pe.wait_ge(taken, b * NH1 + n + C)
                            if n == 0:
                                pe.wait_ge(v_split, (b + 1) * G1 + C)
                        is_free(pe, part, b, ("turn", 2 * n + 1, j, 0), 1)
                        for k in KGROUPS[j]:
                            v = vv[:, k, :, :, :].rearrange("p g c d -> p (g c d)")
                            nc.tensor.matmul(ps_o[:, 0:S], v, pt_hi[n % 2][:, k, :], start=k == 0, stop=False)
                            mm = nc.tensor.matmul(ps_o[:, 0:S], v, pt_lo[n % 2][:, k, :], start=False,
                                                  stop=k == KT - 1)
                        mm.then_inc(pv_done, 1)
                    elif kind == "rows":
                        pe.wait_ge(inv_step, b + 1)
                        for i in range(2):
                            for q in range(QT):
                                at = (q * HPG1 + 2 * n + i) * G1
                                mm = nc.tensor.matmul(ps[:, i * S + q * P:i * S + (q + 1) * P],
                                                      inv_rows[:, at:at + G1, :].rearrange("p g r -> p (g r)"),
                                                      ident[:, :], start=True, stop=True)
                        mm.then_inc(bank_full, 1)
                    elif kind == "wo":
                        if n == 0:
                            for s in (("rows", 0, 0, 0), ("rows", 1, 0, 0)):
                                is_free(pe, part, b, s, 1)
                        for i in range(HPG1):
                            mm = nc.tensor.matmul(ps[:, 0:H], heads[:, i, n * P:(n + 1) * P], wo_s[:, i, :],
                                                  start=i == 0, stop=i == HPG1 - 1)
                        mm.then_inc(bank_full, 1)

            batches(pe, batch)

        @block.scalar
        def _(act):
            act.sem_inc(taken, C)

            def batch(part, b, order):
                for step in order:
                    kind, n, j, nxt = step
                    nb = b + nxt
                    if kind in ("xt", "qp", "kv"):
                        ps = is_full(act, part, b, step)
                        free = bank_free[ring.bank(part, step)]
                        if kind == "xt":
                            nc.scalar.copy(xT[:, :, :].rearrange("p c s -> p (c s)"), ps).then_inc(free, 1)
                        elif kind == "qp":
                            act.wait_ge(q_low, nb * QT * 2 + C)
                            nc.scalar.mul(q_raw[:, :, :].rearrange("p t h -> p (t h)"), ps, float(HD1) ** -0.5).then_inc(free, 1)
                        else:
                            if j == 0:
                                act.wait_ge(k_low, nb * G1 * 2 + C)
                                act.wait_ge(v_split, nb * G1 + C)
                            w, k0 = len(KGROUPS[j]), KGROUPS[j][0]
                            nc.scalar.copy(kv_raw[:, k0:k0 + w, :].rearrange("p k d -> p (k d)"),
                                                  ps[:, 0:w * P]).then_inc(free, 1)
                    elif kind in ("kt", "qt"):
                        ps = is_full(act, part, b, step)
                        free = bank_free[ring.bank(part, step)]
                        if n >= 1 or part:
                            act.wait_ge(scored, (nb * TILES + (n - 1) * HPG1 * QT) * 2 + C + 1)
                        if kind == "kt":
                            w, k0 = len(KGROUPS[j]), KGROUPS[j][0]
                            nc.scalar.copy(kk[n % 2][:, k0 * P:(k0 + w) * P], ps[:, 0:w * P]).then_inc(free, 1)
                        else:
                            nc.scalar.copy(qq[n % 2][:, :, j * P:(j + 1) * P],
                                           ps.rearrange("p (h s) -> p h s", h=HPG1)).then_inc(free, 1)
                    elif kind == "turn":
                        ps = is_full(act, part, b, step)
                        w, k0 = len(KGROUPS[j]), KGROUPS[j][0]
                        head, q = divmod(n, QT)
                        if q == 0:
                            act.wait_ge(pv_done, (b * NH1 + head - 2) * 4 + j + 1 + C if head >= 2
                                        else b * NH1 * 4 + C)
                        nc.scalar.copy(pt_hi[head % 2][:, k0:k0 + w, q * P:(q + 1) * P],
                                       ps[:, 0:w * P].rearrange("p (k s) -> p k s", k=w)).then_inc(high_ok, 1)
                    elif kind == "exp":
                        head, q = divmod(n, QT)
                        act.wait_ge(negmax_ok, nb * TILES + n + 1)
                        if n == 0:
                            act.wait_ge(inv_ok, nb + C)
                        at = (q * HPG1 + head % HPG1) * G1 + head // HPG1
                        nc.scalar.activation(prob[n % PROBS][:, 0:SKC], prob[n % PROBS][:, 0:SKC], ACT.Exp,
                                             bias=negmax[:, n % 4:n % 4 + 1], scale=1.0,
                                             accum_out=total[:, at:at + 1]).then_inc(exp_ok, 1)
                    elif kind == "take":
                        g, i = divmod(n, HPG1)
                        act.wait_ge(pv_done, (b * NH1 + n) * 4 + 4 + C)
                        if n == 0:
                            act.wait_ge(bank_full, ring.before(part, b) + C)
                        own = slice(g * P // G1, (g + 1) * P // G1)
                        nc.scalar.copy(heads[own, i, :], ps_o[own, 0:S]).then_inc(taken, 1)

            batches(act, batch)

        @block.vector
        def _(dve):
            for s in (*bank_free, mask_ok, inv_ok, x_done):
                dve.sem_inc(s, C)
            dve.sem_inc(scored, C + 1)
            nc.vector.memset(maskt[:, SK:], PAD)

            def batch(part, b, order):
                for step in order:
                    kind, n, j, nxt = step
                    nb = b + nxt
                    if kind == "ln":
                        dve.wait_ge(x_in_s, nb * 16 + 16)
                        for q in range(QT):
                            nc.vector.bn_stats(ln6[:, q, :], x_in[:, q, :]).then_inc(ln_step, 1)
                            dve.wait_ge(ln_step, (nb * QT + q) * 2 + 1)
                            stand(dve, dve_passed)
                            nc.vector.bn_aggr(ln2[:, q, :], ln6[:, q, :]).then_inc(ln_step, 1)
                            dve.wait_ge(ln_step, (nb * QT + q) * 2 + 2)
                            nc.vector.tensor_scalar(ln2[:, q, 1:2], ln2[:, q, 1:2], EPS_LN, None,
                                                    ALU.add).then_inc(ln_var, 1)
                        dve.wait_ge(ln_rstd, nb + 1)
                        if part:
                            dve.wait_ge(bank_full, ring.before(part, b) + C)
                        for q in range(QT):
                            nc.vector.tensor_scalar(xn[:, q, :], x_in[:, q, :], ln2[:, q, 0:1], lnr[:, q:q + 1],
                                                    ALU.subtract, ALU.mult).then_inc(x_norm, 1)
                    elif kind == "mask":
                        dve.wait_ge(mask_in, nb * 16 + 16)
                        nc.vector.tensor_scalar(maskt[:, 0:SK], mask8[:, :], -NEG, NEG, ALU.mult,
                                                ALU.add).then_inc(mask_ok, 1)
                    elif kind == "turn":
                        w, k0 = len(KGROUPS[j]), KGROUPS[j][0]
                        head, q = divmod(n, QT)
                        bank = ring.bank(part, step)
                        dve.wait_ge(high_ok, (b * TILES + n) * 4 + j + 1)
                        nc.vector.tensor_tensor(pt_lo[head % 2][:, k0:k0 + w, q * P:(q + 1) * P],
                                                ps_t[:, bank, 0:w * P].rearrange("p (k s) -> p k s", k=w),
                                                f(pt_hi[head % 2][:, k0:k0 + w, q * P:(q + 1) * P]),
                                                ALU.subtract).then_inc(bank_free[bank], 1)
                    elif kind == "max":
                        if n == 0:
                            dve.wait_ge(mask_ok, nb + 1 + C)
                        if n >= PROBS:
                            is_full(dve, part, b, ("turn", n - PROBS, 3, 0))
                        elif nxt and part:
                            is_full(dve, part, b, ("turn", TILES - 2 + n, 3, 0))
                        else:
                            dve.wait_ge(bank_full, ring.before(part, b) + C)
                        for c in range(2):
                            dve.wait_ge(scores_full, (nb * TILES + n) * 2 + c + 1)
                            stand(dve, dve_passed)
                            k = slice(2 * c * CW, (2 * c + 2) * CW)
                            nc.vector.tensor_tensor_reduce(
                                prob[n % PROBS][:, k].rearrange("p (c k) -> p c k", c=2), ps_s[:, 2 * c:2 * c + 2, 0:CW],
                                maskt[:, k].rearrange("p (c k) -> p c k", c=2), 1.0, -3.4e38, ALU.add,
                                ALU.max, top[:, n % 4, c:c + 1]).then_inc(scored, 1)
                    elif kind == "neg":
                        dve.wait_ge(scored, (nb * TILES + n) * 2 + 3 + C)
                        nc.vector.tensor_reduce(negmax[:, n % 4:n % 4 + 1], top[:, n % 4, :], AX.X, ALU.max,
                                                negate=True).then_inc(negmax_ok, 1)
                    elif kind == "inv":
                        dve.wait_ge(exp_ok, (b + 1) * TILES)
                        nc.vector.reciprocal(inv[:, :], total[:, :]).then_inc(inv_ok, 1)
                        dve.wait_ge(inv_ok, b + 1 + C)
                        nc.vector.tensor_copy(inv_rows[:, :, :], inv[:, :].unsqueeze(2).to_broadcast(
                            [P, QT * HPG1 * G1, P // G1])).then_inc(inv_step, 1)
                    elif kind == "rows":
                        ps = is_full(dve, part, b, step)
                        dve.wait_ge(taken, b * NH1 + (NH1 - 2 if n == 0 else NH1) + C)
                        h = heads[:, 2 * n:2 * n + 2, :].rearrange("p h s -> p (h s)")
                        nc.vector.tensor_tensor(h, ps, h, ALU.mult).then_inc(bank_free[ring.bank(part, step)], 1)
                    elif kind == "wo":
                        ps = is_full(dve, part, b, step)
                        if n == 0:
                            dve.wait_ge(x_kept, b + 1 + C)
                            dve.wait_ge(x_stored, b * 16 + C)
                        nc.vector.tensor_tensor(x_out[:, n, :], ps[:, 0:H], x_res[:, n, :],
                                                ALU.add).then_inc(bank_free[ring.bank(part, step)], 1)
                        if n == 1:
                            is_free(dve, part, b, ("wo", 0, 0, 0), 1)
                            is_free(dve, part, b, ("wo", 1, 0, 0), 1)
                            dve.sem_inc(x_done, 1)

            batches(dve, batch)


NE, INNER, TOP2 = 8, 704, 2
IT = -(-INNER // P)
REST = INNER % P
assert REST == P // 2
Q_IN, Q_MIN = 128, -128
MAGIC = 1.5 * 2.0 ** 23


def second_ffn(nc, x, out, wg, w13, w2, table):
    TILES = B * S // P
    BLK = 4
    BLOCKS = TILES // BLK
    NT = -Q_MIN + 1
    C = 1

    with ExitStack() as ctx:
        def sb(name, shape, dt=F32):
            return ctx.enter_context(nc.sbuf_tensor("f1_" + name, shape, dt))

        def sem(name):
            return ctx.enter_context(nc.semaphore("f1_" + name))

        acc = sb("acc", [P, TILES, H])
        xT_hi, xT_lo = (sb(n, [P, KC, TILES * P], F32R) for n in ("xT_hi", "xT_lo"))
        weight = sb("weight", [P, TILES, NE])
        wg_raw = sb("wg_raw", [P, KC, NE])
        table_s, steps_s = sb("table", [P, NT]), sb("steps", [P, NT])
        w13_raw, w2_raw = sb("w13_raw", [P, 2, KC, IT * P]), sb("w2_raw", [P, IT, H])
        w13_hi, w13_lo = ([sb(f"{n}{i}", [P, 2, KC, IT * P], F32R) for i in range(2)] for n in ("w13_hi", "w13_lo"))
        w2_hi, w2_lo = ([sb(f"{n}{i}", [P, IT, H], F32R) for i in range(2)] for n in ("w2_hi", "w2_lo"))
        ident, half = sb("ident", [P, P]), sb("half", [P, BLK])
        xn, xT = sb("xn", [P, BLK, H]), sb("xT", [P, BLK, KC, P])
        ln6, ln2, rstd = sb("ln6", [P, BLK, 6]), sb("ln2", [P, BLK, 2]), sb("rstd", [P, BLK])
        level, top = sb("level", [P, TILES, NE]), sb("top", [P, TILES])
        onehot = sb("onehot", [P, NE, NT])
        value = sb("value", [P, TILES, NE])
        prob, key, other, keep = (sb(n, [P, BLK, NE]) for n in ("prob", "key", "other", "keep"))
        total, best = sb("total", [P, BLK]), sb("best", [P, BLK])
        order = sb("order", [P, NE])
        gate = sb("gate", [P, 2, BLK * P])
        h_raw = sb("h_raw", [P, 3, BLK * P])
        h_hi, h_lo = (sb(n, [P, IT, BLK * P], F32R) for n in ("h_hi", "h_lo"))

        ps_h = ctx.enter_context(nc.psum_tensor("f1_ps_h", [P, 2, 2, BANK], F32))
        ps_y = ctx.enter_context(nc.psum_tensor("f1_ps_y", [P, 2, BANK], F32))
        ps_l = ctx.enter_context(nc.psum_tensor("f1_ps_l", [P, 2, BANK], F32))

        (c_in, w_in, const_set, const_ok, route_step, var_ok, rstd_ok, x_norm, xt_full, xt_ok, xt_high, xt_low,
         l_full, w_high, w_low, h_full, gate_ok, h_ok, h_high, h_split, y_full, y_read, stored) = (
            sem(n) for n in ("c_in", "w_in", "const_set", "const_ok", "route_step", "var_ok", "rstd_ok", "x_norm",
                             "xt_full", "xt_ok", "xt_high", "xt_low", "l_full", "w_high", "w_low", "h_full",
                             "gate_ok", "h_ok", "h_high", "h_split", "y_full", "y_read", "stored"))

        ln_step = sem("ln_step")
        x_in = [sem(f"x_in{i}") for i in range(BLOCKS)]
        dve_passed, pe_passed, sp_passed = sem("dve_passed"), sem("pe_passed"), sem("sp_passed")

        def f(ap):
            return ap.bitcast(F32)

        def own(m):
            return slice(0, P) if m < IT - 1 else slice(P - REST, P)

        def place(m):
            return m % 2 if m < IT - 1 else 2

        block = ctx.enter_context(nc.Block())

        @block.sync
        def _(sp):
            for blk in range(BLOCKS):
                t = slice(blk * BLK, (blk + 1) * BLK)
                sp.dma_start(acc[:, t, :], x[t].rearrange("t p h -> p t h")).then_inc(x_in[blk], 16)
            sp.dma_start(wg_raw[:, :, :], wg).then_inc(c_in, 16)
            sp.dma_start(table_s[:, :], table[0].partition_broadcast(P)).then_inc(c_in, 16)
            sp.dma_start(steps_s[:, :], table[1].partition_broadcast(P)).then_inc(c_in, 16)
            with sp.Fori(0, NE) as e:
                sp.wait_ge(w_low, e * 2 + C)
                stand(sp, sp_passed)
                sp.dma_start(w13_raw[:, :, :, :], w13[e]).then_inc(w_in, 16)
                sp.dma_start(w2_raw[:, :, :], w2[e]).then_inc(w_in, 16)
            sp.wait_ge(y_read, NE * TILES + 1 + C)
            sp.dma_start(out.rearrange("t p h -> p t h"), acc[:, :, :]).then_inc(stored, 16)
            sp.wait_ge(stored, 16)

        @block.gpsimd
        def _(pool):
            nc.gpsimd.memset(half[:, :], -0.5).then_inc(const_ok, 1)
            pool.sem_inc(w_low, C)
            pool.sem_inc(h_split, C)
            nc.gpsimd.iota(order[:, :], pattern=[[-1, NE]], base=NE - 1, channel_multiplier=0,
                           allow_small_or_imprecise_dtypes=True).then_inc(const_ok, 1)
            nc.gpsimd.memset(ident[:, :], 0.0).then_inc(const_set, 1)
            nc.gpsimd.memset(h_raw[:, place(IT - 1), :], 0.0).then_inc(const_ok, 1)
            pool.wait_ge(const_set, 1)
            nc.gpsimd.affine_select(out=ident[:, :], in_=ident[:, :], compare_op=ALU.not_equal, fill=1.0, base=0,
                                    pattern=[[-1, P]], channel_multiplier=1).then_inc(const_ok, 1)
            pool.wait_ge(const_ok, 4)
            with pool.Fori(0, BLOCKS) as blk:
                pool.wait_ge(var_ok, blk + 1)
                nc.gpsimd.tensor_tensor(rstd[:, :], ln2[:, :, 1], half[:, :], ALU.pow).then_inc(rstd_ok, 1)

            def weights(e, i):
                pool.wait_ge(w_in, e * 32 + 32)
                pool.wait_ge(w_high, e * 2 + 2)
                nc.gpsimd.tensor_tensor(w13_lo[i][:, :, :, :], w13_raw[:, :, :, :], f(w13_hi[i][:, :, :, :]),
                                        ALU.subtract).then_inc(w_low, 1)
                nc.gpsimd.tensor_tensor(w2_lo[i][:, :, :], w2_raw[:, :, :], f(w2_hi[i][:, :, :]),
                                        ALU.subtract).then_inc(w_low, 1)

            weights(0, 0)

            def experts(pair, more):
                for i in range(2):
                    e = pair * 2 + i
                    for blk in range(BLOCKS):
                        for m in range(IT):
                            n = (e * BLOCKS + blk) * IT + m
                            pool.wait_ge(h_high, n + 1)
                            nc.gpsimd.tensor_tensor(h_lo[:, m, :], h_raw[:, place(m), :], f(h_hi[:, m, :]),
                                                    ALU.subtract).then_inc(h_split, 1)
                        if blk == 0 and i == 0:
                            weights(e + 1, 1)
                        if blk == 0 and i == 1 and more:
                            weights(e + 1, 0)

            with pool.Fori(0, NE // 2 - 1) as pair:
                experts(pair, True)
            experts(NE // 2 - 1, False)

        @block.tensor
        def _(pe):
            for s in (xt_full, l_full, y_full):
                pe.sem_inc(s, C)
            pe.wait_ge(const_ok, 4)
            pe.wait_ge(c_in, 48)
            def logits(t, n):
                pe.wait_ge(xt_ok, t + 1 + C)
                for c in range(KC):
                    mm = nc.tensor.matmul(ps_l[:, 0, bass.ds(t * NE, NE)], xT[:, n, c, :], wg_raw[:, c, :],
                                          start=c == 0, stop=c == KC - 1)
                mm.then_inc(l_full, 1)

            with pe.Fori(0, BLOCKS) as blk:
                for n in range(BLK):
                    t = blk * BLK + n
                    pe.wait_ge(x_norm, t + 1)
                    if n == 0:
                        pe.wait_ge(xt_low, blk * BLK + C)
                        pe.wait_ge(xt_ok, blk * BLK + C)
                    for c in range(KC):
                        mm = nc.tensor.transpose(ps_h[:, n // 2, n % 2, c * P:(c + 1) * P],
                                                 xn[:, n, c * P:(c + 1) * P], ident[:, :])
                    mm.then_inc(xt_full, 1)
                    if n:
                        logits(t - 1, n - 1)
                logits(blk * BLK + BLK - 1, BLK - 1)
            pe.wait_ge(xt_high, TILES)
            pe.wait_ge(xt_low, TILES + C)

            def split_mm(to, lhs, rhs, first, last):
                (lh, ll), (rh, rl) = lhs, rhs
                nc.tensor.matmul(to, lh, rh, start=first, stop=False)
                nc.tensor.matmul(to, ll, rh, start=False, stop=False)
                return nc.tensor.matmul(to, lh, rl, start=False, stop=last)

            def hidden(e, i, blk, m):
                if blk == 0 and m == 0:
                    pe.wait_ge(w_low, e * 2 + 2 + C)
                pe.wait_ge(h_ok, (e * BLOCKS + blk) * IT + m + C)
                w, k = slice(m * P, (m + 1) * P), slice(blk * BLK * P, (blk + 1) * BLK * P)
                for g in range(2 if m < IT - 1 else 1):
                    for c in range(KC):
                        mm = split_mm(ps_h[:, m % 2, g, :], (w13_hi[i][:, g, c, w], w13_lo[i][:, g, c, w]),
                                      (xT_hi[:, c, k], xT_lo[:, c, k]), c == 0, c == KC - 1)
                mm.then_inc(h_full, 1)

            def outputs(e, i, blk):
                it = e * BLOCKS + blk
                for q in range(BLK):
                    pe.wait_ge(y_read, it * BLK + q + C)
                    for m in range(IT):
                        if q == 0:
                            pe.wait_ge(h_split, it * IT + m + 1 + C)
                        k = slice(q * P, (q + 1) * P)
                        mm = split_mm(ps_y[:, q % 2, 0:H], (h_hi[:, m, k], h_lo[:, m, k]),
                                      (w2_hi[i][:, m, :], w2_lo[i][:, m, :]), m == 0, m == IT - 1)
                    mm.then_inc(y_full, 1)

            def experts(pair, more):
                order = [(i, blk) for i in range(2) for blk in range(BLOCKS)]
                for at, (i, blk) in enumerate(order):
                    e = pair * 2 + i
                    for m in range(1, IT):
                        hidden(e, i, blk, m)
                    if at + 1 < len(order):
                        ni, nblk = order[at + 1]
                        hidden(pair * 2 + ni, ni, nblk, 0)
                    elif more:
                        hidden(pair * 2 + 2, 0, 0, 0)
                    outputs(e, i, blk)

            hidden(0, 0, 0, 0)
            with pe.Fori(0, NE // 2 - 1) as pair:
                experts(pair, True)
            experts(NE // 2 - 1, False)

        @block.scalar
        def _(act):
            act.sem_inc(xt_ok, C)

            def weights(e, i):
                act.wait_ge(w_in, e * 32 + 32)
                nc.scalar.copy(w13_hi[i][:, :, :, :], w13_raw[:, :, :, :]).then_inc(w_high, 1)
                nc.scalar.copy(w2_hi[i][:, :, :], w2_raw[:, :, :]).then_inc(w_high, 1)

            def turned(blk):
                for n in range(BLK):
                    t = blk * BLK + n
                    ps = ps_h[:, n // 2, n % 2, 0:H].rearrange("p (c s) -> p c s", c=KC)
                    act.wait_ge(xt_full, t + 1 + C)
                    nc.scalar.copy(xT_hi[:, :, bass.ts(t, P)], ps).then_inc(xt_high, 1)
                    act.wait_ge(l_full, blk * BLK + C)
                    nc.scalar.copy(xT[:, n, :, :], ps).then_inc(xt_ok, 1)

            with act.Fori(0, BLOCKS - 1) as blk:
                turned(blk)
            weights(0, 0)
            turned(BLOCKS - 1)

            def experts(pair, more):
                for i in range(2):
                    e = pair * 2 + i
                    for blk in range(BLOCKS):
                        for m in range(IT):
                            n = (e * BLOCKS + blk) * IT + m
                            act.wait_ge(h_full, n + 1)
                            if m < 2:
                                act.wait_ge(h_ok, (e * BLOCKS + blk) * IT + 1 + C)
                            else:
                                act.wait_ge(h_ok, n + C)
                            src = ps_h[0:own(m).stop - own(m).start, m % 2, 0, :]
                            nc.scalar.activation(gate[own(m), m % 2, :], src, ACT.Silu).then_inc(gate_ok, 1)
                            act.wait_ge(h_ok, n + 2 + C)
                            act.wait_ge(y_full, (e * BLOCKS + blk) * BLK + C)
                            nc.scalar.copy(h_hi[:, m, :], h_raw[:, place(m), :]).then_inc(h_high, 1)
                        if blk == 0 and i == 0:
                            act.wait_ge(y_full, e * BLOCKS * BLK + C)
                            weights(e + 1, 1)
                        if blk == 0 and i == 1 and more:
                            act.wait_ge(y_full, e * BLOCKS * BLK + C)
                            weights(e + 1, 0)

            with act.Fori(0, NE // 2 - 1) as pair:
                experts(pair, True)
            experts(NE // 2 - 1, False)

        @block.vector
        def _(dve):
            dve.sem_inc(h_ok, C + 1)
            dve.sem_inc(y_read, C + 1)
            dve.sem_inc(xt_low, C)
            dve.wait_ge(const_ok, 4)
            LN_LINKS = 2 * BLK

            def rows(blk, n):
                return acc[:, bass.ds(blk * BLK + n, 1), :].rearrange("p o h -> p (o h)")

            def statistics(blk):
                for n in range(BLK):
                    nc.vector.bn_stats(ln6[:, n, :], rows(blk, n)).then_inc(ln_step, 1)
                    dve.wait_ge(ln_step, blk * LN_LINKS + 2 * n + 1)
                    stand(dve, dve_passed)
                    nc.vector.bn_aggr(ln2[:, n, :], ln6[:, n, :]).then_inc(ln_step, 1)
                dve.wait_ge(ln_step, blk * LN_LINKS + LN_LINKS)
                nc.vector.tensor_scalar(ln2[:, :, 1], ln2[:, :, 1], EPS_LN, None, ALU.add).then_inc(var_ok, 1)

            def norms(blk):
                dve.wait_ge(rstd_ok, blk + 1)
                dve.wait_ge(xt_full, blk * BLK + C)
                for n in range(BLK):
                    nc.vector.tensor_scalar(xn[:, n, :], rows(blk, n), ln2[:, n, 0:1], rstd[:, n:n + 1],
                                            ALU.subtract, ALU.mult).then_inc(x_norm, 1)

            def low_parts(blk):
                for n in range(BLK):
                    t = blk * BLK + n
                    dve.wait_ge(xt_ok, t + 1 + C)
                    dve.wait_ge(xt_high, t + 1)
                    nc.vector.tensor_tensor(xT_lo[:, :, bass.ts(t, P)], xT[:, n, :, :], f(xT_hi[:, :, bass.ts(t, P)]),
                                            ALU.subtract).then_inc(xt_low, 1)

            dve.wait_ge(x_in[0], 16)
            statistics(0)
            for s in x_in[1:]:
                dve.wait_ge(s, 16)
            with dve.Fori(0, BLOCKS - 1) as blk:
                norms(blk)
                statistics(blk + 1)
                low_parts(blk)
            norms(BLOCKS - 1)
            low_parts(BLOCKS - 1)
            dve.wait_ge(c_in, 48)

            done = [0]

            def link(ins):
                done[0] += 1
                ins.then_inc(route_step, 1)
                dve.wait_ge(route_step, done[0])

            def spread(ap, n):
                return ap.unsqueeze(2).to_broadcast([P, ap.shape[1], n])

            dve.wait_ge(l_full, TILES + C)
            flat = level[:, :, :].rearrange("p t e -> p (t e)")
            link(nc.vector.tensor_scalar(flat, ps_l[:, 0, 0:TILES * NE], float(Q_IN), MAGIC, ALU.mult, ALU.add))
            link(nc.vector.tensor_scalar(flat, flat, MAGIC, None, ALU.subtract))
            link(nc.vector.tensor_reduce(top[:, :], level[:, :, :], AX.X, ALU.max))
            link(nc.vector.tensor_tensor(level[:, :, :], level[:, :, :], spread(top[:, :], NE), ALU.subtract))
            link(nc.vector.tensor_scalar(flat, flat, float(Q_MIN), None, ALU.max))

            def exponentials(t):
                link(nc.vector.tensor_tensor(onehot[:, :, :], spread(level[:, t, :], NT),
                                             steps_s[:, :].unsqueeze(1).to_broadcast([P, NE, NT]), ALU.is_equal))
                link(nc.vector.tensor_tensor(onehot[:, :, :], onehot[:, :, :],
                                             table_s[:, :].unsqueeze(1).to_broadcast([P, NE, NT]), ALU.mult))
                link(nc.vector.tensor_reduce(value[:, t, :], onehot[:, :, :], AX.X, ALU.add))

            def route(blk):
                t = slice(blk * BLK, (blk + 1) * BLK)
                link(nc.vector.tensor_reduce(total[:, :], value[:, t, :], AX.X, ALU.add))
                link(nc.vector.reciprocal(total[:, :], total[:, :]))
                link(nc.vector.tensor_tensor(prob[:, :, :], value[:, t, :], spread(total[:, :], NE), ALU.mult))
                link(nc.vector.tensor_scalar(key[:, :, :], value[:, t, :], float(NE), None, ALU.mult))
                link(nc.vector.tensor_tensor(key[:, :, :], key[:, :, :],
                                             order[:, :].unsqueeze(1).to_broadcast([P, BLK, NE]), ALU.add))
                link(nc.vector.tensor_reduce(best[:, :], key[:, :, :], AX.X, ALU.max))
                link(nc.vector.tensor_tensor(other[:, :, :], key[:, :, :], spread(best[:, :], NE), ALU.is_lt))
                link(nc.vector.tensor_tensor(other[:, :, :], other[:, :, :], key[:, :, :], ALU.mult))
                link(nc.vector.tensor_reduce(best[:, :], other[:, :, :], AX.X, ALU.max))
                link(nc.vector.tensor_tensor(keep[:, :, :], key[:, :, :], spread(best[:, :], NE), ALU.is_ge))
                link(nc.vector.tensor_tensor(prob[:, :, :], prob[:, :, :], keep[:, :, :], ALU.mult))
                link(nc.vector.tensor_reduce(total[:, :], prob[:, :, :], AX.X, ALU.add))
                link(nc.vector.reciprocal(total[:, :], total[:, :]))
                link(nc.vector.tensor_tensor(weight[:, t, :], prob[:, :, :], spread(total[:, :], NE), ALU.mult))

            def experts(pair, routing):
                for i in range(2):
                    e = pair * 2 + i
                    for blk in range(BLOCKS):
                        it = e * BLOCKS + blk
                        for m in range(IT):
                            n = it * IT + m
                            dve.wait_ge(gate_ok, n + 1)
                            if m < 2:
                                dve.wait_ge(h_split, it * IT + C)
                            else:
                                dve.wait_ge(h_split, n - 1 + C)
                            nc.vector.tensor_tensor(h_raw[own(m), place(m), :], gate[own(m), m % 2, :],
                                                    ps_h[own(m), m % 2, 1 if m < IT - 1 else 0, :],
                                                    ALU.mult).then_inc(h_ok, 1)
                            if routing and m % 2 and i == 0 and blk + 1 < BLOCKS:
                                exponentials((blk + 1) * BLK + m // 2)
                        for q in range(BLK):
                            t = blk * BLK + q
                            dve.wait_ge(y_full, it * BLK + q + 1 + C)
                            nc.vector.scalar_tensor_tensor(
                                acc[:, t, :], ps_y[:, q % 2, 0:H],
                                weight[:, t, bass.ds(e, 1)], acc[:, t, :], ALU.mult, ALU.add).then_inc(y_read, 1)
                            if routing and q == 1 and i == 0 and blk + 1 < BLOCKS:
                                for n in range(IT // 2, BLK):
                                    exponentials((blk + 1) * BLK + n)
                        if routing and i == 0 and blk + 1 < BLOCKS:
                            route(blk + 1)

            for n in range(BLK):
                exponentials(n)
            route(0)
            experts(0, True)
            with dve.Fori(1, NE // 2) as pair:
                experts(pair, False)


def network(nc, x, mask_q, mask_k, ctxT, wq0, wkv0, wo0, bias0, qn, kn, wa, wb, ww, bias_f, alibi, wq1, wkv1, wo1,
            wg, w13, w2, table, out):
    def rows(name):
        return nc.dram_tensor(name, (B, S, H), F32, kind="Internal").ap()

    def tiles(a):
        return a.rearrange("b (t p) h -> (b t) p h", p=P)

    x1, x2, x3 = rows("x1"), rows("x2"), rows("x3")
    first_attention(nc, x, x1, ctxT, mask_q, wq0, wkv0, wo0, bias0, qn, kn)
    first_ffn(nc, tiles(x1), tiles(x2), wa, wb, ww, bias_f)
    second_attention(nc, x2, x3, ctxT, mask_k, alibi, wq1, wkv1, wo1)
    second_ffn(nc, tiles(x3), tiles(out), wg, w13, w2, table)


def _sliced(np, w, kc):
    return np.ascontiguousarray(w.reshape(kc, w.shape[0] // kc, -1).transpose(1, 0, 2))


def _grouped(np, w, groups):
    n = w.shape[1] // groups
    return w.reshape(KC, P, groups, n).transpose(2, 1, 0, 3)


def kernel(**inputs):
    import numpy as np
    import concourse.bacc as _bacc
    from concourse import mybir as _mybir
    from concourse.bass_utils import run_bass_kernel_spmd as _run

    a = {k: np.asarray(v) for k, v in inputs.items()}
    f32 = np.float32

    ctxT = np.zeros((B, H, SKP), f32)
    ctxT[:, :, :SK] = a["ctx_2048"].transpose(0, 2, 1)
    w1, w3, w2 = a["L1_ffn_w1"], a["L1_ffn_w3"], a["L1_ffn_w2"]
    whole = INNER - REST
    w13 = np.zeros((NE, 2, H, IT * P), f32)
    w13[:, 0, :, :INNER] = w1.transpose(0, 2, 1)
    w13[:, 1, :, :whole] = w3[:, :whole].transpose(0, 2, 1)
    w13[:, 0, :, INNER:] = w3[:, whole:].transpose(0, 2, 1)
    w2T = np.zeros((NE, IT * P, H), f32)
    w2T[:, :whole] = w2[:, :, :whole].transpose(0, 2, 1)
    w2T[:, -REST:] = w2[:, :, whole:].transpose(0, 2, 1)
    wo1 = np.repeat(a["L1_xattn_Wo"].reshape(G1, HPG1, 1, HD1, H), 2, axis=2)

    slopes = f32(2.0 ** -0.5) ** np.arange(1, NH1 + 1, dtype=f32)
    alibi = np.zeros((S, NH1, 2), f32)
    alibi[:, :, 0] = slopes
    alibi[:, :, 1] = -slopes * np.arange(S, dtype=f32)[:, None]
    logits = np.arange(Q_MIN, 1)
    table = np.stack([np.floor(np.exp(logits / float(Q_IN)) * 65536.0), logits]).astype(f32)

    arrays = {
        "x": a["x"],
        "mask_q": a["mask_1xSxS2_ff0"].reshape(S, SK),
        "mask_k": a["mask_BxS2_bf1"].view(np.uint8),
        "ctxT": ctxT.reshape(B, KC, P, SKP).transpose(0, 2, 1, 3).reshape(B, P, KC * SKP),
        "wq0": _grouped(np, a["L0_xattn_Wq"], G0),
        "wkv0": np.concatenate([_grouped(np, a["L0_xattn_Wk"], G0), _grouped(np, a["L0_xattn_Wv"], G0)], axis=3),
        "wo0": a["L0_xattn_Wo"].reshape(G0, HPG0, HD0, H).transpose(0, 2, 1, 3),
        "bias0": np.concatenate([a["L0_xattn_" + n].reshape(G0, -1) for n in ("bq", "bk", "bv")], axis=1),
        "qn": a["L0_xattn_qn_w"].reshape(HD0, 1),
        "kn": a["L0_xattn_kn_w"].reshape(HD0, 1),
        "wa": _sliced(np, a["L0_ffn_A"].reshape(AR, H).T, KC),
        "wb": _sliced(np, a["L0_ffn_B"].transpose(0, 2, 1).reshape(AR, H), AC),
        "ww": _sliced(np, a["L0_ffn_W"].T, KC),
        "bias_f": a["L0_ffn_bias"],
        "alibi": alibi,
        "wq1": _sliced(np, a["L1_xattn_Wq"], KC),
        "wkv1": _sliced(np, np.concatenate([a["L1_xattn_Wk"], a["L1_xattn_Wv"]], axis=1), KC),
        "wo1": wo1.transpose(0, 2, 3, 1, 4).reshape(P, HPG1, H),
        "wg": _sliced(np, a["L1_ffn_w_gate"].T, KC),
        "w13": w13.reshape(NE, 2, KC, P, IT * P).transpose(0, 3, 1, 2, 4),
        "w2": w2T.reshape(NE, IT, P, H).transpose(0, 2, 1, 3),
        "table": table,
    }
    nc = _bacc.Bacc("TRN2", target_bir_lowering=False, num_devices=1)
    feeds, args = {}, {}
    for name, array in arrays.items():
        array = np.ascontiguousarray(array)
        feeds[f"in_{name}"] = array
        args[name] = nc.dram_tensor(f"in_{name}", array.shape, _mybir.dt.from_np(array.dtype), kind="ExternalInput").ap()
    args["out"] = nc.dram_tensor("out_0", (B, S, H), F32, kind="ExternalOutput").ap()
    network(nc, **args)
    return _run(nc, [feeds], core_ids=[0]).results[0]["out_0"]
```
